# Optimizing a Trainium2 kernel written in Bass

```python
import numpy as np
import jax
import jax.numpy as jnp

def _softmax(x, axis=-1):
    return jax.nn.softmax(x, axis=axis)

def _gelu(x):
    return jax.nn.gelu(x, approximate=True)

def _silu(x):
    return jax.nn.silu(x)

def _sigmoid(x):
    return jax.nn.sigmoid(x)

def _layernorm(x, axis=-1, eps=1e-05):
    m = jnp.mean(x, axis=axis, keepdims=True)
    v = jnp.var(x, axis=axis, keepdims=True)
    return (x - m) / jnp.sqrt(v + eps)

def _scatter_add(tgt, idx, src, axis=0):
    return tgt.at[idx].add(src)

def _segment_sum(src, seg, n):
    return jax.ops.segment_sum(src, seg, n)
kernel_name = 'mk_gnn_resnorm_d2_gnn_r32_f093d8'

def setup_inputs(seed: int=0):
    np.random.seed(seed)
    _w = jnp.asarray

    def _rec_inputs():
        import jax
        import jax.numpy as jnp
        _gk = jax.random.key(seed)
        x = -0.000202 + 1 * jax.random.normal(jax.random.fold_in(_gk, 1), (50000, 128), jnp.float32)
        _s = jax.random.randint(jax.random.fold_in(_gk, 2), (12500,), 0, 50000, jnp.int32)
        _d = jax.random.randint(jax.random.fold_in(_gk, 3), (12500,), 0, 50000, jnp.int32)
        _loop = jnp.arange(50000, dtype=jnp.int32)
        src = jnp.concatenate([_s, _d, _loop])
        dst = jnp.concatenate([_d, _s, _loop])
        _o = jnp.argsort(dst, stable=True)
        src = src[_o]
        dst = dst[_o]
        return (x, src, dst)
    x, src, dst = _rec_inputs()

    def _L0_gnn_setup():
        import jax, jax.numpy as jnp
        import numpy as np
        N, E, D = (50000, 25000, 128)
        NEG_SLOPE = 0.2

        def _gatv2(x, src, dst, Wl, Wr, att, b):
            xl = x @ Wl
            xr = x @ Wr
            e = jax.nn.leaky_relu(xl[src] + xr[dst], NEG_SLOPE) @ att
            m = jax.ops.segment_max(e, dst, num_segments=N)
            w = jnp.exp(e - m[dst])
            z = jax.ops.segment_sum(w, dst, num_segments=N)
            alpha = w / z[dst]
            out = jax.ops.segment_sum(alpha[:, None] * xl[src], dst, num_segments=N)
            return out + b
        key = jax.random.key(seed)
        ks = jax.random.split(key, 2 + 12)
        x = jax.random.normal(ks[0], (N, D), dtype=jnp.float32)
        edge_index = jax.random.randint(ks[1], (2, E), 0, N, dtype=jnp.int64)
        scale = (1.0 / D) ** 0.5
        inp = {'x': x, 'edge_index': edge_index}
        k = 2
        for i in range(3):
            inp[f'Wl{i}'] = jax.random.normal(ks[k], (D, D), dtype=jnp.float32) * scale
            k += 1
            inp[f'Wr{i}'] = jax.random.normal(ks[k], (D, D), dtype=jnp.float32) * scale
            k += 1
            inp[f'att{i}'] = jax.random.normal(ks[k], (D,), dtype=jnp.float32) * scale
            k += 1
            inp[f'b{i}'] = jnp.zeros((D,), dtype=jnp.float32)
            k += 1
        return inp
    _L0_gnn_all = _L0_gnn_setup()
    _L0_gnn_in = {k: v for k, v in _L0_gnn_all.items() if k in ('Wl0', 'Wr0', 'att0', 'b0', 'Wl1', 'Wr1', 'att1', 'b1', 'Wl2', 'Wr2', 'att2', 'b2')}
    del _L0_gnn_all

    def _L1_gnn_setup():
        import jax, jax.numpy as jnp
        import numpy as np
        N_NODES = 50000
        N_EDGES = 12500
        IN_DIM = 128
        HIDDEN = 128
        OUT_DIM = 128
        MIX = 4

        def _gelu(x):
            return jax.nn.gelu(x, approximate=False)
        key = jax.random.key(seed)
        ks = jax.random.split(key, 8)
        X = jax.random.normal(ks[0], (N_NODES, IN_DIM), dtype=jnp.float32)
        edge_index = jax.random.randint(ks[1], (2, N_EDGES), 0, N_NODES, dtype=jnp.int64)
        s = lambda fan_in: 1.0 / np.sqrt(fan_in)
        W1 = jax.random.uniform(ks[2], (HIDDEN, IN_DIM), jnp.float32, -s(IN_DIM), s(IN_DIM))
        b1 = jax.random.uniform(ks[3], (HIDDEN,), jnp.float32, -s(IN_DIM), s(IN_DIM))
        WA = jax.random.uniform(ks[4], (HIDDEN, HIDDEN), jnp.float32, -s(HIDDEN), s(HIDDEN))
        WB = jax.random.uniform(ks[5], (MIX, HIDDEN), jnp.float32, -s(HIDDEN), s(HIDDEN))
        W2 = jax.random.uniform(ks[6], (OUT_DIM, 2 * HIDDEN), jnp.float32, -s(2 * HIDDEN), s(2 * HIDDEN))
        b2 = jax.random.uniform(ks[7], (OUT_DIM,), jnp.float32, -s(2 * HIDDEN), s(2 * HIDDEN))
        return {'X': X, 'edge_index': edge_index, 'W1': W1, 'b1': b1, 'WA': WA, 'WB': WB, 'W2': W2, 'b2': b2}
    _L1_gnn_all = _L1_gnn_setup()
    _L1_gnn_in = {k: v for k, v in _L1_gnn_all.items() if k in ('W1', 'b1', 'WA', 'WB', 'W2', 'b2')}
    del _L1_gnn_all
    return {'x': x, 'src': src, 'dst': dst, 'L0_gnn_Wl0': _L0_gnn_in['Wl0'], 'L0_gnn_Wr0': _L0_gnn_in['Wr0'], 'L0_gnn_att0': _L0_gnn_in['att0'], 'L0_gnn_b0': _L0_gnn_in['b0'], 'L0_gnn_Wl1': _L0_gnn_in['Wl1'], 'L0_gnn_Wr1': _L0_gnn_in['Wr1'], 'L0_gnn_att1': _L0_gnn_in['att1'], 'L0_gnn_b1': _L0_gnn_in['b1'], 'L0_gnn_Wl2': _L0_gnn_in['Wl2'], 'L0_gnn_Wr2': _L0_gnn_in['Wr2'], 'L0_gnn_att2': _L0_gnn_in['att2'], 'L0_gnn_b2': _L0_gnn_in['b2'], 'L1_gnn_W1': _L1_gnn_in['W1'], 'L1_gnn_b1': _L1_gnn_in['b1'], 'L1_gnn_WA': _L1_gnn_in['WA'], 'L1_gnn_WB': _L1_gnn_in['WB'], 'L1_gnn_W2': _L1_gnn_in['W2'], 'L1_gnn_b2': _L1_gnn_in['b2']}

def reference(x, src, dst, L0_gnn_Wl0, L0_gnn_Wr0, L0_gnn_att0, L0_gnn_b0, L0_gnn_Wl1, L0_gnn_Wr1, L0_gnn_att1, L0_gnn_b1, L0_gnn_Wl2, L0_gnn_Wr2, L0_gnn_att2, L0_gnn_b2, L1_gnn_W1, L1_gnn_b1, L1_gnn_WA, L1_gnn_WB, L1_gnn_W2, L1_gnn_b2):
    import jax
    import jax.numpy as jnp

    def _L0_gnn_ref(x, edge_index, Wl0, Wr0, att0, b0, Wl1, Wr1, att1, b1, Wl2, Wr2, att2, b2):
        import jax, jax.numpy as jnp
        import numpy as np
        N, E, D = (50000, 25000, 128)
        NEG_SLOPE = 0.2

        def _gatv2(x, src, dst, Wl, Wr, att, b):
            xl = x @ Wl
            xr = x @ Wr
            e = jax.nn.leaky_relu(xl[src] + xr[dst], NEG_SLOPE) @ att
            m = jax.ops.segment_max(e, dst, num_segments=N)
            w = jnp.exp(e - m[dst])
            z = jax.ops.segment_sum(w, dst, num_segments=N)
            alpha = w / z[dst]
            out = jax.ops.segment_sum(alpha[:, None] * xl[src], dst, num_segments=N)
            return out + b
        loop = jnp.arange(N, dtype=edge_index.dtype)
        src = jnp.concatenate([edge_index[0], loop])
        dst = jnp.concatenate([edge_index[1], loop])
        h = jax.nn.relu(_gatv2(x, src, dst, Wl0, Wr0, att0, b0))
        h = jax.nn.relu(_gatv2(h, src, dst, Wl1, Wr1, att1, b1))
        return _gatv2(h, src, dst, Wl2, Wr2, att2, b2)

    def _L1_gnn_ref(X, edge_index, W1, b1, WA, WB, W2, b2):
        import jax, jax.numpy as jnp
        import numpy as np
        N_NODES = 50000
        N_EDGES = 12500
        IN_DIM = 128
        HIDDEN = 128
        OUT_DIM = 128
        MIX = 4

        def _gelu(x):
            return jax.nn.gelu(x, approximate=False)
        num_nodes = X.shape[0]
        H = _gelu(X @ W1.T + b1)
        src, dst = (edge_index[0], edge_index[1])
        X_src = H[src]
        W_tar = _gelu(X_src @ WA.T) @ WB.T
        cross = X_src[:, :, None] * W_tar[:, None, :]
        agg = jax.ops.segment_sum(cross, dst, num_segments=num_nodes)
        agg = _gelu(agg)
        out_edge = jnp.einsum('ehm,em->eh', agg[dst], W_tar)
        ones = jnp.ones((src.shape[0],), X.dtype)
        cnt = jax.ops.segment_sum(ones, dst, num_segments=num_nodes)
        agg_node = jax.ops.segment_sum(out_edge, dst, num_segments=num_nodes)
        agg_node = agg_node / jnp.maximum(cnt, 1.0)[:, None]
        feat = _gelu(jnp.concatenate([agg_node, H], axis=1))
        out = feat @ W2.T + b2
        return out
    edge_index = jnp.stack([src, dst])
    x = _layernorm(x + _L0_gnn_ref(x, edge_index, L0_gnn_Wl0, L0_gnn_Wr0, L0_gnn_att0, L0_gnn_b0, L0_gnn_Wl1, L0_gnn_Wr1, L0_gnn_att1, L0_gnn_b1, L0_gnn_Wl2, L0_gnn_Wr2, L0_gnn_att2, L0_gnn_b2), axis=-1)
    x = _layernorm(x + _L1_gnn_ref(x, edge_index, L1_gnn_W1, L1_gnn_b1, L1_gnn_WA, L1_gnn_WB, L1_gnn_W2, L1_gnn_b2), axis=-1)
    return x

_drawn_inputs = setup_inputs


def setup_inputs(seed=0):
    import zlib

    import numpy as np

    out = dict(_drawn_inputs(seed))
    spreads = {'L0_gnn_b0': (0.0, 0.1), 'L0_gnn_b1': (0.0, 0.1), 'L0_gnn_b2': (0.0, 0.1)}
    factors = {'L0_gnn_Wr0': 2.993,
     'L0_gnn_Wr1': 8.0,
     'L0_gnn_att1': 7.062,
     'L0_gnn_Wr2': 34.821,
     'L0_gnn_att2': 8.0,
     'L1_gnn_b1': 5.671,
     'L1_gnn_WA': 8.0,
     'L1_gnn_WB': 8.0,
     'L1_gnn_b2': 4.754}
    for name, (base, spread) in spreads.items():
        noise = np.random.default_rng([zlib.crc32(name.encode()), seed]).standard_normal(out[name].shape)
        drawn = base * np.exp(spread * noise) if base else spread * noise
        out[name] = jnp.asarray(drawn.astype(out[name].dtype))
    for name, factor in factors.items():
        out[name] = (out[name] * factor).astype(out[name].dtype)
    return out
```

```python
import concourse.bass as bass
from concourse import mybir
from contextlib import ExitStack

F32 = mybir.dt.float32
I32 = mybir.dt.int32
ALU = mybir.AluOpType
ACT = mybir.ActivationFunctionType
AX = mybir.AxisListType

P = 128
D = 128
N = 50000
E = 75000
MIX = 4
K = 8
COLS = -(-E // (P * 2 * K)) * 2 * K
CHUNKS = COLS // K
FULL = E // COLS
REST = E - FULL * COLS
KM = 4
MCHUNKS = COLS // KM
NJ = N // P
KN = 3
NCHUNKS = NJ // KN
TAIL = N - P * NJ
BIG = 1.0e30
SKIP = 65536.0
EPS = 1e-05
SLOPE = 0.2


class Chain:

    def __init__(self, eng, sem):
        self.eng, self.sem, self.n = eng, sem, 0

    def link(self, ins):
        self.n += 1
        ins.then_inc(self.sem, 1)
        self.eng.wait_ge(self.sem, self.n)

    def mark(self, ins):
        self.n += 1
        ins.then_inc(self.sem, 1)

    def settle(self):
        self.eng.wait_ge(self.sem, self.n)

    def restart(self):
        self.eng.sem_inc(self.sem, 1)
        self.eng.wait_ge(self.sem, self.n + 1)
        self.eng.sem_clear(self.sem)
        self.n = 0


def run_bodies(eng, count, body):
    body(0, first=True, last=False)
    with eng.Fori(1, count - 1, 1) as i:
        body(i, first=False, last=False)
    body(count - 1, first=False, last=True)


def build(nc, t, out):
    ctx = ExitStack()
    with ctx:
        def sb(name, shape, dt=F32):
            return ctx.enter_context(nc.sbuf_tensor(name, shape, dt))

        def sem(name):
            return ctx.enter_context(nc.semaphore(name))

        def dram(name, shape):
            return nc.dram_tensor(name, shape, F32, kind="Internal").ap()

        gat_table = [dram(f"gat_table{l}", (N, D)) for l in range(3)]
        normed = dram("normed", (N, D))
        hidden = dram("hidden", (N, D))
        agg_table = dram("agg_table", (N, D))

        ident = sb("ident", [P, P])
        ones = sb("ones", [P, P])
        wlr = sb("wlr", [P, 3, 2 * D])
        att = sb("att", [P, 3, D])
        gat_bias = sb("gat_bias", [P, 3])
        b2_rows = sb("b2_rows", [P, D])
        ob_rows = sb("ob_rows", [P, D])
        w1t = sb("w1t", [P, D])
        wat = sb("wat", [P, D])
        wbt = sb("wbt", [P, MIX])
        w2t = sb("w2t", [P, 2, D])
        b1_col = sb("b1_col", [P, 1])

        edge_dst = sb("edge_dst", [P, COLS + 2])
        gather_idx = sb("gather_idx", [P, COLS + 2 * K], I32)
        scatter_idx = sb("scatter_idx", [P, COLS], I32)
        inherit = sb("inherit", [P, COLS], I32)
        cont = sb("cont", [P, COLS])
        pen = sb("pen", [P, COLS])
        mult = sb("mult", [P, COLS])
        head = sb("head", [P, COLS])
        head_mask = sb("head_mask", [P, COLS], I32)
        count = sb("count", [P, COLS + 1])
        inv_count = sb("inv_count", [P, COLS])
        first_node = sb("first_node", [P, 1], I32)
        fix_idx = sb("fix_idx", [P, 1], I32)
        take = sb("take", [P, P])
        take_pen = sb("take_pen", [P, P])

        run_max = sb("run_max", [P, COLS + 1])
        run_sum = sb("run_sum", [P, COLS + 1])
        wide = sb("wide", [P, COLS])

        with ExitStack() as scope:
            edge_in = scope.enter_context(nc.sbuf_tensor("edge_in", [P, COLS + 2], I32))
            src_in = scope.enter_context(nc.sbuf_tensor("src_in", [P, COLS], I32))
            w_in = scope.enter_context(nc.sbuf_tensor("w_in", [P, 5 * D], F32))
            first_dst = scope.enter_context(nc.sbuf_tensor("first_dst", [P, 1], F32))
            diag = scope.enter_context(nc.sbuf_tensor("diag", [P, P], F32))
            tri = scope.enter_context(nc.sbuf_tensor("tri", [P, P], F32))
            small = scope.enter_context(nc.sbuf_tensor("small", [P, 4], F32))
            ps_w = scope.enter_context(nc.psum_tensor("ps_w", [P, 4 * D], F32))
            ps_w2 = scope.enter_context(nc.psum_tensor("ps_w2", [P, 4 * D], F32))
            ps_g = scope.enter_context(nc.psum_tensor("ps_g", [P, 4 * D], F32))
            padded = sem("padded")
            edges_in = sem("edges_in")
            weights_in = sem("weights_in")
            consts_made = sem("consts_made")
            weights_turned = sem("weights_turned")
            diag_made = sem("diag_made")
            nodes_spread = sem("nodes_spread")
            take_made = sem("take_made")
            take_turned = sem("take_turned")
            setup_chain = sem("setup_chain")

            with nc.Block() as block:
                @block.sync
                def _(sp):
                    sp.wait_ge(padded, 2)
                    dst, src = t["dst"], t["src"]
                    main = dst[0:FULL * COLS].rearrange("(p c) -> p c", c=COLS)
                    with nc.allow_non_contiguous_dma(reason="one word of each run"):
                        sp.dma_start(edge_in[0:FULL, 1:COLS + 1], main).then_inc(edges_in, 16)
                        sp.dma_start(edge_in[FULL:FULL + 1, 1:REST + 1],
                                     dst[FULL * COLS:E].rearrange("(p c) -> p c", p=1)).then_inc(edges_in, 16)
                        sp.dma_start(edge_in[1:FULL + 1, 0:1], main[:, COLS - 1:COLS]).then_inc(edges_in, 16)
                        sp.dma_start(edge_in[0:FULL - 1, COLS + 1:COLS + 2], main[1:FULL, 0:1]).then_inc(edges_in, 16)
                        sp.dma_start(edge_in[FULL - 1:FULL, COLS + 1:COLS + 2],
                                     dst[FULL * COLS:FULL * COLS + 1].rearrange("(p c) -> p c", p=1)).then_inc(edges_in, 16)
                        sp.dma_start(src_in[0:FULL, :],
                                     src[0:FULL * COLS].rearrange("(p c) -> p c", c=COLS)).then_inc(edges_in, 16)
                        sp.dma_start(src_in[FULL:FULL + 1, 0:REST],
                                     src[FULL * COLS:E].rearrange("(p c) -> p c", p=1)).then_inc(edges_in, 16)

                @block.scalar
                def _(act):
                    with nc.allow_non_contiguous_dma(reason="biases, a word for each partition"):
                        for l in range(3):
                            act.dma_start(wlr[:, l, 0:D], t[f"L0_gnn_Wl{l}"]).then_inc(weights_in, 16)
                            act.dma_start(wlr[:, l, D:2 * D], t[f"L0_gnn_Wr{l}"]).then_inc(weights_in, 16)
                            act.dma_start(att[:, l, :], t[f"L0_gnn_att{l}"].unsqueeze(0).broadcast_to([P, D])).then_inc(weights_in, 16)
                            act.dma_start(gat_bias[:, l:l + 1], t[f"L0_gnn_b{l}"].unsqueeze(1)).then_inc(weights_in, 16)
                        act.dma_start(b1_col[:, :], t["L1_gnn_b1"].unsqueeze(1)).then_inc(weights_in, 16)
                    act.dma_start(b2_rows[:, :], t["L0_gnn_b2"].unsqueeze(0).broadcast_to([P, D])).then_inc(weights_in, 16)
                    act.dma_start(ob_rows[:, :], t["L1_gnn_b2"].unsqueeze(0).broadcast_to([P, D])).then_inc(weights_in, 16)
                    act.dma_start(w_in[:, 0:D], t["L1_gnn_W1"]).then_inc(weights_in, 16)
                    act.dma_start(w_in[:, D:2 * D], t["L1_gnn_WA"]).then_inc(weights_in, 16)
                    act.dma_start(w_in[:, 2 * D:4 * D], t["L1_gnn_W2"]).then_inc(weights_in, 16)
                    act.dma_start(w_in[0:MIX, 4 * D:5 * D], t["L1_gnn_WB"]).then_inc(weights_in, 16)

                @block.gpsimd
                def _(pool):
                    pool.memset(ones[:, :], 1.0).then_inc(consts_made, 1)
                    pool.memset(ident[:, :], 0.0).then_inc(consts_made, 1)
                    pool.wait_ge(consts_made, 2)
                    pool.affine_select(out=ident[:, :], in_=ident[:, :], compare_op=ALU.not_equal, fill=1.0,
                                       base=0, pattern=[[-1, P]], channel_multiplier=1).then_inc(consts_made, 1)
                    pool.affine_select(out=tri[:, :], in_=ones[:, :], compare_op=ALU.is_gt, fill=0.0,
                                       base=0, pattern=[[-1, P]], channel_multiplier=1).then_inc(consts_made, 1)

                @block.tensor
                def _(pe):
                    pe.wait_ge(consts_made, 4)
                    pe.wait_ge(weights_in, 16 * 19)
                    for j in range(4):
                        pe.transpose(ps_w[:, j * D:(j + 1) * D], w_in[:, j * D:(j + 1) * D], ident[:, :]).then_inc(weights_turned, 1)
                    pe.transpose(ps_w2[:, 0:MIX], w_in[0:MIX, 4 * D:5 * D], ident[0:MIX, 0:MIX]).then_inc(weights_turned, 1)
                    pe.wait_ge(diag_made, 1)
                    pe.matmul(ps_g[:, 0:P], ones[:, :], diag[:, :], start=True, stop=True).then_inc(nodes_spread, 1)
                    pe.wait_ge(take_made, 1)
                    pe.transpose(ps_g[:, P:2 * P], take[:, :], ident[:, :]).then_inc(take_turned, 1)

                @block.vector
                def _(dve):
                    chain = Chain(dve, setup_chain)
                    dve.memset(edge_in[:, :], N).then_inc(padded, 1)
                    dve.memset(src_in[:, :], 0).then_inc(padded, 1)
                    dve.wait_ge(edges_in, 16 * 7)
                    chain.mark(dve.memset(gather_idx[:, COLS:COLS + 2 * K], 0))
                    chain.mark(dve.memset(count[:, 0:1], 0.0))
                    chain.mark(dve.tensor_copy(gather_idx[:, 0:COLS], src_in[:, ::-1]))
                    chain.link(dve.tensor_copy(edge_dst[:, :], edge_in[:, ::-1]))
                    here, before, after = edge_dst[:, 1:COLS + 1], edge_dst[:, 0:COLS], edge_dst[:, 2:COLS + 2]
                    chain.link(dve.tensor_tensor(cont[:, :], here, before, ALU.is_equal))
                    chain.mark(dve.tensor_copy(inherit[:, :], cont[:, :]))
                    chain.link(dve.tensor_scalar(mult[:, :], cont[:, :], -1.0, 2.0, ALU.mult, ALU.add))
                    chain.link(dve.memset(cont[:, 0:1], 0.0))
                    chain.link(dve.tensor_scalar(pen[:, :], cont[:, :], 1.0, BIG, ALU.subtract, ALU.mult))
                    chain.link(dve.tensor_tensor(wide[:, :], here, after, ALU.is_equal))
                    chain.link(dve.scalar_tensor_tensor(scatter_idx[:, :], wide[:, :], SKIP, here, ALU.mult, ALU.add))
                    chain.link(dve.tensor_copy(first_dst[:, :], edge_dst[:, 1:2]))
                    chain.link(dve.tensor_scalar(wide[:, :], wide[:, :], -1.0, 1.0, ALU.mult, ALU.add))
                    chain.link(dve.scalar_tensor_tensor(head[:, :], here, first_dst[:, 0:1], wide[:, :], ALU.is_equal, ALU.mult))
                    chain.mark(dve.tensor_copy(head_mask[:, :], head[:, :]))
                    chain.link(dve.tensor_reduce(small[:, 0:1], head[:, :], AX.X, ALU.add))
                    chain.link(dve.tensor_scalar(small[:, 1:2], small[:, 0:1], -SKIP, SKIP, ALU.mult, ALU.add))
                    chain.mark(dve.tensor_tensor(fix_idx[:, :], first_dst[:, :], small[:, 1:2], ALU.add))
                    chain.mark(dve.tensor_scalar(first_node[:, :], first_dst[:, :], float(N - 1), None, ALU.min))
                    chain.link(dve.memset(wide[:, :], 1.0))
                    chain.link(dve.tensor_tensor_scan(count[:, 1:COLS + 1], cont[:, :], wide[:, :], 0.0, ALU.mult, ALU.add))
                    chain.mark(dve.reciprocal(inv_count[:, :], count[:, 1:COLS + 1]))
                    dve.wait_ge(consts_made, 4)
                    dve.tensor_scalar(diag[:, :], ident[:, :], first_dst[:, 0:1], None, ALU.mult).then_inc(diag_made, 1)
                    dve.wait_ge(nodes_spread, 1)
                    dve.scalar_tensor_tensor(take[:, :], ps_g[:, 0:P], edge_dst[:, COLS:COLS + 1], tri[:, :],
                                             ALU.is_equal, ALU.mult).then_inc(take_made, 1)
                    dve.wait_ge(take_turned, 1)
                    chain.mark(dve.tensor_scalar(take_pen[:, :], ps_g[:, P:2 * P], 1.0, BIG, ALU.subtract, ALU.mult))
                    dve.wait_ge(weights_turned, 5)
                    chain.mark(dve.tensor_copy(w1t[:, :], ps_w[:, 0:D]))
                    chain.mark(dve.tensor_copy(wat[:, :], ps_w[:, D:2 * D]))
                    chain.mark(dve.tensor_copy(w2t[:, :, :], ps_w[:, 2 * D:4 * D].rearrange("p (a b) -> p a b", a=2)))
                    chain.mark(dve.tensor_copy(wbt[:, :], ps_w2[:, 0:MIX]))
                    chain.settle()

        tables = [t["x"]] + gat_table
        for l in range(3):
            with ExitStack() as scope:
                gat_layer(nc, scope, l, tables[l], tables[l + 1], wlr[:, l, :], att[:, l, :],
                          gat_bias[:, l - 1:l] if l else None,
                          dict(ident=ident, ones=ones, gather_idx=gather_idx, scatter_idx=scatter_idx,
                               inherit=inherit, pen=pen, mult=mult, head=head, first_node=first_node,
                               fix_idx=fix_idx, take_pen=take_pen, run_max=run_max, run_sum=run_sum, wide=wide))

        with ExitStack() as scope:
            node_pass_hidden(nc, scope, t["x"], gat_table[2], normed, hidden,
                             dict(ident=ident, b2_rows=b2_rows, w1t=w1t, b1_col=b1_col))

        with ExitStack() as scope:
            mixing_pass(nc, scope, hidden, agg_table,
                        dict(ident=ident, gather_idx=gather_idx, scatter_idx=scatter_idx, cont=cont,
                             head=head, head_mask=head_mask, count=count, inv_count=inv_count,
                             fix_idx=fix_idx, take=take, wat=wat, wbt=wbt, wide=wide))

        with ExitStack() as scope:
            node_pass_out(nc, scope, agg_table, hidden, normed, out,
                          dict(ident=ident, ob_rows=ob_rows, w2t=w2t))


def gather(pool, dst, table, idx):
    return pool.indirect_dma_start(dst, None, table[:, :], bass.IndirectOffsetOnAxis(ap=idx, axis=0))


def scatter(pool, table, idx, rows):
    return pool.indirect_dma_start(table[:, :], bass.IndirectOffsetOnAxis(ap=idx, axis=0), rows, None,
                                   bounds_check=N - 1, oob_is_err=False)


def gat_layer(nc, scope, l, table_in, table_out, w, att_rows, bias, c):
    def sb(name, shape, dt=F32):
        return scope.enter_context(nc.sbuf_tensor(f"g{l}_{name}", shape, dt))

    def ps(name):
        return scope.enter_context(nc.psum_tensor(f"g{l}_{name}", [P, 512], F32))

    def sem(name):
        return scope.enter_context(nc.semaphore(f"g{l}_{name}"))

    rows = [sb(f"rows{s}", [P, K, D]) for s in range(2)]
    rows_t = [sb(f"rows_t{h}", [P, 4 * P]) for h in range(2)]
    xlr = [sb(f"xlr{s}", [P, K, 2 * D]) for s in range(2)]
    xr_kept = sb("xr_kept", [P, D])
    mixed = sb("mixed", [P, K, D])
    score = sb("score", [P, K])
    drop = sb("drop", [P, 2 * K])
    grown = sb("grown", [P, 2 * K])
    inv_sum = sb("inv_sum", [P, K])
    old_share = sb("old_share", [P, K])
    new_share = sb("new_share", [P, K])
    tmp = sb("tmp", [P, K])
    part = sb("part", [P, K, D])
    outs = [sb(f"outs{s}", [P, K, D]) for s in range(2)]
    gidx = [sb(f"gidx{s}", [P, K], I32) for s in range(2)]
    sidx = [sb(f"sidx{s}", [P, K], I32) for s in range(2)]
    mask = sb("mask", [P, K], I32)
    ps_t = [ps(f"ps_t{h}") for h in range(2)]
    ps_x = [ps(f"ps_x{j}") for j in range(4)]
    ps_b = [ps(f"ps_b{j}") for j in range(2)]
    diag = sb("diag", [P, 2 * P])
    share = sb("share", [P, P + 1])
    share_t = sb("share_t", [P, P])
    fixed = sb("fixed", [P, D])
    st = sb("st", [P, 8])

    seed_gathered = sem("seed_gathered")
    seed_turned = sem("seed_turned")
    seed_evacuated = sem("seed_evacuated")
    seed_projected = sem("seed_projected")
    idx_staged = sem("idx_staged")
    gathered = [sem(f"gathered{s}") for s in range(2)]
    turned = sem("turned")
    evacuated = sem("evacuated")
    projected = sem("projected")
    xlr_ready = sem("xlr_ready")
    summed = sem("summed")
    drop_ready = sem("drop_ready")
    grown_ready = sem("grown_ready")
    share_ready = sem("share_ready")
    part_ready = sem("part_ready")
    outs_ready = sem("outs_ready")
    scattered = [sem(f"scattered{s}") for s in range(2)]
    chain_sem = sem("chain")
    pool_passed = sem("pool_passed")
    dve_passed = sem("dve_passed")
    fix_gathered = sem("fix_gathered")
    fix_scattered = sem("fix_scattered")
    fix_dve = sem("fix_dve")
    fix_pe = sem("fix_pe")
    fix_act = sem("fix_act")

    def activate(act, dst, src):
        if bias is None:
            return act.activation(dst, src, ACT.Copy)
        return act.activation(dst, src, ACT.Relu, bias=bias)

    BODIES = CHUNKS // 2

    with nc.Block() as block:
        @block.gpsimd
        def _(pool):
            gather(pool, rows[1][:, 0, :], table_in, c["first_node"][:, 0:1]).then_inc(seed_gathered, 16)

            def gather_chunk(s):
                for k in range(K):
                    gather(pool, rows[s][:, k, :], table_in, gidx[s][:, k:k + 1]).then_inc(gathered[s], 16)

            def scatter_chunk(s):
                for k in range(K):
                    scatter(pool, table_out, sidx[s][:, k:k + 1], outs[s][:, k, :]).then_inc(scattered[s], 16)

            pool.wait_ge(idx_staged, 1)
            gather_chunk(0)
            pool.wait_ge(seed_turned, 1)
            pool.wait_ge(idx_staged, 2)
            gather_chunk(1)

            def body(i, first, last):
                for s in range(2):
                    n = i * 2 + s
                    if not last:
                        pool.wait_ge(turned, (n + 1) * 2)
                        pool.wait_ge(idx_staged, n + 3)
                        pool.sem_inc(pool_passed, 1)
                        gather_chunk(s)
                    pool.wait_ge(outs_ready, n + 1)
                    pool.sem_inc(pool_passed, 1)
                    scatter_chunk(s)
            run_bodies(pool, BODIES, body)
            for s in range(2):
                pool.wait_ge(scattered[s], 16 * K * BODIES)

        @block.tensor
        def _(pe):
            pe.wait_ge(seed_gathered, 16)
            pe.transpose(ps_b[0][:, 0:P], rows[1][:, 0, :], c["ident"][:, :]).then_inc(seed_turned, 1)
            pe.wait_ge(seed_evacuated, 1)
            pe.matmul(ps_b[0][:, P:2 * P], rows_t[0][:, 0:P], w[:, D:2 * D], start=True, stop=True).then_inc(seed_projected, 1)

            def body(i, first, last):
                for s in range(2):
                    n = i * 2 + s
                    pe.wait_ge(gathered[s], (i + 1) * (16 * K))
                    for h in range(2):
                        if not (first and s == 0):
                            pe.wait_ge(evacuated, n * 2 - 1 + h)
                        for k in range(4):
                            ins = pe.transpose(ps_t[h][:, k * P:(k + 1) * P], rows[s][:, 4 * h + k, :], c["ident"][:, :])
                        ins.then_inc(turned, 1)
                    for j in range(4):
                        if j % 2 == 0:
                            pe.wait_ge(evacuated, n * 2 + 1 + j // 2)
                        if not (first and s == 0):
                            pe.wait_ge(xlr_ready, n * 4 - 3 + j)
                        for k in range(2):
                            kk = (2 * j + k) % 4
                            ins = pe.matmul(ps_x[j][:, k * 2 * D:(k + 1) * 2 * D],
                                            rows_t[j // 2][:, kk * P:(kk + 1) * P], w, start=True, stop=True)
                        ins.then_inc(projected, 1)
            run_bodies(pe, BODIES, body)

        @block.scalar
        def _(act):
            act.wait_ge(seed_turned, 1)
            activate(act, rows_t[0][:, 0:P], ps_b[0][:, 0:P]).then_inc(seed_evacuated, 1)

            def evacuate(n, s, full):
                for h in range(2):
                    act.wait_ge(turned, n * 2 + 1 + h)
                    if full:
                        act.wait_ge(projected, n * 4 - 2 + 2 * h)
                    elif h == 0:
                        act.wait_ge(seed_projected, 1)
                    activate(act, rows_t[h][:, :], ps_t[h][:, :]).then_inc(evacuated, 1)
                for j in range(4):
                    act.wait_ge(projected, n * 4 + 1 + j)
                    act.activation(xlr[s][:, 2 * j:2 * j + 2, :], ps_x[j][:, :].rearrange("p (a b) -> p a b", a=2),
                                   ACT.Copy).then_inc(xlr_ready, 1)

            evacuate(0, 0, False)

            def body(i, first, last):
                for s in range(2):
                    n = i * 2 + s
                    if not (last and s == 1):
                        if not (first and s == 0):
                            act.wait_ge(summed, n)
                            act.wait_ge(part_ready, n * K)
                        evacuate(n + 1, 1 - s, True)
                    act.wait_ge(drop_ready, n + 1)
                    act.activation(grown[:, :], drop[:, :], ACT.Exp).then_inc(grown_ready, 1)
                    for k in range(K):
                        act.wait_ge(share_ready, n + 1)
                        act.activation(part[:, k, :], xlr[s][:, k, 0:D], ACT.Copy,
                                       scale=new_share[:, k:k + 1]).then_inc(part_ready, 1)
            run_bodies(act, BODIES, body)

        @block.vector
        def _(dve):
            chain = Chain(dve, chain_sem)
            chain.mark(dve.memset(c["run_max"][:, 0:1], -BIG))
            chain.mark(dve.memset(c["run_sum"][:, 0:1], 0.0))
            chain.mark(dve.memset(outs[1][:, K - 1, :], 0.0))
            dve.tensor_copy(gidx[0][:, :], c["gather_idx"][:, 0:K]).then_inc(idx_staged, 1)
            dve.tensor_copy(gidx[1][:, :], c["gather_idx"][:, K:2 * K]).then_inc(idx_staged, 1)
            dve.wait_ge(seed_projected, 1)
            chain.mark(dve.tensor_copy(xr_kept[:, :], ps_b[0][:, P:2 * P]))
            chain.settle()
            chain.restart()

            def body(i, first, last):
                for s in range(2):
                    n = i * 2 + s
                    c0 = n * K
                    now = bass.ds(c0, K)
                    new = bass.ds(c0 + 1, K)
                    run_max, run_sum = c["run_max"], c["run_sum"]
                    if not last:
                        dve.wait_ge(gathered[s], (i + 1) * (16 * K))
                        dve.tensor_scalar(gidx[s][:, :], c["gather_idx"][:, bass.ds(c0 + 2 * K, K)], 0.0, None,
                                          ALU.add).then_inc(idx_staged, 1)
                    chain.link(dve.tensor_copy(mask[:, :], c["inherit"][:, now]))
                    dve.wait_ge(xlr_ready, (n + 1) * 4)
                    dve.sem_inc(dve_passed, 1)
                    for k in range(K):
                        prev = xr_kept[:, :] if k == 0 else xlr[s][:, k - 1, D:2 * D]
                        chain.link(dve.copy_predicated(xlr[s][:, k, D:2 * D],
                                                       mask[:, k:k + 1].broadcast_to([P, D]), prev))
                    chain.link(dve.tensor_copy(xr_kept[:, :], xlr[s][:, K - 1, D:2 * D]))
                    dve.tensor_tensor(mixed[:, :, :], xlr[s][:, :, 0:D], xlr[s][:, :, D:2 * D], ALU.add).then_inc(summed, 1)
                    dve.wait_ge(summed, n + 1)
                    chain.link(dve.scalar_tensor_tensor(mixed[:, :, :], mixed[:, :, :], SLOPE, mixed[:, :, :], ALU.mult, ALU.max))
                    chain.link(dve.tensor_tensor(mixed[:, :, :], mixed[:, :, :],
                                                 att_rows.unsqueeze(1).broadcast_to([P, K, D]), ALU.mult))
                    chain.link(dve.tensor_reduce(score[:, :], mixed[:, :, :], AX.X, ALU.add))
                    chain.link(dve.tensor_tensor_scan(run_max[:, new], c["pen"][:, now], score[:, :],
                                                      run_max[:, bass.ds(c0, 1)], ALU.add, ALU.max))
                    chain.mark(dve.tensor_tensor(drop[:, K:2 * K], score[:, :], run_max[:, new], ALU.subtract))
                    chain.link(dve.tensor_tensor(tmp[:, :], run_max[:, now], c["pen"][:, now], ALU.add))
                    dve.tensor_tensor(drop[:, 0:K], tmp[:, :], run_max[:, new], ALU.subtract).then_inc(drop_ready, 1)
                    dve.wait_ge(grown_ready, n + 1)
                    chain.link(dve.tensor_tensor(grown[:, K:2 * K], grown[:, K:2 * K], c["mult"][:, now], ALU.mult))
                    chain.link(dve.tensor_tensor_scan(run_sum[:, new], grown[:, 0:K], grown[:, K:2 * K],
                                                      run_sum[:, bass.ds(c0, 1)], ALU.mult, ALU.add))
                    chain.mark(dve.reciprocal(inv_sum[:, :], run_sum[:, new]))
                    chain.link(dve.tensor_tensor(tmp[:, :], grown[:, 0:K], run_sum[:, now], ALU.mult))
                    chain.link(dve.tensor_tensor(old_share[:, :], tmp[:, :], inv_sum[:, :], ALU.mult))
                    dve.tensor_tensor(new_share[:, :], grown[:, K:2 * K], inv_sum[:, :], ALU.mult).then_inc(share_ready, 1)
                    if not first:
                        dve.wait_ge(scattered[s], i * (16 * K))
                    chain.link(dve.tensor_scalar(sidx[s][:, :], c["scatter_idx"][:, now], 0.0, None, ALU.add))
                    for k in range(K):
                        prev = outs[1 - s][:, K - 1, :] if k == 0 else outs[s][:, k - 1, :]
                        dve.wait_ge(part_ready, n * K + (k + 1))
                        ins = dve.scalar_tensor_tensor(outs[s][:, k, :], prev, old_share[:, k:k + 1], part[:, k, :],
                                                       ALU.mult, ALU.add)
                        if k < K - 1:
                            chain.link(ins)
                        else:
                            ins.then_inc(outs_ready, 1)
                    dve.wait_ge(outs_ready, n + 1)
                chain.restart()
            run_bodies(dve, BODIES, body)

    with nc.Block() as block:
        @block.gpsimd
        def _(pool):
            gather(pool, fixed[:, :], table_out, c["first_node"][:, 0:1]).then_inc(fix_gathered, 16)
            pool.wait_ge(fix_dve, 5)
            pool.wait_ge(fix_gathered, 16)
            scatter(pool, table_out, c["fix_idx"][:, 0:1], fixed[:, :]).then_inc(fix_scattered, 16)
            pool.wait_ge(fix_scattered, 16)

        @block.vector
        def _(dve):
            chain = Chain(dve, chain_sem)
            own_max, own_sum, top, own_share, total, inv = (st[:, j:j + 1] for j in range(6))
            last_max, last_sum = c["run_max"][:, COLS:COLS + 1], c["run_sum"][:, COLS:COLS + 1]
            chain.mark(dve.tensor_scalar(diag[:, 0:P], c["ident"][:, :], last_max, None, ALU.mult))
            chain.settle()
            dve.tensor_scalar(diag[:, P:2 * P], c["ident"][:, :], last_sum, None, ALU.mult).then_inc(fix_dve, 1)
            chain.link(dve.tensor_tensor(c["wide"][:, :], c["run_max"][:, 1:COLS + 1], c["head"][:, :], ALU.mult))
            chain.link(dve.tensor_reduce(own_max, c["wide"][:, :], AX.X, ALU.add))
            chain.link(dve.tensor_tensor(c["wide"][:, :], c["run_sum"][:, 1:COLS + 1], c["head"][:, :], ALU.mult))
            chain.link(dve.tensor_reduce(own_sum, c["wide"][:, :], AX.X, ALU.add))
            dve.wait_ge(fix_pe, 1)
            chain.link(dve.tensor_tensor(share[:, 0:P], ps_b[1][:, 0:P], c["take_pen"][:, :], ALU.add))
            chain.link(dve.tensor_reduce(top, share[:, 0:P], AX.X, ALU.max))
            chain.link(dve.tensor_tensor(top, top, own_max, ALU.max))
            chain.mark(dve.tensor_tensor(share[:, P:P + 1], own_max, top, ALU.subtract))
            chain.settle()
            dve.tensor_scalar(share[:, 0:P], share[:, 0:P], top, None, ALU.subtract).then_inc(fix_dve, 1)
            dve.wait_ge(fix_act, 1)
            chain.mark(dve.tensor_tensor(share[:, 0:P], share[:, 0:P], ps_b[1][:, P:2 * P], ALU.mult))
            chain.link(dve.tensor_tensor(own_share, share[:, P:P + 1], own_sum, ALU.mult))
            chain.link(dve.tensor_reduce(total, share[:, 0:P], AX.X, ALU.add))
            chain.link(dve.tensor_tensor(total, total, own_share, ALU.add))
            chain.link(dve.tensor_scalar(total, total, 1.0 / BIG, None, ALU.max))
            chain.link(dve.reciprocal(inv, total))
            chain.link(dve.tensor_tensor(own_share, own_share, inv, ALU.mult))
            dve.tensor_scalar(share[:, 0:P], share[:, 0:P], inv, None, ALU.mult).then_inc(fix_dve, 1)
            dve.wait_ge(fix_pe, 2)
            dve.tensor_copy(share_t[:, :], ps_b[0][:, 0:P]).then_inc(fix_dve, 1)
            dve.wait_ge(fix_pe, 3)
            dve.wait_ge(fix_gathered, 16)
            dve.scalar_tensor_tensor(fixed[:, :], fixed[:, :], own_share, ps_b[1][:, 2 * P:3 * P],
                                     ALU.mult, ALU.add).then_inc(fix_dve, 1)

        @block.scalar
        def _(act):
            act.wait_ge(fix_dve, 2)
            act.activation(share[:, :], share[:, :], ACT.Exp).then_inc(fix_act, 1)

        @block.tensor
        def _(pe):
            pe.wait_ge(fix_dve, 1)
            pe.matmul(ps_b[1][:, 0:2 * P], c["ones"][:, :], diag[:, :], start=True, stop=True).then_inc(fix_pe, 1)
            pe.wait_ge(fix_dve, 3)
            pe.transpose(ps_b[0][:, 0:P], share[:, 0:P], c["ident"][:, :]).then_inc(fix_pe, 1)
            pe.wait_ge(fix_dve, 4)
            pe.matmul(ps_b[1][:, 2 * P:3 * P], share_t[:, :], outs[1][:, K - 1, :], start=True, stop=True).then_inc(fix_pe, 1)


def norm_steps(dve, chain, rows, mean, var, sq, k):
    wide = [P, k, D]
    chain.link(dve.tensor_reduce(mean, rows, AX.X, ALU.add))
    chain.link(dve.tensor_scalar(mean, mean, 1.0 / D, None, ALU.mult))
    chain.link(dve.tensor_tensor(rows, rows, mean.unsqueeze(2).broadcast_to(wide), ALU.subtract))
    chain.link(dve.tensor_tensor(sq, rows, rows, ALU.mult))
    chain.link(dve.tensor_reduce(var, sq, AX.X, ALU.add))


def node_chunks(eng, body):
    pairs = NCHUNKS // 2
    for s in range(2):
        body(s, s, True)
    with eng.Fori(1, pairs, 1) as i:
        for s in range(2):
            body(i * 2 + s, s, False)
    body(NCHUNKS, 0, False)


def node_rows(table, n, store=False):
    if isinstance(n, int) and n == NCHUNKS:
        lo = N - TAIL if store else N - P
        return table[lo:N, :].rearrange("(p j) d -> p j d", j=1)
    return table[0:P * NJ, :].rearrange("(p j) d -> p j d", p=P)[:, bass.ds(n * KN, KN), :]


def node_pass_hidden(nc, scope, x, gat_out, normed, hidden, c):
    def sb(name, shape, dt=F32):
        return scope.enter_context(nc.sbuf_tensor(f"nh_{name}", shape, dt))

    def ps(name):
        return scope.enter_context(nc.psum_tensor(f"nh_{name}", [P, 512], F32))

    def sem(name):
        return scope.enter_context(nc.semaphore(f"nh_{name}"))

    x_in = [sb(f"x_in{s}", [P, KN, D]) for s in range(2)]
    g_in = [sb(f"g_in{s}", [P, KN, D]) for s in range(2)]
    y = [sb(f"y{s}", [P, KN, D]) for s in range(2)]
    y_t = sb("y_t", [P, KN * P])
    h_t = sb("h_t", [P, KN * P])
    h = [sb(f"h{s}", [P, KN, D]) for s in range(2)]
    sq = sb("sq", [P, KN, D])
    mean, var = sb("mean", [P, KN]), sb("var", [P, KN])
    rstd = sb("rstd", [P, KN])
    half = sb("half", [P, KN])
    ps_y, ps_h, ps_b = ps("ps_y"), ps("ps_h"), ps("ps_b")

    loaded = [sem(f"loaded{s}") for s in range(2)]
    added = sem("added")
    var_ready = sem("var_ready")
    rstd_ready = sem("rstd_ready")
    y_ready = sem("y_ready")
    turned = sem("turned")
    y_t_ready = sem("y_t_ready")
    projected = sem("projected")
    h_t_ready = sem("h_t_ready")
    back = sem("back")
    h_ready = sem("h_ready")
    stored = [sem(f"stored{s}") for s in range(2)]
    chain_sem = sem("chain")

    def cols(n):
        return 1 if isinstance(n, int) and n == NCHUNKS else KN

    def tail(n):
        return isinstance(n, int) and n == NCHUNKS

    def nth(n):
        return NCHUNKS // 2 + 1 if tail(n) else None

    with nc.Block() as block:
        @block.sync
        def _(sp):
            def load(n, s, ahead):
                k = cols(n)
                sp.dma_start(x_in[s][:, 0:k, :], node_rows(x, n)).then_inc(loaded[s], 16)
                sp.dma_start(g_in[s][:, 0:k, :], node_rows(gat_out, n)).then_inc(loaded[s], 16)

            def store(n, s):
                k = cols(n)
                lo = P - TAIL if tail(n) else 0
                sp.wait_ge(y_ready, n + 1)
                sp.dma_start(node_rows(normed, n, True), y[s][lo:P, 0:k, :]).then_inc(stored[s], 16)
                sp.wait_ge(h_ready, n + 1)
                sp.dma_start(node_rows(hidden, n, True), h[s][lo:P, 0:k, :]).then_inc(stored[s], 16)

            load(0, 0, False)
            load(1, 1, False)

            def pair(i, final):
                for s in range(2):
                    n = i * 2 + s
                    sp.wait_ge(added, n + 1)
                    if not final:
                        load(n + 2, s, True)
                    elif s == 0:
                        load(NCHUNKS, s, True)
                    store(n, s)
            with sp.Fori(0, NCHUNKS // 2 - 1, 1) as i:
                pair(i, False)
            pair(NCHUNKS // 2 - 1, True)
            store(NCHUNKS, 0)
            sp.wait_ge(stored[0], 32 * (NCHUNKS // 2 + 1))
            sp.wait_ge(stored[1], 32 * (NCHUNKS // 2))

        @block.gpsimd
        def _(pool):
            pool.memset(half[:, :], -0.5).then_inc(rstd_ready, 1)
            pool.wait_ge(rstd_ready, 1)

            def body(n, s, first):
                k = cols(n)
                pool.wait_ge(var_ready, n + 1)
                pool.tensor_tensor(rstd[:, 0:k], var[:, 0:k], half[:, 0:k], ALU.pow).then_inc(rstd_ready, 1)
            node_chunks(pool, body)

        @block.vector
        def _(dve):
            chain = Chain(dve, chain_sem)

            def chunk(n, s, slot_turn, first):
                k = cols(n)
                wide = [P, k, D]
                dve.wait_ge(loaded[s], slot_turn * 32)
                if not first:
                    dve.wait_ge(stored[s], (slot_turn - 1) * 32)
                dve.tensor_tensor(y[s][:, 0:k, :], x_in[s][:, 0:k, :], g_in[s][:, 0:k, :], ALU.add).then_inc(added, 1)
                dve.wait_ge(added, n + 1)
                rows = y[s][:, 0:k, :]
                chain.link(dve.tensor_tensor(rows, rows, c["b2_rows"][:, :].unsqueeze(1).broadcast_to(wide), ALU.add))
                norm_steps(dve, chain, rows, mean[:, 0:k], var[:, 0:k], sq[:, 0:k, :], k)
                dve.tensor_scalar(var[:, 0:k], var[:, 0:k], 1.0 / D, EPS, ALU.mult, ALU.add).then_inc(var_ready, 1)
                dve.wait_ge(rstd_ready, n + 2)
                dve.tensor_tensor(rows, rows, rstd[:, 0:k].unsqueeze(2).broadcast_to(wide), ALU.mult).then_inc(y_ready, 1)
                dve.wait_ge(y_ready, n + 1)
                chain.restart()
            chunk(0, 0, 1, True)
            chunk(1, 1, 1, True)
            with dve.Fori(1, NCHUNKS // 2, 1) as i:
                for s in range(2):
                    chunk(i * 2 + s, s, i + 1, False)
            chunk(NCHUNKS, 0, NCHUNKS // 2 + 1, False)

        @block.tensor
        def _(pe):
            def body(n, s, first):
                k = cols(n)
                pe.wait_ge(y_ready, n + 1)
                if not (isinstance(n, int) and n == 0):
                    pe.wait_ge(y_t_ready, n)
                for j in range(k):
                    ins = pe.transpose(ps_y[:, j * P:(j + 1) * P], y[s][:, j, :], c["ident"][:, :])
                ins.then_inc(turned, 1)
                pe.wait_ge(y_t_ready, n + 1)
                if not (isinstance(n, int) and n == 0):
                    pe.wait_ge(h_t_ready, n)
                pe.matmul(ps_h[:, 0:k * P], c["w1t"][:, :], y_t[:, 0:k * P], start=True, stop=True).then_inc(projected, 1)
                pe.wait_ge(h_t_ready, n + 1)
                if not (isinstance(n, int) and n == 0):
                    pe.wait_ge(h_ready, n)
                for j in range(k):
                    ins = pe.transpose(ps_b[:, j * P:(j + 1) * P], h_t[:, j * P:(j + 1) * P], c["ident"][:, :])
                ins.then_inc(back, 1)
            node_chunks(pe, body)

        @block.scalar
        def _(act):
            def chunk(n, s, slot_turn, first):
                k = cols(n)
                act.wait_ge(turned, n + 1)
                act.activation(y_t[:, 0:k * P], ps_y[:, 0:k * P], ACT.Copy).then_inc(y_t_ready, 1)
                act.wait_ge(projected, n + 1)
                act.activation(h_t[:, 0:k * P], ps_h[:, 0:k * P], ACT.Gelu, bias=c["b1_col"][:, 0:1]).then_inc(h_t_ready, 1)
                act.wait_ge(back, n + 1)
                if not first:
                    act.wait_ge(stored[s], (slot_turn - 1) * 32)
                act.activation(h[s][:, 0:k, :], ps_b[:, 0:k * P].rearrange("p (a b) -> p a b", a=k),
                               ACT.Copy).then_inc(h_ready, 1)
            chunk(0, 0, 1, True)
            chunk(1, 1, 1, True)
            with act.Fori(1, NCHUNKS // 2, 1) as i:
                for s in range(2):
                    chunk(i * 2 + s, s, i + 1, False)
            chunk(NCHUNKS, 0, NCHUNKS // 2 + 1, False)


def mixing_pass(nc, scope, hidden, agg_table, c):
    def sb(name, shape, dt=F32):
        return scope.enter_context(nc.sbuf_tensor(f"mx_{name}", shape, dt))

    def ps(name):
        return scope.enter_context(nc.psum_tensor(f"mx_{name}", [P, 512], F32))

    def sem(name):
        return scope.enter_context(nc.semaphore(f"mx_{name}"))

    RING = 4
    BODIES = MCHUNKS // RING
    AHEAD = 3
    K = KM
    MD = MIX * D
    rows = [sb(f"rows{r}", [P, K, D]) for r in range(RING)]
    gidx = [sb(f"gidx{r}", [P, K], I32) for r in range(RING)]
    sidx = [sb(f"sidx{s}", [P, K], I32) for s in range(2)]
    mask = sb("mask", [P, K], I32)
    go_on = sb("go_on", [P, K])
    rows_t = [sb(f"rows_t{s}", [P, K * P]) for s in range(2)]
    up_t = [sb(f"up_t{s}", [P, K * P]) for s in range(2)]
    mix = [sb(f"mix{s}", [P, K, MIX]) for s in range(2)]
    prod = [sb(f"prod{s}", [P, K, MD]) for s in range(2)]
    agg = [sb(f"agg{s}", [P, K, MD]) for s in range(2)]
    act_agg = [sb(f"act_agg{s}", [P, K, MD]) for s in range(2)]
    mix_sum = sb("mix_sum", [P, MIX, COLS + 1])
    mix_mean = sb("mix_mean", [P, K, MIX])
    outs = [sb(f"outs{s}", [P, K, D]) for s in range(2)]
    own = sb("own", [P, MD])
    states = sb("states", [P, MIX + 1])
    own_small = sb("own_small", [P, MIX + 1])
    total = sb("total", [P, MD])
    fixed = sb("fixed", [P, D])
    ps_t = [ps(f"ps_t{s}") for s in range(2)]
    ps_u = [ps(f"ps_u{s}") for s in range(2)]
    ps_m = [ps(f"ps_m{s}") for s in range(2)]
    ps_b = [ps(f"ps_b{s}") for s in range(2)]

    idx_staged = sem("idx_staged")
    gathered = [sem(f"gathered{r}") for r in range(RING)]
    turned = sem("turned")
    rows_t_ready = sem("rows_t_ready")
    up_done = sem("up_done")
    up_ready = sem("up_ready")
    mix_done = sem("mix_done")
    mix_ready = sem("mix_ready")
    prod_ready = sem("prod_ready")
    agg_ready = sem("agg_ready")
    gelu_ready = sem("gelu_ready")
    mixed = sem("mixed")
    outs_ready = sem("outs_ready")
    scattered = [sem(f"scattered{s}") for s in range(2)]
    chain_sem = sem("chain")
    pool_passed = sem("pool_passed")
    dve_passed = sem("dve_passed")
    fix_pe, fix_act, fix_dve, fix_scattered = sem("fix_pe"), sem("fix_act"), sem("fix_dve"), sem("fix_scattered")

    def heads(ap):
        return ap.rearrange("p (m d) -> p m d", m=MIX)

    with nc.Block() as block:
        @block.gpsimd
        def _(pool):
            def gather_chunk(r):
                for k in range(K):
                    gather(pool, rows[r][:, k, :], hidden, gidx[r][:, k:k + 1]).then_inc(gathered[r], 16)

            for n in range(AHEAD):
                pool.wait_ge(idx_staged, n + 1)
                gather_chunk(n)

            def body(i, first, last):
                for r in range(RING):
                    n = i * RING + r
                    if not (last and r + AHEAD >= RING):
                        if not (first and r == 0):
                            pool.wait_ge(prod_ready, n * K)
                        pool.wait_ge(idx_staged, n + AHEAD + 1)
                        pool.sem_inc(pool_passed, 1)
                        gather_chunk((r + AHEAD) % RING)
                    pool.wait_ge(outs_ready, n + 1)
                    pool.sem_inc(pool_passed, 1)
                    for k in range(K):
                        scatter(pool, agg_table, sidx[r % 2][:, k:k + 1], outs[r % 2][:, k, :]).then_inc(scattered[r % 2], 16)
            run_bodies(pool, BODIES, body)
            for s in range(2):
                pool.wait_ge(scattered[s], 16 * K * MCHUNKS // 2)

        @block.tensor
        def _(pe):
            def body(i, first, last):
                for r in range(RING):
                    n, s = i * RING + r, r % 2
                    early = first and r < 2
                    pe.wait_ge(gathered[r], (i + 1) * (16 * K))
                    if not early:
                        pe.wait_ge(rows_t_ready, n - 1)
                    for k in range(K):
                        ins = pe.transpose(ps_t[s][:, k * P:(k + 1) * P], rows[r][:, k, :], c["ident"][:, :])
                    ins.then_inc(turned, 1)
                    pe.wait_ge(rows_t_ready, n + 1)
                    if not early:
                        pe.wait_ge(up_ready, n - 1)
                    pe.matmul(ps_u[s][:, :], c["wat"][:, :], rows_t[s][:, :], start=True, stop=True).then_inc(up_done, 1)
                    pe.wait_ge(up_ready, n + 1)
                    if not early:
                        pe.wait_ge(mix_ready, n - 1)
                    for k in range(K):
                        ins = pe.matmul(ps_m[s][:, k * MIX:(k + 1) * MIX], up_t[s][:, k * P:(k + 1) * P],
                                        c["wbt"][:, :], start=True, stop=True)
                    ins.then_inc(mix_done, 1)
            run_bodies(pe, BODIES, body)

        @block.scalar
        def _(act):
            def front(n, r, early):
                s = r % 2
                act.wait_ge(turned, n + 1)
                if not early:
                    act.wait_ge(up_done, n - 1)
                act.activation(rows_t[s][:, :], ps_t[s][:, :], ACT.Copy).then_inc(rows_t_ready, 1)
                act.wait_ge(up_done, n + 1)
                if not early:
                    act.wait_ge(mix_done, n - 1)
                act.activation(up_t[s][:, :], ps_u[s][:, :], ACT.Gelu).then_inc(up_ready, 1)
                act.wait_ge(mix_done, n + 1)
                if not early:
                    act.wait_ge(mixed, n - 1)
                    act.wait_ge(prod_ready, (n - 1) * K)
                act.activation(mix[s][:, :, :], ps_m[s][:, 0:K * MIX].rearrange("p (k m) -> p k m", m=MIX),
                               ACT.Copy).then_inc(mix_ready, 1)
                act.wait_ge(mix_ready, n + 1)

            def products(n, r, early):
                s = r % 2
                for k in range(K):
                    if not early:
                        act.wait_ge(agg_ready, (n - 2) * K + (k + 1))
                    for m in range(MIX):
                        ins = act.activation(prod[s][:, k, m * D:(m + 1) * D], rows[r][:, k, :], ACT.Copy,
                                             scale=mix[s][:, k, m:m + 1])
                    ins.then_inc(prod_ready, 1)

            def gelus(n, r, early):
                s = r % 2
                if not early:
                    act.wait_ge(outs_ready, n - 1)
                for k in range(K):
                    act.wait_ge(agg_ready, n * K + (k + 1))
                    act.activation(act_agg[s][:, k, :], agg[s][:, k, :], ACT.Gelu).then_inc(gelu_ready, 1)

            front(0, 0, True)
            products(0, 0, True)

            def body(i, first, last):
                for r in range(RING):
                    n = i * RING + r
                    if not (last and r == RING - 1):
                        front(n + 1, (r + 1) % RING, first and r < 1)
                        products(n + 1, (r + 1) % RING, first and r < 1)
                    gelus(n, r, first and r < 2)
            run_bodies(act, BODIES, body)

        @block.vector
        def _(dve):
            chain = Chain(dve, chain_sem)
            chain.mark(dve.memset(mix_sum[:, :, 0:1], 0.0))
            chain.mark(dve.memset(agg[1][:, K - 1, :], 0.0))
            chain.mark(dve.memset(own[:, :], 0.0))
            for n in range(AHEAD):
                dve.tensor_copy(gidx[n][:, :], c["gather_idx"][:, n * K:(n + 1) * K]).then_inc(idx_staged, 1)
            chain.settle()
            chain.restart()

            def body(i, first, last):
                for r in range(RING):
                    n, s = i * RING + r, r % 2
                    c0 = n * K
                    now = bass.ds(c0, K)
                    a = (r + AHEAD) % RING
                    if not (last and r + AHEAD >= RING):
                        if not (first and r == 0):
                            dve.wait_ge(gathered[a], (i + (1 if r + AHEAD >= RING and r > 0 else 0)) * (16 * K))
                        dve.tensor_scalar(gidx[a][:, :], c["gather_idx"][:, bass.ds(c0 + AHEAD * K, K)], 0.0, None,
                                          ALU.add).then_inc(idx_staged, 1)
                    chain.mark(dve.tensor_copy(go_on[:, :], c["cont"][:, now]))
                    chain.link(dve.tensor_copy(mask[:, :], c["head_mask"][:, now]))
                    dve.wait_ge(mix_ready, n + 1)
                    for m in range(MIX):
                        ins = dve.tensor_tensor_scan(mix_sum[:, m, bass.ds(c0 + 1, K)], go_on[:, :], mix[s][:, :, m],
                                                     mix_sum[:, m, bass.ds(c0, 1)], ALU.mult, ALU.add)
                        if m < MIX - 1:
                            chain.mark(ins)
                    ins.then_inc(mixed, 1)
                    chain.settle()
                    dve.wait_ge(mixed, n + 1)
                    chain.link(dve.tensor_tensor(mix_mean[:, :, :], mix_sum[:, :, bass.ds(c0 + 1, K)].rearrange("p m k -> p k m"),
                                                 c["inv_count"][:, now].unsqueeze(2).broadcast_to([P, K, MIX]), ALU.mult))
                    if not (first and r < 2):
                        dve.wait_ge(gelu_ready, (n - 1) * K)
                    for k in range(K):
                        prev = agg[1 - s][:, K - 1, :] if k == 0 else agg[s][:, k - 1, :]
                        dve.wait_ge(prod_ready, n * K + (k + 1))
                        dve.scalar_tensor_tensor(agg[s][:, k, :], prev, go_on[:, k:k + 1], prod[s][:, k, :],
                                                 ALU.mult, ALU.add).then_inc(agg_ready, 1)
                        dve.wait_ge(agg_ready, n * K + (k + 1))
                    dve.sem_inc(dve_passed, 1)
                    for k in range(K):
                        chain.link(dve.copy_predicated(own[:, :], mask[:, k:k + 1].broadcast_to([P, MD]), agg[s][:, k, :]))
                    for k in range(K):
                        dve.wait_ge(gelu_ready, n * K + (k + 1))
                        chain.mark(dve.tensor_tensor(heads(act_agg[s][:, k, :]), heads(act_agg[s][:, k, :]),
                                                     mix_mean[:, k, :].unsqueeze(2).broadcast_to([P, MIX, D]), ALU.mult))
                    chain.settle()
                    if not (first and r < 2):
                        turn = (i * RING + (r - r % 2)) // 2 if isinstance(i, int) else i * (RING // 2) + r // 2
                        dve.wait_ge(scattered[s], turn * (16 * K))
                    chain.link(dve.tensor_scalar(sidx[s][:, :], c["scatter_idx"][:, now], 0.0, None, ALU.add))
                    dve.tensor_reduce(outs[s][:, :, :], act_agg[s][:, :, :].rearrange("p k (m d) -> p k d m", m=MIX),
                                      AX.X, ALU.add).then_inc(outs_ready, 1)
                    dve.wait_ge(outs_ready, n + 1)
                chain.restart()
            run_bodies(dve, BODIES, body)

    with nc.Block() as block:
        @block.gpsimd
        def _(pool):
            pool.wait_ge(fix_dve, 3)
            scatter(pool, agg_table, c["fix_idx"][:, 0:1], fixed[:, :]).then_inc(fix_scattered, 16)
            pool.wait_ge(fix_scattered, 16)

        @block.tensor
        def _(pe):
            pe.matmul(ps_b[0][:, :], c["take"][:, :], agg[1][:, K - 1, :], start=True, stop=True).then_inc(fix_pe, 1)
            pe.wait_ge(fix_dve, 1)
            pe.matmul(ps_b[1][:, 0:MIX + 1], c["take"][:, :], states[:, :], start=True, stop=True).then_inc(fix_pe, 1)

        @block.scalar
        def _(act):
            act.wait_ge(fix_dve, 2)
            act.activation(total[:, :], total[:, :], ACT.Gelu).then_inc(fix_act, 1)

        @block.vector
        def _(dve):
            chain = Chain(dve, chain_sem)
            chain.link(dve.tensor_copy(states[:, 0:MIX], mix_sum[:, :, COLS]))
            dve.tensor_copy(states[:, MIX:MIX + 1], c["count"][:, COLS:COLS + 1]).then_inc(fix_dve, 1)
            dve.wait_ge(fix_pe, 1)
            dve.tensor_tensor(total[:, :], own[:, :], ps_b[0][:, :], ALU.add).then_inc(fix_dve, 1)
            for m in range(MIX + 1):
                series = mix_sum[:, m, 1:COLS + 1] if m < MIX else c["count"][:, 1:COLS + 1]
                chain.link(dve.tensor_tensor(c["wide"][:, :], series, c["head"][:, :], ALU.mult))
                chain.link(dve.tensor_reduce(own_small[:, m:m + 1], c["wide"][:, :], AX.X, ALU.add))
            dve.wait_ge(fix_pe, 2)
            chain.link(dve.tensor_tensor(own_small[:, :], own_small[:, :], ps_b[1][:, 0:MIX + 1], ALU.add))
            chain.link(dve.tensor_scalar(own_small[:, MIX:MIX + 1], own_small[:, MIX:MIX + 1], 1.0, None, ALU.max))
            chain.link(dve.reciprocal(states[:, 0:1], own_small[:, MIX:MIX + 1]))
            chain.link(dve.tensor_scalar(own_small[:, 0:MIX], own_small[:, 0:MIX], states[:, 0:1], None, ALU.mult))
            dve.wait_ge(fix_act, 1)
            chain.link(dve.tensor_tensor(heads(total[:, :]), heads(total[:, :]),
                                         own_small[:, 0:MIX].unsqueeze(2).broadcast_to([P, MIX, D]), ALU.mult))
            dve.tensor_reduce(fixed[:, :], total[:, :].rearrange("p (m d) -> p d m", m=MIX), AX.X, ALU.add).then_inc(fix_dve, 1)


def node_pass_out(nc, scope, agg_table, hidden, normed, out, c):
    def sb(name, shape, dt=F32):
        return scope.enter_context(nc.sbuf_tensor(f"no_{name}", shape, dt))

    def ps(name):
        return scope.enter_context(nc.psum_tensor(f"no_{name}", [P, 512], F32))

    def sem(name):
        return scope.enter_context(nc.semaphore(f"no_{name}"))

    parts = [[sb(f"parts{a}{s}", [P, KN, D]) for s in range(2)] for a in range(2)]
    x_in = [sb(f"x_in{s}", [P, KN, D]) for s in range(2)]
    feat_t = [[sb(f"feat_t{a}{s}", [P, KN * P]) for s in range(2)] for a in range(2)]
    y = [sb(f"y{s}", [P, KN, D]) for s in range(2)]
    sq = sb("sq", [P, KN, D])
    mean, var = sb("mean", [P, KN]), sb("var", [P, KN])
    rstd = sb("rstd", [P, KN])
    half = sb("half", [P, KN])
    ps_f = [[ps(f"ps_f{a}{s}") for s in range(2)] for a in range(2)]
    ps_o = [ps(f"ps_o{s}") for s in range(2)]

    loaded = [sem(f"loaded{s}") for s in range(2)]
    turned = sem("turned")
    feat_ready = sem("feat_ready")
    projected = sem("projected")
    added = sem("added")
    var_ready = sem("var_ready")
    rstd_ready = sem("rstd_ready")
    y_ready = sem("y_ready")
    stored = [sem(f"stored{s}") for s in range(2)]
    chain_sem = sem("chain")

    def tail(n):
        return isinstance(n, int) and n == NCHUNKS

    def cols(n):
        return 1 if tail(n) else KN

    with nc.Block() as block:
        @block.sync
        def _(sp):
            def load(n, s):
                k = cols(n)
                for tile, table in ((parts[0][s], agg_table), (parts[1][s], hidden), (x_in[s], normed)):
                    sp.dma_start(tile[:, 0:k, :], node_rows(table, n)).then_inc(loaded[s], 16)

            def store(n, s):
                lo = P - TAIL if tail(n) else 0
                sp.wait_ge(y_ready, n + 1)
                sp.dma_start(node_rows(out, n, True), y[s][lo:P, 0:cols(n), :]).then_inc(stored[s], 16)

            load(0, 0)
            load(1, 1)

            def pair(i, final):
                for s in range(2):
                    n = i * 2 + s
                    if not final or s == 0:
                        sp.wait_ge(added, n + 1)
                        load(NCHUNKS if final else n + 2, s)
                    store(n, s)
            with sp.Fori(0, NCHUNKS // 2 - 1, 1) as i:
                pair(i, False)
            pair(NCHUNKS // 2 - 1, True)
            store(NCHUNKS, 0)
            sp.wait_ge(stored[0], 16 * (NCHUNKS // 2 + 1))
            sp.wait_ge(stored[1], 16 * (NCHUNKS // 2))

        @block.gpsimd
        def _(pool):
            pool.memset(half[:, :], -0.5).then_inc(rstd_ready, 1)
            pool.wait_ge(rstd_ready, 1)

            def body(n, s, first):
                k = cols(n)
                pool.wait_ge(var_ready, n + 1)
                pool.tensor_tensor(rstd[:, 0:k], var[:, 0:k], half[:, 0:k], ALU.pow).then_inc(rstd_ready, 1)
            node_chunks(pool, body)

        @block.tensor
        def _(pe):
            def chunk(n, s, slot_turn, first):
                k = cols(n)
                pe.wait_ge(loaded[s], slot_turn * 48)
                for a in range(2):
                    if not first:
                        pe.wait_ge(feat_ready, n * 2 - 3 + a)
                    for j in range(k):
                        ins = pe.transpose(ps_f[a][s][:, j * P:(j + 1) * P], parts[a][s][:, j, :], c["ident"][:, :])
                    ins.then_inc(turned, 1)
                pe.wait_ge(feat_ready, n * 2 + 2)
                if not first:
                    pe.wait_ge(added, n - 1)
                for j in range(k):
                    for a in range(2):
                        ins = pe.matmul(ps_o[s][:, j * P:(j + 1) * P], feat_t[a][s][:, j * P:(j + 1) * P],
                                        c["w2t"][:, a, :], start=(a == 0), stop=(a == 1))
                ins.then_inc(projected, 1)
            chunk(0, 0, 1, True)
            chunk(1, 1, 1, True)
            with pe.Fori(1, NCHUNKS // 2, 1) as i:
                for s in range(2):
                    chunk(i * 2 + s, s, i + 1, False)
            chunk(NCHUNKS, 0, NCHUNKS // 2 + 1, False)

        @block.scalar
        def _(act):
            def body(n, s, first):
                k = cols(n)
                for a in range(2):
                    act.wait_ge(turned, n * 2 + 1 + a)
                    if not first:
                        act.wait_ge(projected, n - 1)
                    act.activation(feat_t[a][s][:, 0:k * P], ps_f[a][s][:, 0:k * P], ACT.Gelu).then_inc(feat_ready, 1)
            node_chunks(act, body)

        @block.vector
        def _(dve):
            chain = Chain(dve, chain_sem)

            def chunk(n, s, slot_turn, first):
                k = cols(n)
                wide = [P, k, D]
                rows = y[s][:, 0:k, :]
                dve.wait_ge(loaded[s], slot_turn * 48)
                dve.wait_ge(projected, n + 1)
                if not first:
                    dve.wait_ge(stored[s], (slot_turn - 1) * 16)
                dve.tensor_tensor(rows, ps_o[s][:, 0:k * P].rearrange("p (a b) -> p a b", a=k), x_in[s][:, 0:k, :],
                                  ALU.add).then_inc(added, 1)
                dve.wait_ge(added, n + 1)
                chain.link(dve.tensor_tensor(rows, rows, c["ob_rows"][:, :].unsqueeze(1).broadcast_to(wide), ALU.add))
                norm_steps(dve, chain, rows, mean[:, 0:k], var[:, 0:k], sq[:, 0:k, :], k)
                dve.tensor_scalar(var[:, 0:k], var[:, 0:k], 1.0 / D, EPS, ALU.mult, ALU.add).then_inc(var_ready, 1)
                dve.wait_ge(rstd_ready, n + 2)
                dve.tensor_tensor(rows, rows, rstd[:, 0:k].unsqueeze(2).broadcast_to(wide), ALU.mult).then_inc(y_ready, 1)
                dve.wait_ge(y_ready, n + 1)
                chain.restart()
            chunk(0, 0, 1, True)
            chunk(1, 1, 1, True)
            with dve.Fori(1, NCHUNKS // 2, 1) as i:
                for s in range(2):
                    chunk(i * 2 + s, s, i + 1, False)
            chunk(NCHUNKS, 0, NCHUNKS // 2 + 1, False)


_INS = ["x", "src", "dst"] + [f"L0_gnn_{w}{l}" for l in range(3) for w in ("Wl", "Wr", "att", "b")] \
    + [f"L1_gnn_{w}" for w in ("W1", "b1", "WA", "WB", "W2", "b2")]


def kernel(**inputs):
    import numpy as _np
    import concourse.bacc as _bacc
    from concourse import mybir as _mybir
    from concourse.bass_utils import run_bass_kernel_spmd as _run

    nc = _bacc.Bacc("TRN2", target_bir_lowering=False, num_devices=1)
    arrays, args = {}, {}
    for name in _INS:
        a = _np.ascontiguousarray(inputs[name])
        arrays[f"in_{name}"] = a
        args[name] = nc.dram_tensor(f"in_{name}", a.shape, _mybir.dt.from_np(a.dtype), kind="ExternalInput").ap()
    out = nc.dram_tensor("out_0", (N, D), F32, kind="ExternalOutput").ap()
    build(nc, args, out)
    r = _run(nc, [arrays], core_ids=[0])
    return r.results[0]["out_0"]
```

```python
import concourse.bass as bass
from concourse import mybir
from contextlib import ExitStack

F32 = mybir.dt.float32
I32 = mybir.dt.int32
ALU = mybir.AluOpType
ACT = mybir.ActivationFunctionType
AX = mybir.AxisListType

P = 128
D = 128
N = 50000
E = 75000
MIX = 4
K = 8
COLS = -(-E // (P * 2 * K)) * 2 * K
CHUNKS = COLS // K
FULL = E // COLS
REST = E - FULL * COLS
KM = 4
MCHUNKS = COLS // KM
NJ = N // P
KN = 3
NCHUNKS = NJ // KN
TAIL = N - P * NJ
BIG = 1.0e30
SKIP = 65536.0
EPS = 1e-05
SLOPE = 0.2


class Chain:

    def __init__(self, eng, sem):
        self.eng, self.sem, self.n = eng, sem, 0

    def link(self, ins):
        self.n += 1
        ins.then_inc(self.sem, 1)
        self.eng.wait_ge(self.sem, self.n)

    def mark(self, ins):
        self.n += 1
        ins.then_inc(self.sem, 1)

    def settle(self):
        self.eng.wait_ge(self.sem, self.n)

    def restart(self):
        self.eng.sem_inc(self.sem, 1)
        self.eng.wait_ge(self.sem, self.n + 1)
        self.eng.sem_clear(self.sem)
        self.n = 0


def run_bodies(eng, count, body):
    body(0, first=True, last=False)
    with eng.Fori(1, count - 1, 1) as i:
        body(i, first=False, last=False)
    body(count - 1, first=False, last=True)


def build(nc, t, out):
    ctx = ExitStack()
    with ctx:
        def sb(name, shape, dt=F32):
            return ctx.enter_context(nc.sbuf_tensor(name, shape, dt))

        def sem(name):
            return ctx.enter_context(nc.semaphore(name))

        def dram(name, shape):
            return nc.dram_tensor(name, shape, F32, kind="Internal").ap()

        gat_table = [dram(f"gat_table{l}", (N, D)) for l in range(3)]
        normed = dram("normed", (N, D))
        hidden = dram("hidden", (N, D))
        agg_table = dram("agg_table", (N, D))

        ident = sb("ident", [P, P])
        ones = sb("ones", [P, P])
        wlr = sb("wlr", [P, 3, 2 * D])
        att = sb("att", [P, 3, D])
        gat_bias = sb("gat_bias", [P, 3])
        b2_rows = sb("b2_rows", [P, D])
        ob_rows = sb("ob_rows", [P, D])
        w1t = sb("w1t", [P, D])
        wat = sb("wat", [P, D])
        wbt = sb("wbt", [P, MIX])
        w2t = sb("w2t", [P, 2, D])
        b1_col = sb("b1_col", [P, 1])

        edge_dst = sb("edge_dst", [P, COLS + 2])
        gather_idx = sb("gather_idx", [P, COLS + 2 * K], I32)
        scatter_idx = sb("scatter_idx", [P, COLS], I32)
        inherit = sb("inherit", [P, COLS], I32)
        cont = sb("cont", [P, COLS])
        pen = sb("pen", [P, COLS])
        mult = sb("mult", [P, COLS])
        head = sb("head", [P, COLS])
        count = sb("count", [P, COLS + 1])
        inv_count = sb("inv_count", [P, COLS])
        first_node = sb("first_node", [P, 1], I32)
        fix_idx = sb("fix_idx", [P, 1], I32)
        take = sb("take", [P, P])
        take_pen = sb("take_pen", [P, P])

        run_max = sb("run_max", [P, COLS + 1])
        run_sum = sb("run_sum", [P, COLS + 1])
        wide = sb("wide", [P, COLS])

        with ExitStack() as scope:
            edge_in = scope.enter_context(nc.sbuf_tensor("edge_in", [P, COLS + 2], I32))
            src_in = scope.enter_context(nc.sbuf_tensor("src_in", [P, COLS], I32))
            w_in = scope.enter_context(nc.sbuf_tensor("w_in", [P, 5 * D], F32))
            first_dst = scope.enter_context(nc.sbuf_tensor("first_dst", [P, 1], F32))
            diag = scope.enter_context(nc.sbuf_tensor("diag", [P, P], F32))
            tri = scope.enter_context(nc.sbuf_tensor("tri", [P, P], F32))
            small = scope.enter_context(nc.sbuf_tensor("small", [P, 4], F32))
            ps_w = scope.enter_context(nc.psum_tensor("ps_w", [P, 4 * D], F32))
            ps_w2 = scope.enter_context(nc.psum_tensor("ps_w2", [P, 4 * D], F32))
            ps_g = scope.enter_context(nc.psum_tensor("ps_g", [P, 4 * D], F32))
            padded = sem("padded")
            edges_in = sem("edges_in")
            weights_in = sem("weights_in")
            consts_made = sem("consts_made")
            weights_turned = sem("weights_turned")
            diag_made = sem("diag_made")
            nodes_spread = sem("nodes_spread")
            take_made = sem("take_made")
            take_turned = sem("take_turned")
            setup_chain = sem("setup_chain")

            with nc.Block() as block:
                @block.sync
                def _(sp):
                    sp.wait_ge(padded, 2)
                    dst, src = t["dst"], t["src"]
                    main = dst[0:FULL * COLS].rearrange("(p c) -> p c", c=COLS)
                    with nc.allow_non_contiguous_dma(reason="one word of each run"):
                        sp.dma_start(edge_in[0:FULL, 1:COLS + 1], main).then_inc(edges_in, 16)
                        sp.dma_start(edge_in[FULL:FULL + 1, 1:REST + 1],
                                     dst[FULL * COLS:E].rearrange("(p c) -> p c", p=1)).then_inc(edges_in, 16)
                        sp.dma_start(edge_in[1:FULL + 1, 0:1], main[:, COLS - 1:COLS]).then_inc(edges_in, 16)
                        sp.dma_start(edge_in[0:FULL - 1, COLS + 1:COLS + 2], main[1:FULL, 0:1]).then_inc(edges_in, 16)
                        sp.dma_start(edge_in[FULL - 1:FULL, COLS + 1:COLS + 2],
                                     dst[FULL * COLS:FULL * COLS + 1].rearrange("(p c) -> p c", p=1)).then_inc(edges_in, 16)
                        sp.dma_start(src_in[0:FULL, :],
                                     src[0:FULL * COLS].rearrange("(p c) -> p c", c=COLS)).then_inc(edges_in, 16)
                        sp.dma_start(src_in[FULL:FULL + 1, 0:REST],
                                     src[FULL * COLS:E].rearrange("(p c) -> p c", p=1)).then_inc(edges_in, 16)

                @block.scalar
                def _(act):
                    with nc.allow_non_contiguous_dma(reason="biases, a word for each partition"):
                        for l in range(3):
                            act.dma_start(wlr[:, l, 0:D], t[f"L0_gnn_Wl{l}"]).then_inc(weights_in, 16)
                            act.dma_start(wlr[:, l, D:2 * D], t[f"L0_gnn_Wr{l}"]).then_inc(weights_in, 16)
                            act.dma_start(att[:, l, :], t[f"L0_gnn_att{l}"].unsqueeze(0).broadcast_to([P, D])).then_inc(weights_in, 16)
                            act.dma_start(gat_bias[:, l:l + 1], t[f"L0_gnn_b{l}"].unsqueeze(1)).then_inc(weights_in, 16)
                        act.dma_start(b1_col[:, :], t["L1_gnn_b1"].unsqueeze(1)).then_inc(weights_in, 16)
                    act.dma_start(b2_rows[:, :], t["L0_gnn_b2"].unsqueeze(0).broadcast_to([P, D])).then_inc(weights_in, 16)
                    act.dma_start(ob_rows[:, :], t["L1_gnn_b2"].unsqueeze(0).broadcast_to([P, D])).then_inc(weights_in, 16)
                    act.dma_start(w_in[:, 0:D], t["L1_gnn_W1"]).then_inc(weights_in, 16)
                    act.dma_start(w_in[:, D:2 * D], t["L1_gnn_WA"]).then_inc(weights_in, 16)
                    act.dma_start(w_in[:, 2 * D:4 * D], t["L1_gnn_W2"]).then_inc(weights_in, 16)
                    act.dma_start(w_in[0:MIX, 4 * D:5 * D], t["L1_gnn_WB"]).then_inc(weights_in, 16)

                @block.gpsimd
                def _(pool):
                    pool.memset(ones[:, :], 1.0).then_inc(consts_made, 1)
                    pool.memset(ident[:, :], 0.0).then_inc(consts_made, 1)
                    pool.wait_ge(consts_made, 2)
                    pool.affine_select(out=ident[:, :], in_=ident[:, :], compare_op=ALU.not_equal, fill=1.0,
                                       base=0, pattern=[[-1, P]], channel_multiplier=1).then_inc(consts_made, 1)
                    pool.affine_select(out=tri[:, :], in_=ones[:, :], compare_op=ALU.is_gt, fill=0.0,
                                       base=0, pattern=[[-1, P]], channel_multiplier=1).then_inc(consts_made, 1)

                @block.tensor
                def _(pe):
                    pe.wait_ge(consts_made, 4)
                    pe.wait_ge(weights_in, 16 * 19)
                    for j in range(4):
                        pe.transpose(ps_w[:, j * D:(j + 1) * D], w_in[:, j * D:(j + 1) * D], ident[:, :]).then_inc(weights_turned, 1)
                    pe.transpose(ps_w2[:, 0:MIX], w_in[0:MIX, 4 * D:5 * D], ident[0:MIX, 0:MIX]).then_inc(weights_turned, 1)
                    pe.wait_ge(diag_made, 1)
                    pe.matmul(ps_g[:, 0:P], ones[:, :], diag[:, :], start=True, stop=True).then_inc(nodes_spread, 1)
                    pe.wait_ge(take_made, 1)
                    pe.transpose(ps_g[:, P:2 * P], take[:, :], ident[:, :]).then_inc(take_turned, 1)

                @block.vector
                def _(dve):
                    chain = Chain(dve, setup_chain)
                    dve.memset(edge_in[:, :], N).then_inc(padded, 1)
                    dve.memset(src_in[:, :], 0).then_inc(padded, 1)
                    dve.wait_ge(edges_in, 16 * 7)
                    chain.mark(dve.memset(gather_idx[:, COLS:COLS + 2 * K], 0))
                    chain.mark(dve.memset(count[:, 0:1], 0.0))
                    chain.mark(dve.tensor_copy(gather_idx[:, 0:COLS], src_in[:, ::-1]))
                    chain.link(dve.tensor_copy(edge_dst[:, :], edge_in[:, ::-1]))
                    here, before, after = edge_dst[:, 1:COLS + 1], edge_dst[:, 0:COLS], edge_dst[:, 2:COLS + 2]
                    chain.link(dve.tensor_tensor(cont[:, :], here, before, ALU.is_equal))
                    chain.mark(dve.tensor_copy(inherit[:, :], cont[:, :]))
                    chain.link(dve.tensor_scalar(mult[:, :], cont[:, :], -1.0, 2.0, ALU.mult, ALU.add))
                    chain.link(dve.memset(cont[:, 0:1], 0.0))
                    chain.link(dve.tensor_scalar(pen[:, :], cont[:, :], 1.0, BIG, ALU.subtract, ALU.mult))
                    chain.link(dve.tensor_tensor(wide[:, :], here, after, ALU.is_equal))
                    chain.link(dve.scalar_tensor_tensor(scatter_idx[:, :], wide[:, :], SKIP, here, ALU.mult, ALU.add))
                    chain.link(dve.tensor_copy(first_dst[:, :], edge_dst[:, 1:2]))
                    chain.link(dve.tensor_scalar(wide[:, :], wide[:, :], -1.0, 1.0, ALU.mult, ALU.add))
                    chain.link(dve.scalar_tensor_tensor(head[:, :], here, first_dst[:, 0:1], wide[:, :], ALU.is_equal, ALU.mult))
                    chain.link(dve.tensor_reduce(small[:, 0:1], head[:, :], AX.X, ALU.add))
                    chain.link(dve.tensor_scalar(small[:, 1:2], small[:, 0:1], -SKIP, SKIP, ALU.mult, ALU.add))
                    chain.mark(dve.tensor_tensor(fix_idx[:, :], first_dst[:, :], small[:, 1:2], ALU.add))
                    chain.mark(dve.tensor_scalar(first_node[:, :], first_dst[:, :], float(N - 1), None, ALU.min))
                    chain.link(dve.memset(wide[:, :], 1.0))
                    chain.link(dve.tensor_tensor_scan(count[:, 1:COLS + 1], cont[:, :], wide[:, :], 0.0, ALU.mult, ALU.add))
                    chain.mark(dve.reciprocal(inv_count[:, :], count[:, 1:COLS + 1]))
                    dve.wait_ge(consts_made, 4)
                    dve.tensor_scalar(diag[:, :], ident[:, :], first_dst[:, 0:1], None, ALU.mult).then_inc(diag_made, 1)
                    dve.wait_ge(nodes_spread, 1)
                    dve.scalar_tensor_tensor(take[:, :], ps_g[:, 0:P], edge_dst[:, COLS:COLS + 1], tri[:, :],
                                             ALU.is_equal, ALU.mult).then_inc(take_made, 1)
                    dve.wait_ge(take_turned, 1)
                    chain.mark(dve.tensor_scalar(take_pen[:, :], ps_g[:, P:2 * P], 1.0, BIG, ALU.subtract, ALU.mult))
                    dve.wait_ge(weights_turned, 5)
                    chain.mark(dve.tensor_copy(w1t[:, :], ps_w[:, 0:D]))
                    chain.mark(dve.tensor_copy(wat[:, :], ps_w[:, D:2 * D]))
                    chain.mark(dve.tensor_copy(w2t[:, :, :], ps_w[:, 2 * D:4 * D].rearrange("p (a b) -> p a b", a=2)))
                    chain.mark(dve.tensor_copy(wbt[:, :], ps_w2[:, 0:MIX]))
                    chain.settle()

        tables = [t["x"]] + gat_table
        signals = GatSignals(lambda name: sem(f"gat_{name}"))
        for l in range(3):
            with ExitStack() as scope:
                gat_layer(nc, scope, signals, l, tables[l], tables[l + 1], wlr[:, l, :], att[:, l, :],
                          gat_bias[:, l - 1:l] if l else None,
                          dict(ident=ident, ones=ones, gather_idx=gather_idx, scatter_idx=scatter_idx,
                               inherit=inherit, pen=pen, mult=mult, head=head, first_node=first_node,
                               fix_idx=fix_idx, take_pen=take_pen, run_max=run_max, run_sum=run_sum, wide=wide))

        with ExitStack() as scope:
            node_pass_hidden(nc, scope, t["x"], gat_table[2], normed, hidden,
                             dict(ident=ident, b2_rows=b2_rows, w1t=w1t, b1_col=b1_col))

        with ExitStack() as scope:
            mixing_pass(nc, scope, hidden, agg_table,
                        dict(ident=ident, gather_idx=gather_idx, scatter_idx=scatter_idx, cont=cont,
                             head=head, count=count, inv_count=inv_count,
                             fix_idx=fix_idx, take=take, wat=wat, wbt=wbt, wide=wide))

        with ExitStack() as scope:
            node_pass_out(nc, scope, agg_table, hidden, normed, out,
                          dict(ident=ident, ob_rows=ob_rows, w2t=w2t))


def gather(pool, dst, table, idx):
    return pool.indirect_dma_start(dst, None, table[:, :], bass.IndirectOffsetOnAxis(ap=idx, axis=0))


def scatter(pool, table, idx, rows):
    return pool.indirect_dma_start(table[:, :], bass.IndirectOffsetOnAxis(ap=idx, axis=0), rows, None,
                                   bounds_check=N - 1, oob_is_err=False)


class GatSignals:

    def __init__(self, sem):
        self.seed_gathered = sem("seed_gathered")
        self.seed_turned = sem("seed_turned")
        self.seed_evacuated = sem("seed_evacuated")
        self.seed_projected = sem("seed_projected")
        self.idx_staged = sem("idx_staged")
        self.gathered = [sem(f"gathered{s}") for s in range(2)]
        self.turned = sem("turned")
        self.evacuated = sem("evacuated")
        self.projected = sem("projected")
        self.xlr_ready = sem("xlr_ready")
        self.summed = sem("summed")
        self.drop_ready = sem("drop_ready")
        self.grown_ready = sem("grown_ready")
        self.share_ready = sem("share_ready")
        self.part_ready = sem("part_ready")
        self.outs_ready = sem("outs_ready")
        self.scattered = [sem(f"scattered{s}") for s in range(2)]
        self.chain = sem("chain")
        self.pool_passed = sem("pool_passed")
        self.dve_passed = sem("dve_passed")
        self.fix_gathered = sem("fix_gathered")
        self.fix_scattered = sem("fix_scattered")
        self.fix_dve = sem("fix_dve")
        self.fix_pe = sem("fix_pe")
        self.fix_act = sem("fix_act")


def gat_layer(nc, scope, sg, l, table_in, table_out, w, att_rows, bias, c):
    def sb(name, shape, dt=F32):
        return scope.enter_context(nc.sbuf_tensor(f"g{l}_{name}", shape, dt))

    def ps(name):
        return scope.enter_context(nc.psum_tensor(f"g{l}_{name}", [P, 512], F32))

    rows = [sb(f"rows{s}", [P, K, D]) for s in range(2)]
    rows_t = [sb(f"rows_t{h}", [P, 4 * P]) for h in range(2)]
    xlr = [sb(f"xlr{s}", [P, K, 2 * D]) for s in range(2)]
    xr_kept = sb("xr_kept", [P, D])
    mixed = sb("mixed", [P, K, D])
    score = sb("score", [P, K])
    drop = sb("drop", [P, 2 * K])
    grown = sb("grown", [P, 2 * K])
    inv_sum = sb("inv_sum", [P, K])
    old_share = sb("old_share", [P, K])
    new_share = sb("new_share", [P, K])
    tmp = sb("tmp", [P, K])
    part = sb("part", [P, K, D])
    outs = [sb(f"outs{s}", [P, K, D]) for s in range(2)]
    gidx = [sb(f"gidx{s}", [P, K], I32) for s in range(2)]
    sidx = [sb(f"sidx{s}", [P, K], I32) for s in range(2)]
    mask = sb("mask", [P, K], I32)
    ps_t = [ps(f"ps_t{h}") for h in range(2)]
    ps_x = [ps(f"ps_x{j}") for j in range(4)]
    ps_b = [ps(f"ps_b{j}") for j in range(2)]
    diag = sb("diag", [P, 2 * P])
    share = sb("share", [P, P + 1])
    share_t = sb("share_t", [P, P])
    fixed = sb("fixed", [P, D])
    st = sb("st", [P, 8])

    def activate(act, dst, src):
        if bias is None:
            return act.activation(dst, src, ACT.Copy)
        return act.activation(dst, src, ACT.Relu, bias=bias)

    BODIES = CHUNKS // 2
    DONE, TURNS = l * CHUNKS, l * BODIES

    with nc.Block() as block:
        @block.gpsimd
        def _(pool):
            gather(pool, rows[1][:, 0, :], table_in, c["first_node"][:, 0:1]).then_inc(sg.seed_gathered, 16)

            def gather_chunk(s):
                for k in range(K):
                    gather(pool, rows[s][:, k, :], table_in, gidx[s][:, k:k + 1]).then_inc(sg.gathered[s], 16)

            def scatter_chunk(s):
                for k in range(K):
                    scatter(pool, table_out, sidx[s][:, k:k + 1], outs[s][:, k, :]).then_inc(sg.scattered[s], 16)

            pool.wait_ge(sg.idx_staged, DONE + 1)
            gather_chunk(0)
            pool.wait_ge(sg.seed_turned, l + 1)
            pool.wait_ge(sg.idx_staged, DONE + 2)
            gather_chunk(1)

            def body(i, first, last):
                for s in range(2):
                    n = i * 2 + s
                    at = n + DONE
                    if not last:
                        pool.wait_ge(sg.turned, (at + 1) * 2)
                        pool.wait_ge(sg.idx_staged, at + 3)
                        pool.sem_inc(sg.pool_passed, 1)
                        gather_chunk(s)
                    pool.wait_ge(sg.outs_ready, at + 1)
                    pool.sem_inc(sg.pool_passed, 1)
                    scatter_chunk(s)
            run_bodies(pool, BODIES, body)
            for s in range(2):
                pool.wait_ge(sg.scattered[s], 16 * K * (TURNS + BODIES))

        @block.tensor
        def _(pe):
            pe.wait_ge(sg.seed_gathered, 16 * (l + 1))
            pe.transpose(ps_b[0][:, 0:P], rows[1][:, 0, :], c["ident"][:, :]).then_inc(sg.seed_turned, 1)
            pe.wait_ge(sg.seed_evacuated, l + 1)
            pe.matmul(ps_b[0][:, P:2 * P], rows_t[0][:, 0:P], w[:, D:2 * D], start=True, stop=True).then_inc(sg.seed_projected, 1)

            def body(i, first, last):
                for s in range(2):
                    n = i * 2 + s
                    at = n + DONE
                    pe.wait_ge(sg.gathered[s], (i + (TURNS + 1)) * (16 * K))
                    for h in range(2):
                        if not (first and s == 0):
                            pe.wait_ge(sg.evacuated, at * 2 - 1 + h)
                        for k in range(4):
                            ins = pe.transpose(ps_t[h][:, k * P:(k + 1) * P], rows[s][:, 4 * h + k, :], c["ident"][:, :])
                        ins.then_inc(sg.turned, 1)
                    for j in range(4):
                        if j % 2 == 0:
                            pe.wait_ge(sg.evacuated, at * 2 + 1 + j // 2)
                        if not (first and s == 0):
                            pe.wait_ge(sg.xlr_ready, at * 4 - 3 + j)
                        for k in range(2):
                            kk = (2 * j + k) % 4
                            ins = pe.matmul(ps_x[j][:, k * 2 * D:(k + 1) * 2 * D],
                                            rows_t[j // 2][:, kk * P:(kk + 1) * P], w, start=True, stop=True)
                        ins.then_inc(sg.projected, 1)
            run_bodies(pe, BODIES, body)

        @block.scalar
        def _(act):
            act.wait_ge(sg.seed_turned, l + 1)
            activate(act, rows_t[0][:, 0:P], ps_b[0][:, 0:P]).then_inc(sg.seed_evacuated, 1)

            def evacuate(n, s, full):
                for h in range(2):
                    act.wait_ge(sg.turned, (n + DONE) * 2 + 1 + h)
                    if full:
                        act.wait_ge(sg.projected, (n + DONE) * 4 - 2 + 2 * h)
                    elif h == 0:
                        act.wait_ge(sg.seed_projected, l + 1)
                    activate(act, rows_t[h][:, :], ps_t[h][:, :]).then_inc(sg.evacuated, 1)
                for j in range(4):
                    act.wait_ge(sg.projected, (n + DONE) * 4 + 1 + j)
                    act.activation(xlr[s][:, 2 * j:2 * j + 2, :], ps_x[j][:, :].rearrange("p (a b) -> p a b", a=2),
                                   ACT.Copy).then_inc(sg.xlr_ready, 1)

            evacuate(0, 0, False)

            def body(i, first, last):
                for s in range(2):
                    n = i * 2 + s
                    at = n + DONE
                    if not (last and s == 1):
                        if not (first and s == 0):
                            act.wait_ge(sg.summed, at)
                            act.wait_ge(sg.part_ready, at * K)
                        evacuate(n + 1, 1 - s, True)
                    act.wait_ge(sg.drop_ready, at + 1)
                    act.activation(grown[:, :], drop[:, :], ACT.Exp).then_inc(sg.grown_ready, 1)
                    for k in range(K):
                        act.wait_ge(sg.share_ready, at + 1)
                        act.activation(part[:, k, :], xlr[s][:, k, 0:D], ACT.Copy,
                                       scale=new_share[:, k:k + 1]).then_inc(sg.part_ready, 1)
            run_bodies(act, BODIES, body)

        @block.vector
        def _(dve):
            chain = Chain(dve, sg.chain)
            chain.mark(dve.memset(c["run_max"][:, 0:1], -BIG))
            chain.mark(dve.memset(c["run_sum"][:, 0:1], 0.0))
            chain.mark(dve.memset(outs[1][:, K - 1, :], 0.0))
            dve.tensor_copy(gidx[0][:, :], c["gather_idx"][:, 0:K]).then_inc(sg.idx_staged, 1)
            dve.tensor_copy(gidx[1][:, :], c["gather_idx"][:, K:2 * K]).then_inc(sg.idx_staged, 1)
            dve.wait_ge(sg.seed_projected, l + 1)
            chain.mark(dve.tensor_copy(xr_kept[:, :], ps_b[0][:, P:2 * P]))
            chain.settle()
            chain.restart()

            def body(i, first, last):
                for s in range(2):
                    n = i * 2 + s
                    at = n + DONE
                    c0 = n * K
                    now = bass.ds(c0, K)
                    new = bass.ds(c0 + 1, K)
                    run_max, run_sum = c["run_max"], c["run_sum"]
                    if not last:
                        dve.wait_ge(sg.gathered[s], (i + (TURNS + 1)) * (16 * K))
                        dve.tensor_scalar(gidx[s][:, :], c["gather_idx"][:, bass.ds(c0 + 2 * K, K)], 0.0, None,
                                          ALU.add).then_inc(sg.idx_staged, 1)
                    chain.link(dve.tensor_copy(mask[:, :], c["inherit"][:, now]))
                    dve.wait_ge(sg.xlr_ready, (at + 1) * 4)
                    dve.sem_inc(sg.dve_passed, 1)
                    for k in range(K):
                        prev = xr_kept[:, :] if k == 0 else xlr[s][:, k - 1, D:2 * D]
                        chain.link(dve.copy_predicated(xlr[s][:, k, D:2 * D],
                                                       mask[:, k:k + 1].broadcast_to([P, D]), prev))
                    chain.link(dve.tensor_copy(xr_kept[:, :], xlr[s][:, K - 1, D:2 * D]))
                    dve.tensor_tensor(mixed[:, :, :], xlr[s][:, :, 0:D], xlr[s][:, :, D:2 * D], ALU.add).then_inc(sg.summed, 1)
                    dve.wait_ge(sg.summed, at + 1)
                    chain.link(dve.scalar_tensor_tensor(mixed[:, :, :], mixed[:, :, :], SLOPE, mixed[:, :, :], ALU.mult, ALU.max))
                    chain.link(dve.tensor_tensor(mixed[:, :, :], mixed[:, :, :],
                                                 att_rows.unsqueeze(1).broadcast_to([P, K, D]), ALU.mult))
                    chain.link(dve.tensor_reduce(score[:, :], mixed[:, :, :], AX.X, ALU.add))
                    chain.link(dve.tensor_tensor_scan(run_max[:, new], c["pen"][:, now], score[:, :],
                                                      run_max[:, bass.ds(c0, 1)], ALU.add, ALU.max))
                    chain.mark(dve.tensor_tensor(drop[:, K:2 * K], score[:, :], run_max[:, new], ALU.subtract))
                    chain.link(dve.tensor_tensor(tmp[:, :], run_max[:, now], c["pen"][:, now], ALU.add))
                    dve.tensor_tensor(drop[:, 0:K], tmp[:, :], run_max[:, new], ALU.subtract).then_inc(sg.drop_ready, 1)
                    dve.wait_ge(sg.grown_ready, at + 1)
                    chain.link(dve.tensor_tensor(grown[:, K:2 * K], grown[:, K:2 * K], c["mult"][:, now], ALU.mult))
                    chain.link(dve.tensor_tensor_scan(run_sum[:, new], grown[:, 0:K], grown[:, K:2 * K],
                                                      run_sum[:, bass.ds(c0, 1)], ALU.mult, ALU.add))
                    chain.mark(dve.reciprocal(inv_sum[:, :], run_sum[:, new]))
                    chain.link(dve.tensor_tensor(tmp[:, :], grown[:, 0:K], run_sum[:, now], ALU.mult))
                    chain.link(dve.tensor_tensor(old_share[:, :], tmp[:, :], inv_sum[:, :], ALU.mult))
                    dve.tensor_tensor(new_share[:, :], grown[:, K:2 * K], inv_sum[:, :], ALU.mult).then_inc(sg.share_ready, 1)
                    if not first:
                        dve.wait_ge(sg.scattered[s], (i + TURNS) * (16 * K))
                    chain.link(dve.tensor_scalar(sidx[s][:, :], c["scatter_idx"][:, now], 0.0, None, ALU.add))
                    for k in range(K):
                        prev = outs[1 - s][:, K - 1, :] if k == 0 else outs[s][:, k - 1, :]
                        dve.wait_ge(sg.part_ready, at * K + (k + 1))
                        ins = dve.scalar_tensor_tensor(outs[s][:, k, :], prev, old_share[:, k:k + 1], part[:, k, :],
                                                       ALU.mult, ALU.add)
                        if k < K - 1:
                            chain.link(ins)
                        else:
                            ins.then_inc(sg.outs_ready, 1)
                    dve.wait_ge(sg.outs_ready, at + 1)
                chain.restart()
            run_bodies(dve, BODIES, body)

    with nc.Block() as block:
        @block.gpsimd
        def _(pool):
            gather(pool, fixed[:, :], table_out, c["first_node"][:, 0:1]).then_inc(sg.fix_gathered, 16)
            pool.wait_ge(sg.fix_dve, 5 * l + 5)
            pool.wait_ge(sg.fix_gathered, 16 * (l + 1))
            scatter(pool, table_out, c["fix_idx"][:, 0:1], fixed[:, :]).then_inc(sg.fix_scattered, 16)
            pool.wait_ge(sg.fix_scattered, 16 * (l + 1))

        @block.vector
        def _(dve):
            chain = Chain(dve, sg.chain)
            own_max, own_sum, top, own_share, total, inv = (st[:, j:j + 1] for j in range(6))
            last_max, last_sum = c["run_max"][:, COLS:COLS + 1], c["run_sum"][:, COLS:COLS + 1]
            chain.mark(dve.tensor_scalar(diag[:, 0:P], c["ident"][:, :], last_max, None, ALU.mult))
            chain.settle()
            dve.tensor_scalar(diag[:, P:2 * P], c["ident"][:, :], last_sum, None, ALU.mult).then_inc(sg.fix_dve, 1)
            chain.link(dve.tensor_tensor(c["wide"][:, :], c["run_max"][:, 1:COLS + 1], c["head"][:, :], ALU.mult))
            chain.link(dve.tensor_reduce(own_max, c["wide"][:, :], AX.X, ALU.add))
            chain.link(dve.tensor_tensor(c["wide"][:, :], c["run_sum"][:, 1:COLS + 1], c["head"][:, :], ALU.mult))
            chain.link(dve.tensor_reduce(own_sum, c["wide"][:, :], AX.X, ALU.add))
            dve.wait_ge(sg.fix_pe, 3 * l + 1)
            chain.link(dve.tensor_tensor(share[:, 0:P], ps_b[1][:, 0:P], c["take_pen"][:, :], ALU.add))
            chain.link(dve.tensor_reduce(top, share[:, 0:P], AX.X, ALU.max))
            chain.link(dve.tensor_tensor(top, top, own_max, ALU.max))
            chain.mark(dve.tensor_tensor(share[:, P:P + 1], own_max, top, ALU.subtract))
            chain.settle()
            dve.tensor_scalar(share[:, 0:P], share[:, 0:P], top, None, ALU.subtract).then_inc(sg.fix_dve, 1)
            dve.wait_ge(sg.fix_act, l + 1)
            chain.mark(dve.tensor_tensor(share[:, 0:P], share[:, 0:P], ps_b[1][:, P:2 * P], ALU.mult))
            chain.link(dve.tensor_tensor(own_share, share[:, P:P + 1], own_sum, ALU.mult))
            chain.link(dve.tensor_reduce(total, share[:, 0:P], AX.X, ALU.add))
            chain.link(dve.tensor_tensor(total, total, own_share, ALU.add))
            chain.link(dve.tensor_scalar(total, total, 1.0 / BIG, None, ALU.max))
            chain.link(dve.reciprocal(inv, total))
            chain.link(dve.tensor_tensor(own_share, own_share, inv, ALU.mult))
            dve.tensor_scalar(share[:, 0:P], share[:, 0:P], inv, None, ALU.mult).then_inc(sg.fix_dve, 1)
            dve.wait_ge(sg.fix_pe, 3 * l + 2)
            dve.tensor_copy(share_t[:, :], ps_b[0][:, 0:P]).then_inc(sg.fix_dve, 1)
            dve.wait_ge(sg.fix_pe, 3 * l + 3)
            dve.wait_ge(sg.fix_gathered, 16 * (l + 1))
            dve.scalar_tensor_tensor(fixed[:, :], fixed[:, :], own_share, ps_b[1][:, 2 * P:3 * P],
                                     ALU.mult, ALU.add).then_inc(sg.fix_dve, 1)
            chain.restart()

        @block.scalar
        def _(act):
            act.wait_ge(sg.fix_dve, 5 * l + 2)
            act.activation(share[:, :], share[:, :], ACT.Exp).then_inc(sg.fix_act, 1)

        @block.tensor
        def _(pe):
            pe.wait_ge(sg.fix_dve, 5 * l + 1)
            pe.matmul(ps_b[1][:, 0:2 * P], c["ones"][:, :], diag[:, :], start=True, stop=True).then_inc(sg.fix_pe, 1)
            pe.wait_ge(sg.fix_dve, 5 * l + 3)
            pe.transpose(ps_b[0][:, 0:P], share[:, 0:P], c["ident"][:, :]).then_inc(sg.fix_pe, 1)
            pe.wait_ge(sg.fix_dve, 5 * l + 4)
            pe.matmul(ps_b[1][:, 2 * P:3 * P], share_t[:, :], outs[1][:, K - 1, :], start=True, stop=True).then_inc(sg.fix_pe, 1)


class Step:

    def __init__(self, i, u, unroll, total):
        self.i, self.u, self.unroll, self.total = i, u, unroll, total

    def chunk(self, lag):
        return self.i * self.unroll + (self.u - lag)

    def slot(self, lag, ring):
        return (self.u - lag) % ring

    def turn(self, lag, ring):
        return self.i * (self.unroll // ring) + (self.u - lag) // ring

    def live(self, lag):
        n = self.chunk(lag)
        return not isinstance(n, int) or 0 <= n < self.total


def pipeline(eng, total, unroll, lags, ring, step, after=None):
    first = -(-(lags + ring) // unroll)
    last = total // unroll
    for v in range(first * unroll):
        step(Step(v // unroll, v % unroll, unroll, total))
        if after:
            after()
    with eng.Fori(first, last, 1) as i:
        for u in range(unroll):
            step(Step(i, u, unroll, total))
        if after:
            after()
    for v in range(last * unroll, total + lags):
        step(Step(v // unroll, v % unroll, unroll, total))
        if after:
            after()


def wait(eng, sem, value):
    if not isinstance(value, int) or value > 0:
        eng.wait_ge(sem, value)


def is_tail(n):
    return isinstance(n, int) and n == NCHUNKS


def node_cols(n):
    return 1 if is_tail(n) else KN


def node_rows(table, n, store=False):
    if is_tail(n):
        lo = N - TAIL if store else N - P
        return table[lo:N, :].rearrange("(p j) d -> p j d", j=1)
    return table[0:P * NJ, :].rearrange("(p j) d -> p j d", p=P)[:, bass.ds(n * KN, KN), :]


def store_lo(n):
    return P - TAIL if is_tail(n) else 0


class RowNorm:

    def __init__(self, sb, sem, rows, ring):
        self.rows, self.ring = rows, ring
        self.neg_mean = [sb(f"neg_mean{r}", [P, KN]) for r in range(ring)]
        self.sq_sum = [sb(f"sq_sum{r}", [P, KN]) for r in range(ring)]
        self.var = [sb(f"var{r}", [P, KN]) for r in range(ring)]
        self.rstd = [sb(f"rstd{r}", [P, KN]) for r in range(ring)]
        self.sq = sb("sq", [P, ring, KN, D])
        self.half = sb("half", [P, KN])
        self.mean_ready = sem("mean_ready")
        self.sq_ready = sem("sq_ready")
        self.var_ready = sem("var_ready")
        self.rstd_ready = sem("rstd_ready")
        self.y_ready = sem("y_ready")

    def sums(self, dve, chain, v):
        n, r, k = v.chunk(0), v.slot(0, self.ring), node_cols(v.chunk(0))
        chain.link(dve.tensor_reduce(self.neg_mean[r][:, 0:k], self.rows[r][:, 0:k, :], AX.X, ALU.add))
        dve.tensor_scalar(self.neg_mean[r][:, 0:k], self.neg_mean[r][:, 0:k], -1.0 / D, None,
                          ALU.mult).then_inc(self.mean_ready, 1)

    def squares(self, act, v, lag=0):
        n, r, k = v.chunk(lag), v.slot(lag, self.ring), node_cols(v.chunk(lag))
        act.wait_ge(self.mean_ready, n + 1)
        wait(act, self.sq_ready, n - self.ring + 1)
        for j in range(k):
            ins = act.activation(self.sq[:, r, j, :], self.rows[r][:, j, :], ACT.Square,
                                 bias=self.neg_mean[r][:, j:j + 1], accum_out=self.sq_sum[r][:, j:j + 1])
        ins.then_inc(self.sq_ready, 1)

    def variances(self, dve, v):
        n, r, k = v.chunk(1), v.slot(1, self.ring), node_cols(v.chunk(1))
        dve.wait_ge(self.sq_ready, n + 1)
        dve.tensor_scalar(self.var[r][:, 0:k], self.sq_sum[r][:, 0:k], 1.0 / D, EPS,
                          ALU.mult, ALU.add).then_inc(self.var_ready, 1)

    def rstds(self, pool, v):
        n, r, k = v.chunk(1), v.slot(1, self.ring), node_cols(v.chunk(1))
        pool.wait_ge(self.var_ready, n + 1)
        pool.tensor_tensor(self.rstd[r][:, 0:k], self.var[r][:, 0:k], self.half[:, 0:k],
                           ALU.pow).then_inc(self.rstd_ready, 1)

    def normalise(self, dve, chain, v):
        n, r, k = v.chunk(2), v.slot(2, self.ring), node_cols(v.chunk(2))
        dve.wait_ge(self.rstd_ready, n + 1)
        for j in range(k):
            ins = dve.tensor_scalar(self.rows[r][:, j, :], self.rows[r][:, j, :], self.neg_mean[r][:, j:j + 1],
                                    self.rstd[r][:, j:j + 1], ALU.add, ALU.mult)
            if j < k - 1:
                chain.mark(ins)
        chain.settle()
        ins.then_inc(self.y_ready, 1)


def node_pass_hidden(nc, scope, x, gat_out, normed, hidden, c):
    def sb(name, shape, dt=F32):
        return scope.enter_context(nc.sbuf_tensor(f"nh_{name}", shape, dt))

    def ps(name):
        return scope.enter_context(nc.psum_tensor(f"nh_{name}", [P, 512], F32))

    def sem(name):
        return scope.enter_context(nc.semaphore(f"nh_{name}"))

    R = 8
    L = R
    total = NCHUNKS + 1
    x_in = [sb(f"x_in{r}", [P, KN, D]) for r in range(L)]
    g_in = [sb(f"g_in{r}", [P, KN, D]) for r in range(L)]
    y = [sb(f"y{r}", [P, KN, D]) for r in range(R)]
    h = [sb(f"h{r}", [P, KN, D]) for r in range(R)]
    y_t = [sb(f"y_t{s}", [P, KN * P]) for s in range(2)]
    h_t = [sb(f"h_t{s}", [P, KN * P]) for s in range(2)]
    ps_y, ps_h, ps_b = ([ps(f"{name}{s}") for s in range(2)] for name in ("ps_y", "ps_h", "ps_b"))

    norm = RowNorm(sb, sem, y, R)
    loaded = [sem(f"loaded{r}") for r in range(L)]
    biased = sem("biased")
    added = sem("added")
    turned = sem("turned")
    y_t_ready = sem("y_t_ready")
    projected = sem("projected")
    h_t_ready = sem("h_t_ready")
    back = sem("back")
    h_ready = sem("h_ready")
    stored_y = [sem(f"stored_y{r}") for r in range(R)]
    stored_h = [sem(f"stored_h{r}") for r in range(R)]
    chain_sem = sem("chain")

    with nc.Block() as block:
        @block.sync
        def _(sp):
            def step(v):
                if v.live(0):
                    n, r, k = v.chunk(0), v.slot(0, L), node_cols(v.chunk(0))
                    wait(sp, added, n - L + 1)
                    sp.dma_start(x_in[r][:, 0:k, :], node_rows(x, n)).then_inc(loaded[r], 16)
                    sp.dma_start(g_in[r][:, 0:k, :], node_rows(gat_out, n)).then_inc(loaded[r], 16)
                if v.live(8):
                    n, r, k = v.chunk(8), v.slot(8, R), node_cols(v.chunk(8))
                    sp.wait_ge(norm.y_ready, n + 1)
                    sp.dma_start(node_rows(normed, n, True), y[r][store_lo(n):P, 0:k, :]).then_inc(stored_y[r], 16)
                if v.live(9):
                    n, r, k = v.chunk(9), v.slot(9, R), node_cols(v.chunk(9))
                    sp.wait_ge(h_ready, n + 1)
                    sp.dma_start(node_rows(hidden, n, True), h[r][store_lo(n):P, 0:k, :]).then_inc(stored_h[r], 16)
            pipeline(sp, total, L, 9, L, step)
            for r in range(R):
                turns = len(range(r, total, R))
                sp.wait_ge(stored_y[r], 16 * turns)
                sp.wait_ge(stored_h[r], 16 * turns)

        @block.gpsimd
        def _(pool):
            pool.memset(norm.half[:, :], -0.5).then_inc(biased, 1)
            pool.wait_ge(biased, 1)

            def step(v):
                if v.live(0):
                    n, r, k = v.chunk(0), v.slot(0, L), node_cols(v.chunk(0))
                    pool.wait_ge(loaded[r], (v.turn(0, L) + 1) * 32)
                    pool.tensor_tensor(g_in[r][:, 0:k, :], g_in[r][:, 0:k, :],
                                       c["b2_rows"][:, :].unsqueeze(1).broadcast_to([P, k, D]),
                                       ALU.add).then_inc(biased, 1)
                if v.live(1):
                    norm.rstds(pool, v)
            pipeline(pool, total, L, 1, L, step)

        @block.vector
        def _(dve):
            chain = Chain(dve, chain_sem)

            def step(v):
                if v.live(0):
                    n, r, q, k = v.chunk(0), v.slot(0, R), v.slot(0, L), node_cols(v.chunk(0))
                    dve.wait_ge(biased, n + 2)
                    wait(dve, stored_y[r], v.turn(0, R) * 16)
                    wait(dve, turned, n - R + 1)
                    dve.tensor_tensor(y[r][:, 0:k, :], x_in[q][:, 0:k, :], g_in[q][:, 0:k, :], ALU.add).then_inc(added, 1)
                    dve.wait_ge(added, n + 1)
                    norm.sums(dve, chain, v)
                if v.live(1):
                    norm.variances(dve, v)
                if v.live(2):
                    norm.normalise(dve, chain, v)
            pipeline(dve, total, L, 2, L, step, chain.restart)

        @block.tensor
        def _(pe):
            def step(v):
                if v.live(3):
                    n, r, s, k = v.chunk(3), v.slot(3, R), v.slot(3, 2), node_cols(v.chunk(3))
                    pe.wait_ge(norm.y_ready, n + 1)
                    wait(pe, y_t_ready, n - 1)
                    for j in range(k):
                        ins = pe.transpose(ps_y[s][:, j * P:(j + 1) * P], y[r][:, j, :], c["ident"][:, :])
                    ins.then_inc(turned, 1)
                if v.live(4):
                    n, s, k = v.chunk(4), v.slot(4, 2), node_cols(v.chunk(4))
                    pe.wait_ge(y_t_ready, n + 1)
                    wait(pe, h_t_ready, n - 1)
                    pe.matmul(ps_h[s][:, 0:k * P], c["w1t"][:, :], y_t[s][:, 0:k * P], start=True, stop=True).then_inc(projected, 1)
                if v.live(5):
                    n, s, k = v.chunk(5), v.slot(5, 2), node_cols(v.chunk(5))
                    pe.wait_ge(h_t_ready, n + 1)
                    wait(pe, h_ready, n - 1)
                    for j in range(k):
                        ins = pe.transpose(ps_b[s][:, j * P:(j + 1) * P], h_t[s][:, j * P:(j + 1) * P], c["ident"][:, :])
                    ins.then_inc(back, 1)
            pipeline(pe, total, L, 5, L, step)

        @block.scalar
        def _(act):
            def step(v):
                if v.live(0):
                    norm.squares(act, v)
                if v.live(3):
                    n, s, k = v.chunk(3), v.slot(3, 2), node_cols(v.chunk(3))
                    act.wait_ge(turned, n + 1)
                    wait(act, projected, n - 1)
                    act.activation(y_t[s][:, 0:k * P], ps_y[s][:, 0:k * P], ACT.Copy).then_inc(y_t_ready, 1)
                if v.live(4):
                    n, s, k = v.chunk(4), v.slot(4, 2), node_cols(v.chunk(4))
                    act.wait_ge(projected, n + 1)
                    wait(act, back, n - 1)
                    act.activation(h_t[s][:, 0:k * P], ps_h[s][:, 0:k * P], ACT.Gelu, bias=c["b1_col"][:, 0:1]).then_inc(h_t_ready, 1)
                if v.live(5):
                    n, r, s, k = v.chunk(5), v.slot(5, R), v.slot(5, 2), node_cols(v.chunk(5))
                    act.wait_ge(back, n + 1)
                    wait(act, stored_h[r], v.turn(5, R) * 16)
                    act.activation(h[r][:, 0:k, :], ps_b[s][:, 0:k * P].rearrange("p (a b) -> p a b", a=k),
                                   ACT.Copy).then_inc(h_ready, 1)
            pipeline(act, total, L, 5, L, step)


def mixing_pass(nc, scope, hidden, agg_table, c):
    def sb(name, shape, dt=F32):
        return scope.enter_context(nc.sbuf_tensor(f"mx_{name}", shape, dt))

    def ps(name):
        return scope.enter_context(nc.psum_tensor(f"mx_{name}", [P, 512], F32))

    def sem(name):
        return scope.enter_context(nc.semaphore(f"mx_{name}"))

    R = 4
    K = KM
    MD = MIX * D
    LATE = 5
    rows = [sb(f"rows{r}", [P, K, D]) for r in range(R)]
    gidx = [sb(f"gidx{r}", [P, K], I32) for r in range(R)]
    sidx = [sb(f"sidx{r}", [P, K], I32) for r in range(R)]
    rows_t = [sb(f"rows_t{s}", [P, K * P]) for s in range(2)]
    up_t = [sb(f"up_t{s}", [P, K * P]) for s in range(2)]
    mix = [sb(f"mix{s}", [P, K, MIX]) for s in range(2)]
    prod = [sb(f"prod{s}", [P, K, MD]) for s in range(2)]
    agg = [sb(f"agg{s}", [P, K, MD]) for s in range(2)]
    act_agg = [sb(f"act_agg{s}", [P, K, MD]) for s in range(2)]
    head_diag = [sb(f"head_diag{s}", [P, K, P]) for s in range(2)]
    mix_sum = sb("mix_sum", [P, MIX, COLS + 1])
    mix_mean = [sb(f"mix_mean{s}", [P, K, MIX]) for s in range(2)]
    outs = [sb(f"outs{r}", [P, K, D]) for r in range(R)]
    states = sb("states", [P, MIX + 1])
    own_small = sb("own_small", [P, MIX + 1])
    total = sb("total", [P, MD])
    fixed = sb("fixed", [P, D])
    ps_t = [ps(f"ps_t{s}") for s in range(2)]
    ps_u = [ps(f"ps_u{s}") for s in range(2)]
    ps_m = [ps(f"ps_m{s}") for s in range(2)]
    ps_own = ps("ps_own")
    ps_b = ps("ps_b")

    idx_staged = sem("idx_staged")
    gathered = [sem(f"gathered{r}") for r in range(R)]
    turned = sem("turned")
    rows_t_ready = sem("rows_t_ready")
    up_done = sem("up_done")
    up_ready = sem("up_ready")
    mix_done = sem("mix_done")
    mix_ready = sem("mix_ready")
    prod_ready = sem("prod_ready")
    agg_ready = sem("agg_ready")
    diag_ready = sem("diag_ready")
    own_added = sem("own_added")
    gelu_ready = sem("gelu_ready")
    mixed = sem("mixed")
    outs_ready = sem("outs_ready")
    scattered = [sem(f"scattered{r}") for r in range(R)]
    chain_sem = sem("chain")
    pool_passed = sem("pool_passed")
    fix_pe, fix_act, fix_dve, fix_scattered = sem("fix_pe"), sem("fix_act"), sem("fix_dve"), sem("fix_scattered")

    def heads(ap):
        return ap.rearrange("p (m d) -> p m d", m=MIX)

    with nc.Block() as block:
        @block.gpsimd
        def _(pool):
            def step(v):
                if v.live(0):
                    n, r = v.chunk(0), v.slot(0, R)
                    wait(pool, prod_ready, (n - (R - 1)) * K)
                    pool.wait_ge(idx_staged, n + 1)
                    pool.sem_inc(pool_passed, 1)
                    for k in range(K):
                        gather(pool, rows[r][:, k, :], hidden, gidx[r][:, k:k + 1]).then_inc(gathered[r], 16)
                if v.live(LATE):
                    n, r = v.chunk(LATE), v.slot(LATE, R)
                    pool.wait_ge(outs_ready, n + 1)
                    pool.sem_inc(pool_passed, 1)
                    for k in range(K):
                        scatter(pool, agg_table, sidx[r][:, k:k + 1], outs[r][:, k, :]).then_inc(scattered[r], 16)
            pipeline(pool, MCHUNKS, R, LATE, R, step)
            for r in range(R):
                pool.wait_ge(scattered[r], 16 * K * MCHUNKS // R)

        @block.tensor
        def _(pe):
            def step(v):
                if v.live(0):
                    n, r, s = v.chunk(0), v.slot(0, R), v.slot(0, 2)
                    pe.wait_ge(gathered[r], (v.turn(0, R) + 1) * (16 * K))
                    wait(pe, rows_t_ready, n - 1)
                    for k in range(K):
                        ins = pe.transpose(ps_t[s][:, k * P:(k + 1) * P], rows[r][:, k, :], c["ident"][:, :])
                    ins.then_inc(turned, 1)
                if v.live(1):
                    n, s = v.chunk(1), v.slot(1, 2)
                    pe.wait_ge(rows_t_ready, n + 1)
                    wait(pe, up_ready, n - 1)
                    pe.matmul(ps_u[s][:, :], c["wat"][:, :], rows_t[s][:, :], start=True, stop=True).then_inc(up_done, 1)
                if v.live(2):
                    n, s = v.chunk(2), v.slot(2, 2)
                    pe.wait_ge(up_ready, n + 1)
                    wait(pe, mix_ready, n - 1)
                    for k in range(K):
                        ins = pe.matmul(ps_m[s][:, k * MIX:(k + 1) * MIX], up_t[s][:, k * P:(k + 1) * P],
                                        c["wbt"][:, :], start=True, stop=True)
                    ins.then_inc(mix_done, 1)
                if v.live(3):
                    n, s = v.chunk(3), v.slot(3, 2)
                    pe.wait_ge(diag_ready, n + 1)
                    pe.wait_ge(agg_ready, (n + 1) * K)
                    for k in range(K):
                        ins = pe.matmul(ps_own[:, :], head_diag[s][:, k, :], agg[s][:, k, :],
                                        start=isinstance(n, int) and n == 0 and k == 0, stop=False)
                    ins.then_inc(own_added, 1)
            pipeline(pe, MCHUNKS, R, 3, R, step)

        @block.scalar
        def _(act):
            def step(v):
                if v.live(0):
                    n, s = v.chunk(0), v.slot(0, 2)
                    act.wait_ge(turned, n + 1)
                    wait(act, up_done, n - 1)
                    act.activation(rows_t[s][:, :], ps_t[s][:, :], ACT.Copy).then_inc(rows_t_ready, 1)
                if v.live(1):
                    n, s = v.chunk(1), v.slot(1, 2)
                    act.wait_ge(up_done, n + 1)
                    wait(act, mix_done, n - 1)
                    act.activation(up_t[s][:, :], ps_u[s][:, :], ACT.Gelu).then_inc(up_ready, 1)
                if v.live(2):
                    n, s, r = v.chunk(2), v.slot(2, 2), v.slot(2, R)
                    act.wait_ge(mix_done, n + 1)
                    wait(act, mixed, n - 1)
                    wait(act, prod_ready, (n - 1) * K)
                    act.activation(mix[s][:, :, :], ps_m[s][:, 0:K * MIX].rearrange("p (k m) -> p k m", m=MIX),
                                   ACT.Copy).then_inc(mix_ready, 1)
                if v.live(3):
                    n, s = v.chunk(3), v.slot(3, 2)
                    wait(act, outs_ready, n - 1)
                    for k in range(K):
                        act.wait_ge(agg_ready, n * K + (k + 1))
                        act.activation(act_agg[s][:, k, :], agg[s][:, k, :], ACT.Gelu).then_inc(gelu_ready, 1)
                if v.live(2):
                    n, s, r = v.chunk(2), v.slot(2, 2), v.slot(2, R)
                    act.wait_ge(mix_ready, n + 1)
                    for k in range(K):
                        wait(act, agg_ready, (n - 2) * K + (k + 1))
                        for m in range(MIX):
                            ins = act.activation(prod[s][:, k, m * D:(m + 1) * D], rows[r][:, k, :], ACT.Copy,
                                                 scale=mix[s][:, k, m:m + 1])
                        ins.then_inc(prod_ready, 1)
            pipeline(act, MCHUNKS, R, 3, R, step)

        @block.vector
        def _(dve):
            chain = Chain(dve, chain_sem)
            chain.mark(dve.memset(mix_sum[:, :, 0:1], 0.0))
            chain.mark(dve.memset(agg[1][:, K - 1, :], 0.0))
            for n in range(R):
                dve.tensor_copy(gidx[n][:, :], c["gather_idx"][:, n * K:(n + 1) * K]).then_inc(idx_staged, 1)
            chain.settle()
            chain.restart()

            def prepare(v):
                n, s, r = v.chunk(2), v.slot(2, 2), v.slot(2, R)
                c0 = n * K
                now, new = bass.ds(c0, K), bass.ds(c0 + 1, K)
                dve.wait_ge(gathered[r], (v.turn(2, R) + 1) * (16 * K))
                dve.tensor_scalar(gidx[r][:, :], c["gather_idx"][:, bass.ds(c0 + R * K, K)], 0.0, None,
                                  ALU.add).then_inc(idx_staged, 1)
                wait(dve, own_added, n - 1)
                dve.tensor_tensor(head_diag[s][:, :, :], c["ident"][:, :].unsqueeze(1).broadcast_to([P, K, P]),
                                  c["head"][:, now].unsqueeze(2).broadcast_to([P, K, P]), ALU.mult).then_inc(diag_ready, 1)
                dve.wait_ge(mix_ready, n + 1)
                for m in range(MIX):
                    ins = dve.tensor_tensor_scan(mix_sum[:, m, new], c["cont"][:, now], mix[s][:, :, m],
                                                 mix_sum[:, m, bass.ds(c0, 1)], ALU.mult, ALU.add)
                    if m < MIX - 1:
                        chain.mark(ins)
                chain.settle()
                ins.then_inc(mixed, 1)
                dve.wait_ge(mixed, n + 1)
                chain.mark(dve.tensor_tensor(mix_mean[s][:, :, :], mix_sum[:, :, new].rearrange("p m k -> p k m"),
                                             c["inv_count"][:, now].unsqueeze(2).broadcast_to([P, K, MIX]), ALU.mult))
                wait(dve, gelu_ready, (n - 1) * K)

            def accumulate(v, k):
                n, s = v.chunk(2), v.slot(2, 2)
                prev = agg[1 - s][:, K - 1, :] if k == 0 else agg[s][:, k - 1, :]
                dve.wait_ge(prod_ready, n * K + (k + 1))
                if not (isinstance(n, int) and n == 0 and k == 0):
                    dve.wait_ge(agg_ready, n * K + k)
                dve.scalar_tensor_tensor(agg[s][:, k, :], prev, c["cont"][:, bass.ds(n * K + k, 1)], prod[s][:, k, :],
                                         ALU.mult, ALU.add).then_inc(agg_ready, 1)

            def contract(v, m):
                n, s, r = v.chunk(3), v.slot(3, 2), v.slot(3, R)
                if m == 0:
                    wait(dve, scattered[r], v.turn(3, R) * (16 * K))
                    dve.wait_ge(gelu_ready, (n + 1) * K)
                    chain.mark(dve.tensor_scalar(sidx[r][:, :], c["scatter_idx"][:, bass.ds(n * K, K)], 0.0, None, ALU.add))
                chain.settle()
                for k in range(K):
                    if m == 0:
                        ins = dve.tensor_scalar(outs[r][:, k, :], act_agg[s][:, k, 0:D], mix_mean[s][:, k, 0:1],
                                                None, ALU.mult)
                    else:
                        ins = dve.scalar_tensor_tensor(outs[r][:, k, :], act_agg[s][:, k, m * D:(m + 1) * D],
                                                       mix_mean[s][:, k, m:m + 1], outs[r][:, k, :], ALU.mult, ALU.add)
                    if m == MIX - 1 and k == K - 1:
                        chain.settle()
                        ins.then_inc(outs_ready, 1)
                    else:
                        chain.mark(ins)

            def step(v):
                if v.live(2):
                    prepare(v)
                for j in range(MIX):
                    if v.live(2):
                        accumulate(v, j)
                    if v.live(3):
                        contract(v, j)
            pipeline(dve, MCHUNKS, R, 3, R, step, chain.restart)

    with nc.Block() as block:
        @block.gpsimd
        def _(pool):
            pool.wait_ge(fix_dve, 3)
            scatter(pool, agg_table, c["fix_idx"][:, 0:1], fixed[:, :]).then_inc(fix_scattered, 16)
            pool.wait_ge(fix_scattered, 16)

        @block.tensor
        def _(pe):
            pe.matmul(ps_own[:, :], c["take"][:, :], agg[1][:, K - 1, :], start=False, stop=True).then_inc(fix_pe, 1)
            pe.wait_ge(fix_dve, 1)
            pe.matmul(ps_b[:, 0:MIX + 1], c["take"][:, :], states[:, :], start=True, stop=True).then_inc(fix_pe, 1)

        @block.scalar
        def _(act):
            act.wait_ge(fix_dve, 2)
            act.activation(total[:, :], total[:, :], ACT.Gelu).then_inc(fix_act, 1)

        @block.vector
        def _(dve):
            chain = Chain(dve, chain_sem)
            chain.link(dve.tensor_copy(states[:, 0:MIX], mix_sum[:, :, COLS]))
            dve.tensor_copy(states[:, MIX:MIX + 1], c["count"][:, COLS:COLS + 1]).then_inc(fix_dve, 1)
            dve.wait_ge(fix_pe, 1)
            dve.tensor_copy(total[:, :], ps_own[:, :]).then_inc(fix_dve, 1)
            for m in range(MIX + 1):
                series = mix_sum[:, m, 1:COLS + 1] if m < MIX else c["count"][:, 1:COLS + 1]
                chain.link(dve.tensor_tensor(c["wide"][:, :], series, c["head"][:, :], ALU.mult))
                chain.link(dve.tensor_reduce(own_small[:, m:m + 1], c["wide"][:, :], AX.X, ALU.add))
            dve.wait_ge(fix_pe, 2)
            chain.link(dve.tensor_tensor(own_small[:, :], own_small[:, :], ps_b[:, 0:MIX + 1], ALU.add))
            chain.link(dve.tensor_scalar(own_small[:, MIX:MIX + 1], own_small[:, MIX:MIX + 1], 1.0, None, ALU.max))
            dve.wait_ge(fix_dve, 2)
            chain.link(dve.reciprocal(states[:, 0:1], own_small[:, MIX:MIX + 1]))
            chain.link(dve.tensor_scalar(own_small[:, 0:MIX], own_small[:, 0:MIX], states[:, 0:1], None, ALU.mult))
            dve.wait_ge(fix_act, 1)
            chain.link(dve.tensor_tensor(heads(total[:, :]), heads(total[:, :]),
                                         own_small[:, 0:MIX].unsqueeze(2).broadcast_to([P, MIX, D]), ALU.mult))
            dve.tensor_reduce(fixed[:, :], total[:, :].rearrange("p (m d) -> p d m", m=MIX), AX.X, ALU.add).then_inc(fix_dve, 1)


def node_pass_out(nc, scope, agg_table, hidden, normed, out, c):
    def sb(name, shape, dt=F32):
        return scope.enter_context(nc.sbuf_tensor(f"no_{name}", shape, dt))

    def ps(name):
        return scope.enter_context(nc.psum_tensor(f"no_{name}", [P, 512], F32))

    def sem(name):
        return scope.enter_context(nc.semaphore(f"no_{name}"))

    R = 4
    L = 8
    total = NCHUNKS + 1
    parts = [[sb(f"parts{a}{r}", [P, KN, D]) for r in range(L)] for a in range(2)]
    x_in = [sb(f"x_in{r}", [P, KN, D]) for r in range(L)]
    feat_t = [[sb(f"feat_t{a}{s}", [P, KN * P]) for s in range(2)] for a in range(2)]
    y = [sb(f"y{r}", [P, KN, D]) for r in range(R)]
    ps_f = [[ps(f"ps_f{a}{s}") for s in range(2)] for a in range(2)]
    ps_o = [ps(f"ps_o{s}") for s in range(2)]

    norm = RowNorm(sb, sem, y, R)
    loaded = [sem(f"loaded{r}") for r in range(L)]
    turned = sem("turned")
    feat_ready = sem("feat_ready")
    projected = sem("projected")
    biased = sem("biased")
    added = sem("added")
    stored = [sem(f"stored{r}") for r in range(R)]
    chain_sem = sem("chain")

    with nc.Block() as block:
        @block.sync
        def _(sp):
            def step(v):
                if v.live(0):
                    n, r, k = v.chunk(0), v.slot(0, L), node_cols(v.chunk(0))
                    wait(sp, added, n - L + 1)
                    for tile, table in ((parts[0][r], agg_table), (parts[1][r], hidden), (x_in[r], normed)):
                        sp.dma_start(tile[:, 0:k, :], node_rows(table, n)).then_inc(loaded[r], 16)
                if v.live(8):
                    n, r, k = v.chunk(8), v.slot(8, R), node_cols(v.chunk(8))
                    sp.wait_ge(norm.y_ready, n + 1)
                    sp.dma_start(node_rows(out, n, True), y[r][store_lo(n):P, 0:k, :]).then_inc(stored[r], 16)
            pipeline(sp, total, L, 8, L, step)
            for r in range(R):
                sp.wait_ge(stored[r], 16 * len(range(r, total, R)))

        @block.gpsimd
        def _(pool):
            pool.memset(norm.half[:, :], -0.5).then_inc(biased, 1)
            pool.wait_ge(biased, 1)

            def step(v):
                if v.live(0):
                    n, r, k = v.chunk(0), v.slot(0, L), node_cols(v.chunk(0))
                    pool.wait_ge(loaded[r], (v.turn(0, L) + 1) * 48)
                    pool.tensor_tensor(x_in[r][:, 0:k, :], x_in[r][:, 0:k, :],
                                       c["ob_rows"][:, :].unsqueeze(1).broadcast_to([P, k, D]),
                                       ALU.add).then_inc(biased, 1)
                if v.live(1):
                    norm.rstds(pool, v)
            pipeline(pool, total, L, 1, L, step)

        @block.tensor
        def _(pe):
            def step(v):
                if v.live(0):
                    n, r, s, k = v.chunk(0), v.slot(0, L), v.slot(0, 2), node_cols(v.chunk(0))
                    pe.wait_ge(loaded[r], (v.turn(0, L) + 1) * 48)
                    for a in range(2):
                        wait(pe, feat_ready, n * 2 - 3 + a)
                        for j in range(k):
                            ins = pe.transpose(ps_f[a][s][:, j * P:(j + 1) * P], parts[a][r][:, j, :], c["ident"][:, :])
                        ins.then_inc(turned, 1)
                if v.live(1):
                    n, s, k = v.chunk(1), v.slot(1, 2), node_cols(v.chunk(1))
                    pe.wait_ge(feat_ready, n * 2 + 2)
                    wait(pe, added, n - 1)
                    for j in range(k):
                        for a in range(2):
                            ins = pe.matmul(ps_o[s][:, j * P:(j + 1) * P], feat_t[a][s][:, j * P:(j + 1) * P],
                                            c["w2t"][:, a, :], start=(a == 0), stop=(a == 1))
                    ins.then_inc(projected, 1)
            pipeline(pe, total, L, 1, L, step)

        @block.scalar
        def _(act):
            def step(v):
                if v.live(0):
                    n, s, k = v.chunk(0), v.slot(0, 2), node_cols(v.chunk(0))
                    for a in range(2):
                        act.wait_ge(turned, n * 2 + 1 + a)
                        wait(act, projected, n - 1)
                        act.activation(feat_t[a][s][:, 0:k * P], ps_f[a][s][:, 0:k * P], ACT.Gelu).then_inc(feat_ready, 1)
                if v.live(2):
                    norm.squares(act, v, 2)
            pipeline(act, total, L, 2, L, step)

        @block.vector
        def _(dve):
            chain = Chain(dve, chain_sem)

            def step(v):
                if v.live(0):
                    n, r, q, s, k = v.chunk(0), v.slot(0, R), v.slot(0, L), v.slot(0, 2), node_cols(v.chunk(0))
                    dve.wait_ge(biased, n + 2)
                    dve.wait_ge(projected, n + 1)
                    wait(dve, stored[r], v.turn(0, R) * 16)
                    dve.tensor_tensor(y[r][:, 0:k, :], ps_o[s][:, 0:k * P].rearrange("p (a b) -> p a b", a=k),
                                      x_in[q][:, 0:k, :], ALU.add).then_inc(added, 1)
                    dve.wait_ge(added, n + 1)
                    norm.sums(dve, chain, v)
                if v.live(1):
                    norm.variances(dve, v)
                if v.live(2):
                    norm.normalise(dve, chain, v)
            pipeline(dve, total, L, 2, L, step, chain.restart)


_INS = ["x", "src", "dst"] + [f"L0_gnn_{w}{l}" for l in range(3) for w in ("Wl", "Wr", "att", "b")] \
    + [f"L1_gnn_{w}" for w in ("W1", "b1", "WA", "WB", "W2", "b2")]


def kernel(**inputs):
    import numpy as _np
    import concourse.bacc as _bacc
    from concourse import mybir as _mybir
    from concourse.bass_utils import run_bass_kernel_spmd as _run

    nc = _bacc.Bacc("TRN2", target_bir_lowering=False, num_devices=1)
    arrays, args = {}, {}
    for name in _INS:
        a = _np.ascontiguousarray(inputs[name])
        arrays[f"in_{name}"] = a
        args[name] = nc.dram_tensor(f"in_{name}", a.shape, _mybir.dt.from_np(a.dtype), kind="ExternalInput").ap()
    out = nc.dram_tensor("out_0", (N, D), F32, kind="ExternalOutput").ap()
    build(nc, args, out)
    r = _run(nc, [arrays], core_ids=[0])
    return r.results[0]["out_0"]
```

```python
import concourse.bass as bass
from concourse import mybir
from contextlib import ExitStack

F32 = mybir.dt.float32
I32 = mybir.dt.int32
ALU = mybir.AluOpType
ACT = mybir.ActivationFunctionType
AX = mybir.AxisListType

P = 128
D = 128
N = 50000
E = 75000
MIX = 4
K = 8
COLS = -(-E // (P * 2 * K)) * 2 * K
CHUNKS = COLS // K
FULL = E // COLS
REST = E - FULL * COLS
KM = 4
MCHUNKS = COLS // KM
NJ = N // P
KN = 3
NCHUNKS = NJ // KN
TAIL = N - P * NJ
BIG = 1.0e30
SKIP = 65536.0
PAIRS = COLS // 2
KP = K // 2
DUMP = N + 2
ALONE = DUMP + 2 * P
GAT_ROWS = ALONE + 2 * P
EPS = 1e-05
SLOPE = 0.2


class Chain:

    def __init__(self, eng, sem):
        self.eng, self.sem, self.n = eng, sem, 0

    def link(self, ins):
        self.n += 1
        ins.then_inc(self.sem, 1)
        self.eng.wait_ge(self.sem, self.n)

    def mark(self, ins):
        self.n += 1
        ins.then_inc(self.sem, 1)
        return self.n

    def after(self, n):
        if n is not None:
            self.eng.wait_ge(self.sem, n)

    def settle(self):
        self.eng.wait_ge(self.sem, self.n)

    def restart(self):
        self.eng.sem_inc(self.sem, 1)
        self.eng.wait_ge(self.sem, self.n + 1)
        self.eng.sem_clear(self.sem)
        self.n = 0


def run_bodies(eng, count, body):
    body(0, first=True, last=False)
    with eng.Fori(1, count - 1, 1) as i:
        body(i, first=False, last=False)
    body(count - 1, first=False, last=True)


def build(nc, t, out):
    ctx = ExitStack()
    with ctx:
        def sb(name, shape, dt=F32):
            return ctx.enter_context(nc.sbuf_tensor(name, shape, dt))

        def sem(name):
            return ctx.enter_context(nc.semaphore(name))

        def dram(name, shape):
            return nc.dram_tensor(name, shape, F32, kind="Internal").ap()

        gat_table = [dram(f"gat_table{l}", (GAT_ROWS, D)) for l in range(3)]
        normed = dram("normed", (N, D))
        hidden = dram("hidden", (N, D))
        agg_table = dram("agg_table", (N, D))

        ident = sb("ident", [P, P])
        ones = sb("ones", [P, P])
        wlr = sb("wlr", [P, 3, 2 * D])
        att = sb("att", [P, 3, D])
        gat_bias = sb("gat_bias", [P, 3])
        b2_rows = sb("b2_rows", [P, D])
        ob_rows = sb("ob_rows", [P, D])
        w1t = sb("w1t", [P, D])
        wat = sb("wat", [P, D])
        wbt = sb("wbt", [P, MIX])
        w2t = sb("w2t", [P, 2, D])
        b1_col = sb("b1_col", [P, 1])

        edge_dst = sb("edge_dst", [P, COLS + 2])
        gather_idx = sb("gather_idx", [P, COLS + 2 * K], I32)
        scatter_idx = sb("scatter_idx", [P, COLS], I32)
        pair_idx = sb("pair_idx", [P, PAIRS], I32)
        pick = sb("pick", [P, 3, PAIRS + 2 * KP], I32)
        inherit = sb("inherit", [P, COLS + 2 * K], I32)
        cont = sb("cont", [P, COLS])
        pen = sb("pen", [P, COLS])
        mult = sb("mult", [P, COLS])
        head = sb("head", [P, COLS])
        count = sb("count", [P, COLS + 1])
        inv_count = sb("inv_count", [P, COLS])
        first_node = sb("first_node", [P, 1], I32)
        own_row = sb("own_row", [P, 1], I32)
        fix_idx = sb("fix_idx", [P, 1], I32)
        take = sb("take", [P, P])
        take_pen = sb("take_pen", [P, P])

        run_max = sb("run_max", [P, COLS + 1])
        run_sum = sb("run_sum", [P, COLS + 1])
        wide = sb("wide", [P, COLS])

        with ExitStack() as scope:
            edge_in = scope.enter_context(nc.sbuf_tensor("edge_in", [P, COLS + 2], I32))
            src_in = scope.enter_context(nc.sbuf_tensor("src_in", [P, COLS], I32))
            w_in = scope.enter_context(nc.sbuf_tensor("w_in", [P, 5 * D], F32))
            first_dst = scope.enter_context(nc.sbuf_tensor("first_dst", [P, 1], F32))
            diag = scope.enter_context(nc.sbuf_tensor("diag", [P, P], F32))
            tri = scope.enter_context(nc.sbuf_tensor("tri", [P, P], F32))
            small = scope.enter_context(nc.sbuf_tensor("small", [P, 8], F32))
            both, only, dst_diff, pair_dst = (scope.enter_context(nc.sbuf_tensor(name, [P, PAIRS], F32))
                                              for name in ("both", "only", "dst_diff", "pair_dst"))
            ps_w = scope.enter_context(nc.psum_tensor("ps_w", [P, 4 * D], F32))
            ps_w2 = scope.enter_context(nc.psum_tensor("ps_w2", [P, 4 * D], F32))
            ps_g = scope.enter_context(nc.psum_tensor("ps_g", [P, 4 * D], F32))
            zeros = scope.enter_context(nc.sbuf_tensor("zeros", [P, 4 * D], F32))
            padded = sem("padded")
            zeroed = sem("zeroed")
            edges_in = sem("edges_in")
            weights_in = sem("weights_in")
            consts_made = sem("consts_made")
            weights_turned = sem("weights_turned")
            diag_made = sem("diag_made")
            nodes_spread = sem("nodes_spread")
            take_made = sem("take_made")
            take_turned = sem("take_turned")
            setup_chain = sem("setup_chain")

            with nc.Block() as block:
                @block.sync
                def _(sp):
                    sp.wait_ge(padded, 3)
                    dst, src = t["dst"], t["src"]
                    main = dst[0:FULL * COLS].rearrange("(p c) -> p c", c=COLS)
                    with nc.allow_non_contiguous_dma(reason="one word of each run"):
                        sp.dma_start(edge_in[0:FULL, 1:COLS + 1], main).then_inc(edges_in, 16)
                        sp.dma_start(edge_in[FULL:FULL + 1, 1:REST + 1],
                                     dst[FULL * COLS:E].rearrange("(p c) -> p c", p=1)).then_inc(edges_in, 16)
                        sp.dma_start(edge_in[1:FULL + 1, 0:1], main[:, COLS - 1:COLS]).then_inc(edges_in, 16)
                        sp.dma_start(edge_in[0:FULL - 1, COLS + 1:COLS + 2], main[1:FULL, 0:1]).then_inc(edges_in, 16)
                        sp.dma_start(edge_in[FULL - 1:FULL, COLS + 1:COLS + 2],
                                     dst[FULL * COLS:FULL * COLS + 1].rearrange("(p c) -> p c", p=1)).then_inc(edges_in, 16)
                        sp.dma_start(src_in[0:FULL, :],
                                     src[0:FULL * COLS].rearrange("(p c) -> p c", c=COLS)).then_inc(edges_in, 16)
                        sp.dma_start(src_in[FULL:FULL + 1, 0:REST],
                                     src[FULL * COLS:E].rearrange("(p c) -> p c", p=1)).then_inc(edges_in, 16)
                    for table in gat_table:
                        sp.dma_start(table[N:DUMP, :], zeros[0:2, 0:D]).then_inc(zeroed, 16)
                        sp.dma_start(table[DUMP:GAT_ROWS, :].rearrange("(p j) d -> p (j d)", p=P), zeros[:, :]).then_inc(zeroed, 16)
                    sp.wait_ge(zeroed, 16 * 6)

                @block.scalar
                def _(act):
                    with nc.allow_non_contiguous_dma(reason="biases, a word for each partition"):
                        for l in range(3):
                            act.dma_start(wlr[:, l, 0:D], t[f"L0_gnn_Wl{l}"]).then_inc(weights_in, 16)
                            act.dma_start(wlr[:, l, D:2 * D], t[f"L0_gnn_Wr{l}"]).then_inc(weights_in, 16)
                            act.dma_start(att[:, l, :], t[f"L0_gnn_att{l}"].unsqueeze(0).broadcast_to([P, D])).then_inc(weights_in, 16)
                            act.dma_start(gat_bias[:, l:l + 1], t[f"L0_gnn_b{l}"].unsqueeze(1)).then_inc(weights_in, 16)
                        act.dma_start(b1_col[:, :], t["L1_gnn_b1"].unsqueeze(1)).then_inc(weights_in, 16)
                    act.dma_start(b2_rows[:, :], t["L0_gnn_b2"].unsqueeze(0).broadcast_to([P, D])).then_inc(weights_in, 16)
                    act.dma_start(ob_rows[:, :], t["L1_gnn_b2"].unsqueeze(0).broadcast_to([P, D])).then_inc(weights_in, 16)
                    act.dma_start(w_in[:, 0:D], t["L1_gnn_W1"]).then_inc(weights_in, 16)
                    act.dma_start(w_in[:, D:2 * D], t["L1_gnn_WA"]).then_inc(weights_in, 16)
                    act.dma_start(w_in[:, 2 * D:4 * D], t["L1_gnn_W2"]).then_inc(weights_in, 16)
                    act.dma_start(w_in[0:MIX, 4 * D:5 * D], t["L1_gnn_WB"]).then_inc(weights_in, 16)

                @block.gpsimd
                def _(pool):
                    pool.memset(ones[:, :], 1.0).then_inc(consts_made, 1)
                    pool.memset(ident[:, :], 0.0).then_inc(consts_made, 1)
                    pool.wait_ge(consts_made, 2)
                    pool.affine_select(out=ident[:, :], in_=ident[:, :], compare_op=ALU.not_equal, fill=1.0,
                                       base=0, pattern=[[-1, P]], channel_multiplier=1).then_inc(consts_made, 1)
                    pool.affine_select(out=tri[:, :], in_=ones[:, :], compare_op=ALU.is_gt, fill=0.0,
                                       base=0, pattern=[[-1, P]], channel_multiplier=1).then_inc(consts_made, 1)

                @block.tensor
                def _(pe):
                    pe.wait_ge(consts_made, 4)
                    pe.wait_ge(weights_in, 16 * 19)
                    for j in range(4):
                        pe.transpose(ps_w[:, j * D:(j + 1) * D], w_in[:, j * D:(j + 1) * D], ident[:, :]).then_inc(weights_turned, 1)
                    pe.transpose(ps_w2[:, 0:MIX], w_in[0:MIX, 4 * D:5 * D], ident[0:MIX, 0:MIX]).then_inc(weights_turned, 1)
                    pe.wait_ge(diag_made, 1)
                    pe.matmul(ps_g[:, 0:P], ones[:, :], diag[:, :], start=True, stop=True).then_inc(nodes_spread, 1)
                    pe.wait_ge(take_made, 1)
                    pe.transpose(ps_g[:, P:2 * P], take[:, :], ident[:, :]).then_inc(take_turned, 1)

                @block.vector
                def _(dve):
                    chain = Chain(dve, setup_chain)
                    dve.memset(edge_in[:, :], N).then_inc(padded, 1)
                    dve.memset(src_in[:, :], 0).then_inc(padded, 1)
                    dve.memset(zeros[:, :], 0.0).then_inc(padded, 1)
                    dve.wait_ge(edges_in, 16 * 7)
                    chain.mark(dve.memset(gather_idx[:, COLS:COLS + 2 * K], 0))
                    chain.mark(dve.memset(inherit[:, COLS:COLS + 2 * K], 0))
                    chain.mark(dve.memset(pick[:, :, :], 0))
                    chain.mark(dve.memset(count[:, 0:1], 0.0))
                    chain.mark(dve.tensor_copy(gather_idx[:, 0:COLS], src_in[:, ::-1]))
                    chain.link(dve.tensor_copy(edge_dst[:, :], edge_in[:, ::-1]))
                    here, before, after = edge_dst[:, 1:COLS + 1], edge_dst[:, 0:COLS], edge_dst[:, 2:COLS + 2]
                    chain.link(dve.tensor_tensor(cont[:, :], here, before, ALU.is_equal))
                    chain.mark(dve.tensor_copy(inherit[:, 0:COLS], cont[:, :]))
                    chain.link(dve.tensor_scalar(mult[:, :], cont[:, :], -1.0, 2.0, ALU.mult, ALU.add))
                    chain.link(dve.memset(cont[:, 0:1], 0.0))
                    chain.link(dve.tensor_scalar(pen[:, :], cont[:, :], 1.0, BIG, ALU.subtract, ALU.mult))
                    chain.link(dve.tensor_tensor(wide[:, :], here, after, ALU.is_equal))
                    chain.link(dve.scalar_tensor_tensor(scatter_idx[:, :], wide[:, :], SKIP, here, ALU.mult, ALU.add))
                    chain.link(dve.tensor_copy(first_dst[:, :], edge_dst[:, 1:2]))
                    chain.link(dve.tensor_scalar(wide[:, :], wide[:, :], -1.0, 1.0, ALU.mult, ALU.add))
                    chain.link(dve.scalar_tensor_tensor(head[:, :], here, first_dst[:, 0:1], wide[:, :], ALU.is_equal, ALU.mult))
                    chain.link(dve.tensor_reduce(small[:, 0:1], head[:, :], AX.X, ALU.add))
                    chain.link(dve.tensor_scalar(small[:, 1:2], small[:, 0:1], -SKIP, SKIP, ALU.mult, ALU.add))
                    chain.mark(dve.tensor_tensor(fix_idx[:, :], first_dst[:, :], small[:, 1:2], ALU.add))
                    chain.mark(dve.tensor_scalar(first_node[:, :], first_dst[:, :], float(N - 1), None, ALU.min))
                    def pairs(ap):
                        p2 = ap.rearrange("p (c t) -> p c t", t=2)
                        return p2[:, :, 0], p2[:, :, 1]
                    (end_a, end_b), (dst_a, dst_b), (head_a, head_b) = pairs(wide[:, :]), pairs(here), pairs(head[:, :])
                    chain.link(dve.tensor_tensor(both[:, :], end_a, end_b, ALU.mult))
                    chain.mark(dve.tensor_scalar(pick[:, 0, KP:KP + PAIRS], both[:, :], -1.0, 1.0, ALU.mult, ALU.add))
                    chain.link(dve.tensor_tensor(only[:, :], end_a, both[:, :], ALU.subtract))
                    chain.mark(dve.tensor_copy(pick[:, 1, KP:KP + PAIRS], only[:, :]))
                    chain.link(dve.tensor_tensor(dst_diff[:, :], dst_a, dst_b, ALU.subtract))
                    chain.link(dve.tensor_tensor(dst_diff[:, :], dst_diff[:, :], only[:, :], ALU.mult))
                    chain.link(dve.tensor_tensor(pair_dst[:, :], dst_b, dst_diff[:, :], ALU.add))
                    dve.wait_ge(consts_made, 4)
                    chain.link(dve.tensor_reduce(small[:, 2:3], tri[:, :], AX.X, ALU.add))
                    chain.link(dve.tensor_scalar(small[:, 3:4], small[:, 2:3], 2.0, float(DUMP), ALU.mult, ALU.add))
                    chain.link(dve.tensor_scalar(small[:, 4:5], small[:, 2:3], 2.0, float(ALONE), ALU.mult, ALU.add))
                    chain.link(dve.tensor_tensor(only[:, :], only[:, :], end_b, ALU.add))
                    chain.link(dve.tensor_scalar(only[:, :], only[:, :], -1.0, 1.0, ALU.mult, ALU.add))
                    chain.mark(dve.tensor_copy(pick[:, 2, KP:KP + PAIRS], only[:, :]))
                    chain.link(dve.tensor_scalar(dst_diff[:, :], pair_dst[:, :], -1.0, small[:, 3:4], ALU.mult, ALU.add))
                    chain.link(dve.tensor_tensor(dst_diff[:, :], dst_diff[:, :], only[:, :], ALU.mult))
                    chain.link(dve.tensor_tensor(pair_dst[:, :], pair_dst[:, :], dst_diff[:, :], ALU.add))
                    chain.link(dve.tensor_tensor(only[:, :], head_a, head_b, ALU.add))
                    chain.link(dve.tensor_scalar(both[:, :], both[:, :], -1.0, 1.0, ALU.mult, ALU.add))
                    chain.link(dve.tensor_tensor(only[:, :], only[:, :], both[:, :], ALU.mult))
                    chain.link(dve.tensor_scalar(dst_diff[:, :], pair_dst[:, :], -1.0, small[:, 4:5], ALU.mult, ALU.add))
                    chain.link(dve.tensor_tensor(dst_diff[:, :], dst_diff[:, :], only[:, :], ALU.mult))
                    chain.mark(dve.tensor_tensor(pair_idx[:, :], pair_dst[:, :], dst_diff[:, :], ALU.add))
                    chain.link(dve.tensor_reduce(small[:, 5:6], only[:, :], AX.X, ALU.add))
                    chain.link(dve.tensor_tensor(small[:, 6:7], small[:, 4:5], first_dst[:, :], ALU.subtract))
                    chain.link(dve.scalar_tensor_tensor(small[:, 6:7], small[:, 6:7], small[:, 5:6], first_dst[:, :], ALU.mult, ALU.add))
                    chain.link(dve.tensor_tensor(small[:, 7:8], small[:, 6:7], small[:, 3:4], ALU.subtract))
                    chain.mark(dve.scalar_tensor_tensor(own_row[:, :], small[:, 7:8], small[:, 0:1], small[:, 3:4], ALU.mult, ALU.add))
                    chain.link(dve.memset(wide[:, :], 1.0))
                    chain.link(dve.tensor_tensor_scan(count[:, 1:COLS + 1], cont[:, :], wide[:, :], 0.0, ALU.mult, ALU.add))
                    chain.mark(dve.reciprocal(inv_count[:, :], count[:, 1:COLS + 1]))
                    dve.wait_ge(consts_made, 4)
                    dve.tensor_scalar(diag[:, :], ident[:, :], first_dst[:, 0:1], None, ALU.mult).then_inc(diag_made, 1)
                    dve.wait_ge(nodes_spread, 1)
                    dve.scalar_tensor_tensor(take[:, :], ps_g[:, 0:P], edge_dst[:, COLS:COLS + 1], tri[:, :],
                                             ALU.is_equal, ALU.mult).then_inc(take_made, 1)
                    dve.wait_ge(take_turned, 1)
                    chain.mark(dve.tensor_scalar(take_pen[:, :], ps_g[:, P:2 * P], 1.0, BIG, ALU.subtract, ALU.mult))
                    dve.wait_ge(weights_turned, 5)
                    chain.mark(dve.tensor_copy(w1t[:, :], ps_w[:, 0:D]))
                    chain.mark(dve.tensor_copy(wat[:, :], ps_w[:, D:2 * D]))
                    chain.mark(dve.tensor_copy(w2t[:, :, :], ps_w[:, 2 * D:4 * D].rearrange("p (a b) -> p a b", a=2)))
                    chain.mark(dve.tensor_copy(wbt[:, :], ps_w2[:, 0:MIX]))
                    chain.settle()

        tables = [t["x"]] + gat_table
        signals = GatSignals(lambda name: sem(f"gat_{name}"))
        for l in range(3):
            with ExitStack() as scope:
                gat_layer(nc, scope, signals, l, tables[l], tables[l + 1], wlr[:, l, :], att[:, l, :],
                          gat_bias[:, l - 1:l] if l else None,
                          dict(ident=ident, ones=ones, gather_idx=gather_idx, inherit=inherit, pen=pen,
                               mult=mult, head=head, first_node=first_node,
                               own_row=own_row, pair_idx=pair_idx, pick=pick,
                               fix_idx=fix_idx, take_pen=take_pen, run_max=run_max, run_sum=run_sum, wide=wide))

        with ExitStack() as scope:
            node_pass_hidden(nc, scope, t["x"], gat_table[2], normed, hidden,
                             dict(ident=ident, b2_rows=b2_rows, w1t=w1t, b1_col=b1_col))

        with ExitStack() as scope:
            mixing_pass(nc, scope, hidden, agg_table,
                        dict(ident=ident, gather_idx=gather_idx, scatter_idx=scatter_idx, cont=cont,
                             head=head, count=count, inv_count=inv_count,
                             fix_idx=fix_idx, take=take, wat=wat, wbt=wbt, wide=wide))

        with ExitStack() as scope:
            node_pass_out(nc, scope, agg_table, hidden, normed, out,
                          dict(ident=ident, ob_rows=ob_rows, w2t=w2t))


def gather(pool, dst, table, idx):
    return pool.indirect_dma_start(dst, None, table[:, :], bass.IndirectOffsetOnAxis(ap=idx, axis=0))


def scatter(pool, table, idx, rows):
    return pool.indirect_dma_start(table[:, :], bass.IndirectOffsetOnAxis(ap=idx, axis=0), rows, None,
                                   bounds_check=N - 1, oob_is_err=False)


def scatter_block(pool, table, idx, rows):
    return pool.indirect_dma_start(table[:, :], bass.IndirectOffsetOnAxis(ap=idx, axis=0), rows, None)


class GatSignals:

    def __init__(self, sem):
        self.seed_gathered = sem("seed_gathered")
        self.seed_turned = sem("seed_turned")
        self.seed_evacuated = sem("seed_evacuated")
        self.seed_projected = sem("seed_projected")
        self.idx_staged = sem("idx_staged")
        self.gathered = [sem(f"gathered{s}") for s in range(2)]
        self.turned = sem("turned")
        self.evacuated = sem("evacuated")
        self.projected = sem("projected")
        self.xlr_ready = sem("xlr_ready")
        self.xr_taken = sem("xr_taken")
        self.drop_ready = sem("drop_ready")
        self.grown_ready = sem("grown_ready")
        self.share_ready = sem("share_ready")
        self.part_ready = sem("part_ready")
        self.outs_ready = sem("outs_ready")
        self.scattered = sem("scattered")
        self.chain = sem("chain")
        self.pool_passed = sem("pool_passed")
        self.dve_passed = sem("dve_passed")
        self.fix_gathered = sem("fix_gathered")
        self.fix_scattered = sem("fix_scattered")
        self.fix_dve = sem("fix_dve")
        self.fix_pe = sem("fix_pe")
        self.fix_act = sem("fix_act")


def gat_layer(nc, scope, sg, l, table_in, table_out, w, att_rows, bias, c):
    def sb(name, shape, dt=F32):
        return scope.enter_context(nc.sbuf_tensor(f"g{l}_{name}", shape, dt))

    def ps(name):
        return scope.enter_context(nc.psum_tensor(f"g{l}_{name}", [P, 512], F32))

    rows = [sb(f"rows{s}", [P, K, D]) for s in range(2)]
    rows_t = [sb(f"rows_t{h}", [P, 4 * P]) for h in range(2)]
    xlr = [sb(f"xlr{s}", [P, K, 2 * D]) for s in range(2)]
    mixed = sb("mixed", [P, K, D])
    score = sb("score", [P, K])
    drop = sb("drop", [P, 2 * K])
    grown = sb("grown", [P, 2 * K])
    inv_sum = sb("inv_sum", [P, K])
    old_share = [sb(f"old_share{s}", [P, K]) for s in range(2)]
    new_share = sb("new_share", [P, K])
    tmp = sb("tmp", [P, K])
    part = sb("part", [P, K, D])
    carry = sb("carry", [P, D])
    blocks = [sb(f"blocks{s}", [P, KP, 2, D]) for s in range(2)]
    gidx = [sb(f"gidx{r}", [P, K], I32) for r in range(4)]
    sidx = [sb(f"sidx{s}", [P, KP], I32) for s in range(2)]
    picked = sb("picked", [P, 3, 4 * KP], I32)
    mask = sb("mask", [P, 4 * K], I32)
    ps_t = [ps(f"ps_t{h}") for h in range(2)]
    ps_x = [ps(f"ps_x{j}") for j in range(4)]
    ps_b = [ps(f"ps_b{j}") for j in range(2)]
    diag = sb("diag", [P, 2 * P])
    share = sb("share", [P, P + 1])
    share_t = sb("share_t", [P, P])
    fixed = sb("fixed", [P, D])
    st = sb("st", [P, 8])

    def activate(act, dst, src):
        if bias is None:
            return act.activation(dst, src, ACT.Copy)
        return act.activation(dst, src, ACT.Relu, bias=bias)

    BODIES = CHUNKS // 2
    DONE, TURNS = l * CHUNKS, l * BODIES
    STAGED = l * (CHUNKS // 4 * 4 + 4)

    with nc.Block() as block:
        @block.gpsimd
        def _(pool):
            gather(pool, rows[1][:, 0, :], table_in, c["first_node"][:, 0:1]).then_inc(sg.seed_gathered, 16)

            pool.wait_ge(sg.idx_staged, STAGED + 1)
            scatter(pool, table_out, c["fix_idx"][:, 0:1], fixed[:, :]).then_inc(sg.fix_scattered, 16)

            def step(v):
                if v.live(0):
                    n, s, r = v.chunk(0), v.slot(0, 2), v.slot(0, 4)
                    if not isinstance(n, int) or n >= 2:
                        pool.wait_ge(sg.turned, (n + (DONE - 1)) * 2)
                    elif n == 1:
                        pool.wait_ge(sg.seed_turned, l + 1)
                    pool.wait_ge(sg.idx_staged, n + (STAGED + 1))
                    pool.sem_inc(sg.pool_passed, 1)
                if v.live(4):
                    pool.wait_ge(sg.outs_ready, v.chunk(4) + (DONE + 1))
                    pool.sem_inc(sg.pool_passed, 1)
                    if isinstance(v.chunk(4), int) and v.chunk(4) == 0:
                        pool.wait_ge(sg.fix_scattered, 16 * (2 * l + 1))
                for j in range(KP):
                    if v.live(4):
                        n, s = v.chunk(4), v.slot(4, 2)
                        if not (isinstance(n, int) and n == 0 and j == 0):
                            pool.wait_ge(sg.scattered, n * (16 * KP) + (DONE * KP + j) * 16)
                            pool.sem_inc(sg.pool_passed, 1)
                        scatter_block(pool, table_out, sidx[s][:, j:j + 1],
                                      blocks[s][:, j, :, :].rearrange("p a d -> p (a d)")).then_inc(sg.scattered, 16)
                    if v.live(0):
                        s, r = v.slot(0, 2), v.slot(0, 4)
                        for k in (2 * j, 2 * j + 1):
                            gather(pool, rows[s][:, k, :], table_in, gidx[r][:, k:k + 1]).then_inc(sg.gathered[s], 16)
            pipeline(pool, CHUNKS, 4, 4, 4, step)
            pool.wait_ge(sg.scattered, 16 * KP * (DONE + CHUNKS))

        @block.tensor
        def _(pe):
            pe.wait_ge(sg.seed_gathered, 16 * (l + 1))
            pe.transpose(ps_b[0][:, 0:P], rows[1][:, 0, :], c["ident"][:, :]).then_inc(sg.seed_turned, 1)
            pe.wait_ge(sg.seed_evacuated, l + 1)
            pe.matmul(ps_b[0][:, P:2 * P], rows_t[0][:, 0:P], w[:, D:2 * D], start=True, stop=True).then_inc(sg.seed_projected, 1)

            def body(i, first, last):
                for s in range(2):
                    n = i * 2 + s
                    at = n + DONE
                    pe.wait_ge(sg.gathered[s], (i + (TURNS + 1)) * (16 * K))
                    for h in range(2):
                        if not (first and s == 0):
                            pe.wait_ge(sg.evacuated, at * 2 - 1 + h)
                        for k in range(4):
                            ins = pe.transpose(ps_t[h][:, k * P:(k + 1) * P], rows[s][:, 4 * h + k, :], c["ident"][:, :])
                        ins.then_inc(sg.turned, 1)
                    for j in range(4):
                        if j % 2 == 0:
                            pe.wait_ge(sg.evacuated, at * 2 + 1 + j // 2)
                        if not (first and s == 0):
                            pe.wait_ge(sg.xlr_ready, at * 4 - 3 + j)
                        for k in range(2):
                            kk = (2 * j + k) % 4
                            ins = pe.matmul(ps_x[j][:, k * 2 * D:(k + 1) * 2 * D],
                                            rows_t[j // 2][:, kk * P:(kk + 1) * P], w, start=True, stop=True)
                        ins.then_inc(sg.projected, 1)
            run_bodies(pe, BODIES, body)

        @block.scalar
        def _(act):
            act.wait_ge(sg.seed_turned, l + 1)
            activate(act, rows_t[0][:, 0:P], ps_b[0][:, 0:P]).then_inc(sg.seed_evacuated, 1)

            def evacuate(n, s, full):
                for h in range(2):
                    act.wait_ge(sg.turned, (n + DONE) * 2 + 1 + h)
                    if full:
                        act.wait_ge(sg.projected, (n + DONE) * 4 - 2 + 2 * h)
                    elif h == 0:
                        act.wait_ge(sg.seed_projected, l + 1)
                    activate(act, rows_t[h][:, :], ps_t[h][:, :]).then_inc(sg.evacuated, 1)
                for j in range(4):
                    act.wait_ge(sg.projected, (n + DONE) * 4 + 1 + j)
                    act.activation(xlr[s][:, 2 * j:2 * j + 2, :], ps_x[j][:, :].rearrange("p (a b) -> p a b", a=2),
                                   ACT.Copy).then_inc(sg.xlr_ready, 1)

            evacuate(0, 0, False)

            def body(i, first, last):
                for s in range(2):
                    n = i * 2 + s
                    at = n + DONE
                    if not (last and s == 1):
                        act.wait_ge(sg.xr_taken, at + 1)
                        if not (first and s == 0):
                            act.wait_ge(sg.part_ready, at * K)
                        evacuate(n + 1, 1 - s, True)
                    act.wait_ge(sg.drop_ready, at + 1)
                    act.activation(grown[:, :], drop[:, :], ACT.Exp).then_inc(sg.grown_ready, 1)
                    for k in range(K):
                        act.wait_ge(sg.share_ready, at + 1)
                        act.activation(part[:, k, :], xlr[s][:, k, 0:D], ACT.Copy,
                                       scale=new_share[:, k:k + 1]).then_inc(sg.part_ready, 1)
            run_bodies(act, BODIES, body)

        @block.vector
        def _(dve):
            chain = Chain(dve, sg.chain)
            chain.mark(dve.memset(c["run_max"][:, 0:1], -BIG))
            chain.mark(dve.memset(c["run_sum"][:, 0:1], 0.0))
            chain.mark(dve.memset(carry[:, :], 0.0))
            chain.mark(dve.memset(blocks[1][:, KP - 1, 0, :], 0.0))
            chain.link(dve.memset(fixed[:, :], 0.0))
            for r in range(4):
                dve.tensor_copy(gidx[r][:, :], c["gather_idx"][:, r * K:(r + 1) * K]).then_inc(sg.idx_staged, 1)
            dve.wait_ge(sg.seed_projected, l + 1)
            chain.mark(dve.tensor_copy(xlr[1][:, K - 1, D:2 * D], ps_b[0][:, P:2 * P]))
            chain.settle()
            chain.restart()
            run_max, run_sum = c["run_max"], c["run_sum"]
            done = {}

            def inherit_xr(v, k):
                s = v.slot(0, 2)
                prev = xlr[1 - s][:, K - 1, D:2 * D] if k == 0 else xlr[s][:, k - 1, D:2 * D]
                if k == 1:
                    dve.wait_ge(sg.xr_taken, v.chunk(0) + (DONE + 1))
                    dve.sem_inc(sg.dve_passed, 1)
                elif k > 1:
                    chain.after(done["xr"])
                m = v.u * K + k
                ins = dve.copy_predicated(xlr[s][:, k, D:2 * D], mask[:, m:m + 1].broadcast_to([P, D]), prev)
                if k == 0:
                    ins.then_inc(sg.xr_taken, 1)
                else:
                    done["xr"] = chain.mark(ins)

            def state(v, k):
                n, s, j = v.chunk(1), v.slot(1, 2), k // 2

                def place(k):
                    return carry[:, :] if k in (-1, K - 1) else blocks[s][:, k // 2, 1 - k % 2, :]
                dve.wait_ge(sg.part_ready, n * K + (DONE * K + k + 1))
                chain.after(done.get("old_share") if k == 0 else done["state"])
                done["state"] = chain.mark(dve.scalar_tensor_tensor(place(k), place(k - 1), old_share[s][:, k:k + 1],
                                                                    part[:, k, :], ALU.mult, ALU.add))

            def chosen(v, row, lo, hi):
                at = v.u * KP
                return picked[:, row, at + lo:at + hi].unsqueeze(2).broadcast_to([P, hi - lo, D])

            def place_last(v):
                if v.live(1):
                    chain.after(done["state"])
                    done["last"] = chain.mark(dve.tensor_copy(blocks[v.slot(1, 2)][:, KP - 1, 0, :], carry[:, :]))

            def take_first(v):
                if v.live(1):
                    b = blocks[v.slot(1, 2)]
                    chain.after(done["last"])
                    done["first"] = chain.mark(dve.copy_predicated(b[:, :, 0, :], chosen(v, 1, 0, KP), b[:, :, 1, :]))

            def take_kept(v, j):
                if v.live(1):
                    s = v.slot(1, 2)
                    kept = blocks[1 - s][:, KP - 1, 0:1, :] if j == 0 else blocks[s][:, j - 1, 0:1, :]
                    chain.after(done["first"] if j == 0 else done["kept"])
                    done["kept"] = chain.mark(dve.copy_predicated(blocks[s][:, j, 0:1, :], chosen(v, 2, j, j + 1), kept))

            def pair_up(v, lo, hi):
                if v.live(1):
                    s = v.slot(1, 2)
                    kept = blocks[1 - s][:, KP - 1:KP, 0, :] if lo == 0 else blocks[s][:, lo - 1:hi - 1, 0, :]
                    if lo == 0:
                        chain.after(done["first"])
                    else:
                        chain.settle()
                    ins = dve.copy_predicated(blocks[s][:, lo:hi, 1, :], chosen(v, 0, lo, hi), kept)
                    if hi < KP:
                        chain.mark(ins)
                    else:
                        ins.then_inc(sg.outs_ready, 1)

            def step(v):
                new_chunk, old_chunk = v.live(0), v.live(1)
                n, s = v.chunk(0), v.slot(0, 2)
                at = n + DONE
                now, new = bass.ds(n * K, K), bass.ds(n * K + 1, K)
                if old_chunk:
                    m, q = v.chunk(1), v.slot(1, 2)
                    if not isinstance(m, int) or m >= 1:
                        dve.wait_ge(sg.outs_ready, m + DONE)
                if v.u == 0:
                    chain.mark(dve.tensor_scalar(mask[:, :], c["inherit"][:, bass.ds(n * K, 4 * K)], 0, None, ALU.add))
                    chain.link(dve.tensor_scalar(picked[:, :, :], c["pick"][:, :, bass.ds(n * KP, 4 * KP)], 0, None, ALU.add))
                if new_chunk:
                    dve.wait_ge(sg.xlr_ready, at * 4 + 4)
                    dve.sem_inc(sg.dve_passed, 1)
                for k in range(K):
                    if new_chunk:
                        inherit_xr(v, k)
                    if old_chunk:
                        if k == 0 and (not isinstance(m, int) or m >= 2):
                            dve.wait_ge(sg.scattered, (m + (DONE - 1)) * (16 * KP))
                        state(v, k)
                if old_chunk:
                    chain.mark(dve.tensor_scalar(sidx[q][:, :], c["pair_idx"][:, bass.ds(m * KP, KP)], 0.0, None, ALU.add))
                place_last(v)
                if new_chunk:
                    chain.after(done["xr"])
                    summed = chain.mark(dve.tensor_tensor(mixed[:, :, :], xlr[s][:, :, 0:D], xlr[s][:, :, D:2 * D], ALU.add))
                take_first(v)
                if new_chunk:
                    chain.after(summed)
                    leaky = chain.mark(dve.scalar_tensor_tensor(mixed[:, :, :], mixed[:, :, :], SLOPE, mixed[:, :, :],
                                                                ALU.mult, ALU.max))
                take_kept(v, 0)
                if new_chunk:
                    chain.after(leaky)
                    weighted = chain.mark(dve.tensor_tensor(mixed[:, :, :], mixed[:, :, :],
                                                            att_rows.unsqueeze(1).broadcast_to([P, K, D]), ALU.mult))
                pair_up(v, 0, 1)
                if new_chunk:
                    chain.after(weighted)
                    scored = chain.mark(dve.tensor_reduce(score[:, :], mixed[:, :, :], AX.X, ALU.add))
                take_kept(v, 1)
                if new_chunk:
                    if not isinstance(n, int) or n >= 1:
                        dve.wait_ge(sg.share_ready, at)
                    chain.after(scored)
                    top = chain.mark(dve.tensor_tensor_scan(run_max[:, new], c["pen"][:, now], score[:, :],
                                                            run_max[:, bass.ds(n * K, 1)], ALU.add, ALU.max))
                take_kept(v, 2)
                if new_chunk:
                    chain.after(top)
                    chain.mark(dve.tensor_tensor(drop[:, K:2 * K], score[:, :], run_max[:, new], ALU.subtract))
                    sunk = chain.mark(dve.tensor_tensor(tmp[:, :], run_max[:, now], c["pen"][:, now], ALU.add))
                take_kept(v, 3)
                if new_chunk:
                    chain.after(sunk)
                    dve.tensor_tensor(drop[:, 0:K], tmp[:, :], run_max[:, new], ALU.subtract).then_inc(sg.drop_ready, 1)
                pair_up(v, 1, KP)
                if new_chunk:
                    dve.wait_ge(sg.grown_ready, at + 1)
                    fresh = chain.mark(dve.tensor_tensor(grown[:, K:2 * K], grown[:, K:2 * K], c["mult"][:, now], ALU.mult))
                    if not isinstance(n, int) or n < CHUNKS // 4 * 4:
                        dve.wait_ge(sg.gathered[s], (v.turn(0, 2) + (TURNS + 1)) * (16 * K))
                        dve.tensor_scalar(gidx[v.slot(0, 4)][:, :], c["gather_idx"][:, bass.ds((n + 4) * K, K)], 0.0, None,
                                          ALU.add).then_inc(sg.idx_staged, 1)
                    chain.after(fresh)
                    total = chain.mark(dve.tensor_tensor_scan(run_sum[:, new], grown[:, 0:K], grown[:, K:2 * K],
                                                              run_sum[:, bass.ds(n * K, 1)], ALU.mult, ALU.add))
                    chain.after(total)
                    inverse = chain.mark(dve.reciprocal(inv_sum[:, :], run_sum[:, new]))
                    carried = chain.mark(dve.tensor_tensor(tmp[:, :], grown[:, 0:K], run_sum[:, now], ALU.mult))
                    chain.after(inverse)
                    dve.tensor_tensor(new_share[:, :], grown[:, K:2 * K], inv_sum[:, :], ALU.mult).then_inc(sg.share_ready, 1)
                    chain.after(carried)
                    done["old_share"] = chain.mark(dve.tensor_tensor(old_share[s][:, :], tmp[:, :], inv_sum[:, :], ALU.mult))

            def settle():
                chain.settle()
                chain.restart()
                done.clear()
            pipeline(dve, CHUNKS, 4, 1, 4, step, settle)
            dve.wait_ge(sg.outs_ready, DONE + CHUNKS)

    with nc.Block() as block:
        @block.gpsimd
        def _(pool):
            gather(pool, fixed[:, :], table_out, c["own_row"][:, 0:1]).then_inc(sg.fix_gathered, 16)
            pool.wait_ge(sg.fix_dve, 5 * l + 5)
            pool.wait_ge(sg.fix_gathered, 16 * (l + 1))
            scatter(pool, table_out, c["fix_idx"][:, 0:1], fixed[:, :]).then_inc(sg.fix_scattered, 16)
            pool.wait_ge(sg.fix_scattered, 16 * (2 * l + 2))

        @block.vector
        def _(dve):
            chain = Chain(dve, sg.chain)
            own_max, own_sum, top, own_share, total, inv = (st[:, j:j + 1] for j in range(6))
            last_max, last_sum = c["run_max"][:, COLS:COLS + 1], c["run_sum"][:, COLS:COLS + 1]
            chain.mark(dve.tensor_scalar(diag[:, 0:P], c["ident"][:, :], last_max, None, ALU.mult))
            chain.settle()
            dve.tensor_scalar(diag[:, P:2 * P], c["ident"][:, :], last_sum, None, ALU.mult).then_inc(sg.fix_dve, 1)
            chain.link(dve.tensor_tensor(c["wide"][:, :], c["run_max"][:, 1:COLS + 1], c["head"][:, :], ALU.mult))
            chain.link(dve.tensor_reduce(own_max, c["wide"][:, :], AX.X, ALU.add))
            chain.link(dve.tensor_tensor(c["wide"][:, :], c["run_sum"][:, 1:COLS + 1], c["head"][:, :], ALU.mult))
            chain.link(dve.tensor_reduce(own_sum, c["wide"][:, :], AX.X, ALU.add))
            dve.wait_ge(sg.fix_pe, 3 * l + 1)
            chain.link(dve.tensor_tensor(share[:, 0:P], ps_b[1][:, 0:P], c["take_pen"][:, :], ALU.add))
            chain.link(dve.tensor_reduce(top, share[:, 0:P], AX.X, ALU.max))
            chain.link(dve.tensor_tensor(top, top, own_max, ALU.max))
            chain.mark(dve.tensor_tensor(share[:, P:P + 1], own_max, top, ALU.subtract))
            chain.settle()
            dve.tensor_scalar(share[:, 0:P], share[:, 0:P], top, None, ALU.subtract).then_inc(sg.fix_dve, 1)
            dve.wait_ge(sg.fix_act, l + 1)
            chain.mark(dve.tensor_tensor(share[:, 0:P], share[:, 0:P], ps_b[1][:, P:2 * P], ALU.mult))
            chain.link(dve.tensor_tensor(own_share, share[:, P:P + 1], own_sum, ALU.mult))
            chain.link(dve.tensor_reduce(total, share[:, 0:P], AX.X, ALU.add))
            chain.link(dve.tensor_tensor(total, total, own_share, ALU.add))
            chain.link(dve.tensor_scalar(total, total, 1.0 / BIG, None, ALU.max))
            chain.link(dve.reciprocal(inv, total))
            chain.link(dve.tensor_tensor(own_share, own_share, inv, ALU.mult))
            dve.tensor_scalar(share[:, 0:P], share[:, 0:P], inv, None, ALU.mult).then_inc(sg.fix_dve, 1)
            dve.wait_ge(sg.fix_pe, 3 * l + 2)
            dve.tensor_copy(share_t[:, :], ps_b[0][:, 0:P]).then_inc(sg.fix_dve, 1)
            dve.wait_ge(sg.fix_pe, 3 * l + 3)
            dve.wait_ge(sg.fix_gathered, 16 * (l + 1))
            dve.scalar_tensor_tensor(fixed[:, :], fixed[:, :], own_share, ps_b[1][:, 2 * P:3 * P],
                                     ALU.mult, ALU.add).then_inc(sg.fix_dve, 1)
            chain.restart()

        @block.scalar
        def _(act):
            act.wait_ge(sg.fix_dve, 5 * l + 2)
            act.activation(share[:, :], share[:, :], ACT.Exp).then_inc(sg.fix_act, 1)

        @block.tensor
        def _(pe):
            pe.wait_ge(sg.fix_dve, 5 * l + 1)
            pe.matmul(ps_b[1][:, 0:2 * P], c["ones"][:, :], diag[:, :], start=True, stop=True).then_inc(sg.fix_pe, 1)
            pe.wait_ge(sg.fix_dve, 5 * l + 3)
            pe.transpose(ps_b[0][:, 0:P], share[:, 0:P], c["ident"][:, :]).then_inc(sg.fix_pe, 1)
            pe.wait_ge(sg.fix_dve, 5 * l + 4)
            pe.matmul(ps_b[1][:, 2 * P:3 * P], share_t[:, :], carry[:, :], start=True, stop=True).then_inc(sg.fix_pe, 1)


class Step:

    def __init__(self, i, u, unroll, total):
        self.i, self.u, self.unroll, self.total = i, u, unroll, total

    def chunk(self, lag):
        return self.i * self.unroll + (self.u - lag)

    def slot(self, lag, ring):
        return (self.u - lag) % ring

    def turn(self, lag, ring):
        return self.i * (self.unroll // ring) + (self.u - lag) // ring

    def live(self, lag):
        n = self.chunk(lag)
        return not isinstance(n, int) or 0 <= n < self.total


def pipeline(eng, total, unroll, lags, ring, step, after=None):
    first = -(-(lags + ring) // unroll)
    last = total // unroll

    def group(i, steps):
        for u in range(steps):
            step(Step(i, u, unroll, total))
        if after:
            after()

    for i in range(first):
        group(i, unroll)
    with eng.Fori(first, last, 1) as i:
        group(i, unroll)
    for v in range(last * unroll, total + lags, unroll):
        group(v // unroll, min(unroll, total + lags - v))


def wait(eng, sem, value):
    if not isinstance(value, int) or value > 0:
        eng.wait_ge(sem, value)


def is_tail(n):
    return isinstance(n, int) and n == NCHUNKS


def node_cols(n):
    return 1 if is_tail(n) else KN


def node_rows(table, n, store=False):
    if is_tail(n):
        lo = N - TAIL if store else N - P
        return table[lo:N, :].rearrange("(p j) d -> p j d", j=1)
    return table[0:P * NJ, :].rearrange("(p j) d -> p j d", p=P)[:, bass.ds(n * KN, KN), :]


def store_lo(n):
    return P - TAIL if is_tail(n) else 0


class RowNorm:

    def __init__(self, sb, sem, rows, ring):
        self.rows, self.ring = rows, ring
        self.neg_mean = [sb(f"neg_mean{r}", [P, KN]) for r in range(ring)]
        self.sq_sum = [sb(f"sq_sum{r}", [P, KN]) for r in range(ring)]
        self.var = [sb(f"var{r}", [P, KN]) for r in range(ring)]
        self.rstd = [sb(f"rstd{r}", [P, KN]) for r in range(ring)]
        self.sq = sb("sq", [P, ring, KN, D])
        self.half = sb("half", [P, KN])
        self.mean_ready = sem("mean_ready")
        self.sq_ready = sem("sq_ready")
        self.var_ready = sem("var_ready")
        self.rstd_ready = sem("rstd_ready")
        self.y_ready = sem("y_ready")

    def sums(self, dve, chain, v):
        n, r, k = v.chunk(0), v.slot(0, self.ring), node_cols(v.chunk(0))
        chain.link(dve.tensor_reduce(self.neg_mean[r][:, 0:k], self.rows[r][:, 0:k, :], AX.X, ALU.add))
        dve.tensor_scalar(self.neg_mean[r][:, 0:k], self.neg_mean[r][:, 0:k], -1.0 / D, None,
                          ALU.mult).then_inc(self.mean_ready, 1)

    def squares(self, act, v, lag=0):
        n, r, k = v.chunk(lag), v.slot(lag, self.ring), node_cols(v.chunk(lag))
        act.wait_ge(self.mean_ready, n + 1)
        wait(act, self.sq_ready, n - self.ring + 1)
        for j in range(k):
            ins = act.activation(self.sq[:, r, j, :], self.rows[r][:, j, :], ACT.Square,
                                 bias=self.neg_mean[r][:, j:j + 1], accum_out=self.sq_sum[r][:, j:j + 1])
        ins.then_inc(self.sq_ready, 1)

    def variances(self, dve, v):
        n, r, k = v.chunk(2), v.slot(2, self.ring), node_cols(v.chunk(2))
        dve.wait_ge(self.sq_ready, n + 1)
        dve.tensor_scalar(self.var[r][:, 0:k], self.sq_sum[r][:, 0:k], 1.0 / D, EPS,
                          ALU.mult, ALU.add).then_inc(self.var_ready, 1)

    def rstds(self, pool, v):
        n, r, k = v.chunk(3), v.slot(3, self.ring), node_cols(v.chunk(3))
        pool.wait_ge(self.var_ready, n + 1)
        pool.tensor_tensor(self.rstd[r][:, 0:k], self.var[r][:, 0:k], self.half[:, 0:k],
                           ALU.pow).then_inc(self.rstd_ready, 1)

    def normalise(self, dve, chain, v):
        n, r, k = v.chunk(3), v.slot(3, self.ring), node_cols(v.chunk(3))
        dve.wait_ge(self.rstd_ready, n + 1)
        for j in range(k):
            ins = dve.tensor_scalar(self.rows[r][:, j, :], self.rows[r][:, j, :], self.neg_mean[r][:, j:j + 1],
                                    self.rstd[r][:, j:j + 1], ALU.add, ALU.mult)
            if j < k - 1:
                chain.mark(ins)
        chain.settle()
        ins.then_inc(self.y_ready, 1)


def node_pass_hidden(nc, scope, x, gat_out, normed, hidden, c):
    def sb(name, shape, dt=F32):
        return scope.enter_context(nc.sbuf_tensor(f"nh_{name}", shape, dt))

    def ps(name):
        return scope.enter_context(nc.psum_tensor(f"nh_{name}", [P, 512], F32))

    def sem(name):
        return scope.enter_context(nc.semaphore(f"nh_{name}"))

    R = 8
    L = R
    total = NCHUNKS + 1
    x_in = [sb(f"x_in{r}", [P, KN, D]) for r in range(L)]
    g_in = [sb(f"g_in{r}", [P, KN, D]) for r in range(L)]
    y = [sb(f"y{r}", [P, KN, D]) for r in range(R)]
    h = [sb(f"h{r}", [P, KN, D]) for r in range(R)]
    y_t = [sb(f"y_t{s}", [P, KN * P]) for s in range(2)]
    h_t = [sb(f"h_t{s}", [P, KN * P]) for s in range(2)]
    ps_y, ps_h, ps_b = ([ps(f"{name}{s}") for s in range(2)] for name in ("ps_y", "ps_h", "ps_b"))

    norm = RowNorm(sb, sem, y, R)
    loaded = [sem(f"loaded{r}") for r in range(L)]
    biased = sem("biased")
    added = sem("added")
    turned = sem("turned")
    y_t_ready = sem("y_t_ready")
    projected = sem("projected")
    h_t_ready = sem("h_t_ready")
    back = sem("back")
    h_ready = sem("h_ready")
    stored_y = [sem(f"stored_y{r}") for r in range(R)]
    stored_h = [sem(f"stored_h{r}") for r in range(R)]
    chain_sem = sem("chain")

    with nc.Block() as block:
        @block.sync
        def _(sp):
            def step(v):
                if v.live(0):
                    n, r, k = v.chunk(0), v.slot(0, L), node_cols(v.chunk(0))
                    wait(sp, added, n - L + 1)
                    sp.dma_start(x_in[r][:, 0:k, :], node_rows(x, n)).then_inc(loaded[r], 16)
                    sp.dma_start(g_in[r][:, 0:k, :], node_rows(gat_out, n)).then_inc(loaded[r], 16)
                if v.live(8):
                    n, r, k = v.chunk(8), v.slot(8, R), node_cols(v.chunk(8))
                    sp.wait_ge(norm.y_ready, n + 1)
                    sp.dma_start(node_rows(normed, n, True), y[r][store_lo(n):P, 0:k, :]).then_inc(stored_y[r], 16)
                if v.live(10):
                    n, r, k = v.chunk(10), v.slot(10, R), node_cols(v.chunk(10))
                    sp.wait_ge(h_ready, n + 1)
                    sp.dma_start(node_rows(hidden, n, True), h[r][store_lo(n):P, 0:k, :]).then_inc(stored_h[r], 16)
            pipeline(sp, total, L, 10, L, step)
            for r in range(R):
                turns = len(range(r, total, R))
                sp.wait_ge(stored_y[r], 16 * turns)
                sp.wait_ge(stored_h[r], 16 * turns)

        @block.gpsimd
        def _(pool):
            pool.memset(norm.half[:, :], -0.5).then_inc(biased, 1)
            pool.wait_ge(biased, 1)

            def step(v):
                if v.live(0):
                    n, r, k = v.chunk(0), v.slot(0, L), node_cols(v.chunk(0))
                    pool.wait_ge(loaded[r], (v.turn(0, L) + 1) * 32)
                    pool.tensor_tensor(g_in[r][:, 0:k, :], g_in[r][:, 0:k, :],
                                       c["b2_rows"][:, :].unsqueeze(1).broadcast_to([P, k, D]),
                                       ALU.add).then_inc(biased, 1)
                if v.live(3):
                    norm.rstds(pool, v)
            pipeline(pool, total, L, 3, L, step)

        @block.vector
        def _(dve):
            chain = Chain(dve, chain_sem)

            def step(v):
                if v.live(2):
                    norm.variances(dve, v)
                if v.live(0):
                    n, r, q, k = v.chunk(0), v.slot(0, R), v.slot(0, L), node_cols(v.chunk(0))
                    dve.wait_ge(biased, n + 2)
                    wait(dve, stored_y[r], v.turn(0, R) * 16)
                    wait(dve, turned, n - R + 1)
                    dve.tensor_tensor(y[r][:, 0:k, :], x_in[q][:, 0:k, :], g_in[q][:, 0:k, :], ALU.add).then_inc(added, 1)
                    dve.wait_ge(added, n + 1)
                    norm.sums(dve, chain, v)
                if v.live(3):
                    norm.normalise(dve, chain, v)
            pipeline(dve, total, L, 3, L, step, chain.restart)

        @block.tensor
        def _(pe):
            def step(v):
                if v.live(4):
                    n, r, s, k = v.chunk(4), v.slot(4, R), v.slot(4, 2), node_cols(v.chunk(4))
                    pe.wait_ge(norm.y_ready, n + 1)
                    wait(pe, y_t_ready, n - 1)
                    for j in range(k):
                        ins = pe.transpose(ps_y[s][:, j * P:(j + 1) * P], y[r][:, j, :], c["ident"][:, :])
                    ins.then_inc(turned, 1)
                if v.live(5):
                    n, s, k = v.chunk(5), v.slot(5, 2), node_cols(v.chunk(5))
                    pe.wait_ge(y_t_ready, n + 1)
                    wait(pe, h_t_ready, n - 1)
                    pe.matmul(ps_h[s][:, 0:k * P], c["w1t"][:, :], y_t[s][:, 0:k * P], start=True, stop=True).then_inc(projected, 1)
                if v.live(6):
                    n, s, k = v.chunk(6), v.slot(6, 2), node_cols(v.chunk(6))
                    pe.wait_ge(h_t_ready, n + 1)
                    wait(pe, h_ready, n - 1)
                    for j in range(k):
                        ins = pe.transpose(ps_b[s][:, j * P:(j + 1) * P], h_t[s][:, j * P:(j + 1) * P], c["ident"][:, :])
                    ins.then_inc(back, 1)
            pipeline(pe, total, L, 6, L, step)

        @block.scalar
        def _(act):
            def step(v):
                if v.live(0):
                    norm.squares(act, v)
                if v.live(4):
                    n, s, k = v.chunk(4), v.slot(4, 2), node_cols(v.chunk(4))
                    act.wait_ge(turned, n + 1)
                    wait(act, projected, n - 1)
                    act.activation(y_t[s][:, 0:k * P], ps_y[s][:, 0:k * P], ACT.Copy).then_inc(y_t_ready, 1)
                if v.live(5):
                    n, s, k = v.chunk(5), v.slot(5, 2), node_cols(v.chunk(5))
                    act.wait_ge(projected, n + 1)
                    wait(act, back, n - 1)
                    act.activation(h_t[s][:, 0:k * P], ps_h[s][:, 0:k * P], ACT.Gelu, bias=c["b1_col"][:, 0:1]).then_inc(h_t_ready, 1)
                if v.live(6):
                    n, r, s, k = v.chunk(6), v.slot(6, R), v.slot(6, 2), node_cols(v.chunk(6))
                    act.wait_ge(back, n + 1)
                    wait(act, stored_h[r], v.turn(6, R) * 16)
                    act.activation(h[r][:, 0:k, :], ps_b[s][:, 0:k * P].rearrange("p (a b) -> p a b", a=k),
                                   ACT.Copy).then_inc(h_ready, 1)
            pipeline(act, total, L, 6, L, step)


def mixing_pass(nc, scope, hidden, agg_table, c):
    def sb(name, shape, dt=F32):
        return scope.enter_context(nc.sbuf_tensor(f"mx_{name}", shape, dt))

    def ps(name):
        return scope.enter_context(nc.psum_tensor(f"mx_{name}", [P, 512], F32))

    def sem(name):
        return scope.enter_context(nc.semaphore(f"mx_{name}"))

    R = 4
    K = KM
    MD = MIX * D
    LATE = 5
    rows = [sb(f"rows{r}", [P, K, D]) for r in range(R)]
    gidx = [sb(f"gidx{r}", [P, K], I32) for r in range(R)]
    sidx = [sb(f"sidx{r}", [P, K], I32) for r in range(R)]
    rows_t = [sb(f"rows_t{s}", [P, K * P]) for s in range(2)]
    up_t = [sb(f"up_t{s}", [P, K * P]) for s in range(2)]
    mix = [sb(f"mix{s}", [P, K, MIX]) for s in range(2)]
    prod = [sb(f"prod{s}", [P, K, MD]) for s in range(2)]
    agg = [sb(f"agg{s}", [P, K, MD]) for s in range(2)]
    act_agg = [sb(f"act_agg{s}", [P, K, MD]) for s in range(2)]
    head_diag = [sb(f"head_diag{s}", [P, K, P]) for s in range(2)]
    mix_sum = sb("mix_sum", [P, MIX, COLS + 1])
    mix_mean = [sb(f"mix_mean{s}", [P, K, MIX]) for s in range(2)]
    outs = [sb(f"outs{r}", [P, K, D]) for r in range(R)]
    states = sb("states", [P, MIX + 1])
    own_small = sb("own_small", [P, MIX + 1])
    total = sb("total", [P, MD])
    fixed = sb("fixed", [P, D])
    ps_t = [ps(f"ps_t{s}") for s in range(2)]
    ps_u = [ps(f"ps_u{s}") for s in range(2)]
    ps_m = [ps(f"ps_m{s}") for s in range(2)]
    ps_own = ps("ps_own")
    ps_b = ps("ps_b")

    idx_staged = sem("idx_staged")
    gathered = [sem(f"gathered{r}") for r in range(R)]
    turned = sem("turned")
    rows_t_ready = sem("rows_t_ready")
    up_done = sem("up_done")
    up_ready = sem("up_ready")
    mix_done = sem("mix_done")
    mix_ready = sem("mix_ready")
    prod_ready = sem("prod_ready")
    agg_ready = sem("agg_ready")
    diag_ready = sem("diag_ready")
    own_added = sem("own_added")
    gelu_ready = sem("gelu_ready")
    mixed = sem("mixed")
    outs_ready = sem("outs_ready")
    scattered = [sem(f"scattered{r}") for r in range(R)]
    chain_sem = sem("chain")
    pool_passed = sem("pool_passed")
    fix_pe, fix_act, fix_dve, fix_scattered = sem("fix_pe"), sem("fix_act"), sem("fix_dve"), sem("fix_scattered")

    def heads(ap):
        return ap.rearrange("p (m d) -> p m d", m=MIX)

    with nc.Block() as block:
        @block.gpsimd
        def _(pool):
            def step(v):
                if v.live(0):
                    n, r = v.chunk(0), v.slot(0, R)
                    wait(pool, prod_ready, (n - (R - 1)) * K)
                    pool.wait_ge(idx_staged, n + 1)
                    pool.sem_inc(pool_passed, 1)
                    for k in range(K):
                        gather(pool, rows[r][:, k, :], hidden, gidx[r][:, k:k + 1]).then_inc(gathered[r], 16)
                if v.live(LATE):
                    n, r = v.chunk(LATE), v.slot(LATE, R)
                    pool.wait_ge(outs_ready, n + 1)
                    pool.sem_inc(pool_passed, 1)
                    for k in range(K):
                        scatter(pool, agg_table, sidx[r][:, k:k + 1], outs[r][:, k, :]).then_inc(scattered[r], 16)
            pipeline(pool, MCHUNKS, R, LATE, R, step)
            for r in range(R):
                pool.wait_ge(scattered[r], 16 * K * MCHUNKS // R)

        @block.tensor
        def _(pe):
            def step(v):
                if v.live(0):
                    n, r, s = v.chunk(0), v.slot(0, R), v.slot(0, 2)
                    pe.wait_ge(gathered[r], (v.turn(0, R) + 1) * (16 * K))
                    wait(pe, rows_t_ready, n - 1)
                    for k in range(K):
                        ins = pe.transpose(ps_t[s][:, k * P:(k + 1) * P], rows[r][:, k, :], c["ident"][:, :])
                    ins.then_inc(turned, 1)
                if v.live(1):
                    n, s = v.chunk(1), v.slot(1, 2)
                    pe.wait_ge(rows_t_ready, n + 1)
                    wait(pe, up_ready, n - 1)
                    pe.matmul(ps_u[s][:, :], c["wat"][:, :], rows_t[s][:, :], start=True, stop=True).then_inc(up_done, 1)
                if v.live(2):
                    n, s = v.chunk(2), v.slot(2, 2)
                    pe.wait_ge(up_ready, n + 1)
                    wait(pe, mix_ready, n - 1)
                    for k in range(K):
                        ins = pe.matmul(ps_m[s][:, k * MIX:(k + 1) * MIX], up_t[s][:, k * P:(k + 1) * P],
                                        c["wbt"][:, :], start=True, stop=True)
                    ins.then_inc(mix_done, 1)
                if v.live(3):
                    n, s = v.chunk(3), v.slot(3, 2)
                    pe.wait_ge(diag_ready, n + 1)
                    pe.wait_ge(agg_ready, (n + 1) * K)
                    for k in range(K):
                        ins = pe.matmul(ps_own[:, :], head_diag[s][:, k, :], agg[s][:, k, :],
                                        start=isinstance(n, int) and n == 0 and k == 0, stop=False)
                    ins.then_inc(own_added, 1)
            pipeline(pe, MCHUNKS, R, 3, R, step)

        @block.scalar
        def _(act):
            def step(v):
                if v.live(0):
                    n, s = v.chunk(0), v.slot(0, 2)
                    act.wait_ge(turned, n + 1)
                    wait(act, up_done, n - 1)
                    act.activation(rows_t[s][:, :], ps_t[s][:, :], ACT.Copy).then_inc(rows_t_ready, 1)
                if v.live(1):
                    n, s = v.chunk(1), v.slot(1, 2)
                    act.wait_ge(up_done, n + 1)
                    wait(act, mix_done, n - 1)
                    act.activation(up_t[s][:, :], ps_u[s][:, :], ACT.Gelu).then_inc(up_ready, 1)
                if v.live(2):
                    n, s, r = v.chunk(2), v.slot(2, 2), v.slot(2, R)
                    act.wait_ge(mix_done, n + 1)
                    wait(act, mixed, n - 1)
                    wait(act, prod_ready, (n - 1) * K)
                    act.activation(mix[s][:, :, :], ps_m[s][:, 0:K * MIX].rearrange("p (k m) -> p k m", m=MIX),
                                   ACT.Copy).then_inc(mix_ready, 1)
                if v.live(3):
                    n, s = v.chunk(3), v.slot(3, 2)
                    wait(act, outs_ready, n - 1)
                    for k in range(K):
                        act.wait_ge(agg_ready, n * K + (k + 1))
                        act.activation(act_agg[s][:, k, :], agg[s][:, k, :], ACT.Gelu).then_inc(gelu_ready, 1)
                if v.live(2):
                    n, s, r = v.chunk(2), v.slot(2, 2), v.slot(2, R)
                    act.wait_ge(mix_ready, n + 1)
                    for k in range(K):
                        wait(act, agg_ready, (n - 2) * K + (k + 1))
                        for m in range(MIX):
                            ins = act.activation(prod[s][:, k, m * D:(m + 1) * D], rows[r][:, k, :], ACT.Copy,
                                                 scale=mix[s][:, k, m:m + 1])
                        ins.then_inc(prod_ready, 1)
            pipeline(act, MCHUNKS, R, 3, R, step)

        @block.vector
        def _(dve):
            chain = Chain(dve, chain_sem)
            chain.mark(dve.memset(mix_sum[:, :, 0:1], 0.0))
            chain.mark(dve.memset(agg[1][:, K - 1, :], 0.0))
            for n in range(R):
                dve.tensor_copy(gidx[n][:, :], c["gather_idx"][:, n * K:(n + 1) * K]).then_inc(idx_staged, 1)
            chain.settle()
            chain.restart()

            def prepare(v):
                n, s, r = v.chunk(2), v.slot(2, 2), v.slot(2, R)
                c0 = n * K
                now, new = bass.ds(c0, K), bass.ds(c0 + 1, K)
                dve.wait_ge(gathered[r], (v.turn(2, R) + 1) * (16 * K))
                dve.tensor_scalar(gidx[r][:, :], c["gather_idx"][:, bass.ds(c0 + R * K, K)], 0.0, None,
                                  ALU.add).then_inc(idx_staged, 1)
                wait(dve, own_added, n - 1)
                dve.tensor_tensor(head_diag[s][:, :, :], c["ident"][:, :].unsqueeze(1).broadcast_to([P, K, P]),
                                  c["head"][:, now].unsqueeze(2).broadcast_to([P, K, P]), ALU.mult).then_inc(diag_ready, 1)
                dve.wait_ge(mix_ready, n + 1)
                for m in range(MIX):
                    ins = dve.tensor_tensor_scan(mix_sum[:, m, new], c["cont"][:, now], mix[s][:, :, m],
                                                 mix_sum[:, m, bass.ds(c0, 1)], ALU.mult, ALU.add)
                    if m < MIX - 1:
                        chain.mark(ins)
                chain.settle()
                ins.then_inc(mixed, 1)

            def average_mix(v):
                n, s = v.chunk(2), v.slot(2, 2)
                now, new = bass.ds(n * K, K), bass.ds(n * K + 1, K)
                dve.wait_ge(mixed, n + 1)
                chain.mark(dve.tensor_tensor(mix_mean[s][:, :, :], mix_sum[:, :, new].rearrange("p m k -> p k m"),
                                             c["inv_count"][:, now].unsqueeze(2).broadcast_to([P, K, MIX]), ALU.mult))

            def accumulate(v, k):
                n, s = v.chunk(2), v.slot(2, 2)
                prev = agg[1 - s][:, K - 1, :] if k == 0 else agg[s][:, k - 1, :]
                dve.wait_ge(prod_ready, n * K + (k + 1))
                if not (isinstance(n, int) and n == 0 and k == 0):
                    dve.wait_ge(agg_ready, n * K + k)
                dve.scalar_tensor_tensor(agg[s][:, k, :], prev, c["cont"][:, bass.ds(n * K + k, 1)], prod[s][:, k, :],
                                         ALU.mult, ALU.add).then_inc(agg_ready, 1)

            def contract(v, m):
                n, s, r = v.chunk(3), v.slot(3, 2), v.slot(3, R)
                if m == 0:
                    wait(dve, scattered[r], v.turn(3, R) * (16 * K))
                    dve.wait_ge(gelu_ready, (n + 1) * K)
                    chain.mark(dve.tensor_scalar(sidx[r][:, :], c["scatter_idx"][:, bass.ds(n * K, K)], 0.0, None, ALU.add))
                chain.settle()
                for k in range(K):
                    if m == 0:
                        ins = dve.tensor_scalar(outs[r][:, k, :], act_agg[s][:, k, 0:D], mix_mean[s][:, k, 0:1],
                                                None, ALU.mult)
                    else:
                        ins = dve.scalar_tensor_tensor(outs[r][:, k, :], act_agg[s][:, k, m * D:(m + 1) * D],
                                                       mix_mean[s][:, k, m:m + 1], outs[r][:, k, :], ALU.mult, ALU.add)
                    if m == MIX - 1 and k == K - 1:
                        chain.settle()
                        ins.then_inc(outs_ready, 1)
                    else:
                        chain.mark(ins)

            def step(v):
                if v.live(2):
                    prepare(v)
                for j in range(MIX):
                    if v.live(2):
                        accumulate(v, j)
                        if j == 0:
                            average_mix(v)
                    if v.live(3):
                        contract(v, j)
            pipeline(dve, MCHUNKS, R, 3, R, step, chain.restart)

    with nc.Block() as block:
        @block.gpsimd
        def _(pool):
            pool.wait_ge(fix_dve, 3)
            scatter(pool, agg_table, c["fix_idx"][:, 0:1], fixed[:, :]).then_inc(fix_scattered, 16)
            pool.wait_ge(fix_scattered, 16)

        @block.tensor
        def _(pe):
            pe.matmul(ps_own[:, :], c["take"][:, :], agg[1][:, K - 1, :], start=False, stop=True).then_inc(fix_pe, 1)
            pe.wait_ge(fix_dve, 1)
            pe.matmul(ps_b[:, 0:MIX + 1], c["take"][:, :], states[:, :], start=True, stop=True).then_inc(fix_pe, 1)

        @block.scalar
        def _(act):
            act.wait_ge(fix_dve, 2)
            act.activation(total[:, :], total[:, :], ACT.Gelu).then_inc(fix_act, 1)

        @block.vector
        def _(dve):
            chain = Chain(dve, chain_sem)
            chain.link(dve.tensor_copy(states[:, 0:MIX], mix_sum[:, :, COLS]))
            dve.tensor_copy(states[:, MIX:MIX + 1], c["count"][:, COLS:COLS + 1]).then_inc(fix_dve, 1)
            dve.wait_ge(fix_pe, 1)
            dve.tensor_copy(total[:, :], ps_own[:, :]).then_inc(fix_dve, 1)
            for m in range(MIX + 1):
                series = mix_sum[:, m, 1:COLS + 1] if m < MIX else c["count"][:, 1:COLS + 1]
                chain.link(dve.tensor_tensor(c["wide"][:, :], series, c["head"][:, :], ALU.mult))
                chain.link(dve.tensor_reduce(own_small[:, m:m + 1], c["wide"][:, :], AX.X, ALU.add))
            dve.wait_ge(fix_pe, 2)
            chain.link(dve.tensor_tensor(own_small[:, :], own_small[:, :], ps_b[:, 0:MIX + 1], ALU.add))
            chain.link(dve.tensor_scalar(own_small[:, MIX:MIX + 1], own_small[:, MIX:MIX + 1], 1.0, None, ALU.max))
            dve.wait_ge(fix_dve, 2)
            chain.link(dve.reciprocal(states[:, 0:1], own_small[:, MIX:MIX + 1]))
            chain.link(dve.tensor_scalar(own_small[:, 0:MIX], own_small[:, 0:MIX], states[:, 0:1], None, ALU.mult))
            dve.wait_ge(fix_act, 1)
            chain.link(dve.tensor_tensor(heads(total[:, :]), heads(total[:, :]),
                                         own_small[:, 0:MIX].unsqueeze(2).broadcast_to([P, MIX, D]), ALU.mult))
            dve.tensor_reduce(fixed[:, :], total[:, :].rearrange("p (m d) -> p d m", m=MIX), AX.X, ALU.add).then_inc(fix_dve, 1)


def node_pass_out(nc, scope, agg_table, hidden, normed, out, c):
    def sb(name, shape, dt=F32):
        return scope.enter_context(nc.sbuf_tensor(f"no_{name}", shape, dt))

    def ps(name):
        return scope.enter_context(nc.psum_tensor(f"no_{name}", [P, 512], F32))

    def sem(name):
        return scope.enter_context(nc.semaphore(f"no_{name}"))

    R = 8
    L = R
    total = NCHUNKS + 1
    parts = [[sb(f"parts{a}{r}", [P, KN, D]) for r in range(L)] for a in range(2)]
    x_in = [sb(f"x_in{r}", [P, KN, D]) for r in range(L)]
    feat_t = [[sb(f"feat_t{a}{s}", [P, KN * P]) for s in range(2)] for a in range(2)]
    y = [sb(f"y{r}", [P, KN, D]) for r in range(R)]
    ps_f = [[ps(f"ps_f{a}{s}") for s in range(2)] for a in range(2)]
    ps_o = [ps(f"ps_o{s}") for s in range(2)]

    norm = RowNorm(sb, sem, y, R)
    loaded = [sem(f"loaded{r}") for r in range(L)]
    turned = sem("turned")
    feat_ready = sem("feat_ready")
    projected = sem("projected")
    biased = sem("biased")
    added = sem("added")
    stored = [sem(f"stored{r}") for r in range(R)]
    chain_sem = sem("chain")

    with nc.Block() as block:
        @block.sync
        def _(sp):
            def step(v):
                if v.live(0):
                    n, r, k = v.chunk(0), v.slot(0, L), node_cols(v.chunk(0))
                    wait(sp, added, n - L + 1)
                    for tile, table in ((parts[0][r], agg_table), (parts[1][r], hidden), (x_in[r], normed)):
                        sp.dma_start(tile[:, 0:k, :], node_rows(table, n)).then_inc(loaded[r], 16)
                if v.live(8):
                    n, r, k = v.chunk(8), v.slot(8, R), node_cols(v.chunk(8))
                    sp.wait_ge(norm.y_ready, n + 1)
                    sp.dma_start(node_rows(out, n, True), y[r][store_lo(n):P, 0:k, :]).then_inc(stored[r], 16)
            pipeline(sp, total, L, 8, L, step)
            for r in range(R):
                sp.wait_ge(stored[r], 16 * len(range(r, total, R)))

        @block.gpsimd
        def _(pool):
            pool.memset(norm.half[:, :], -0.5).then_inc(biased, 1)
            pool.wait_ge(biased, 1)

            def step(v):
                if v.live(0):
                    n, r, k = v.chunk(0), v.slot(0, L), node_cols(v.chunk(0))
                    pool.wait_ge(loaded[r], (v.turn(0, L) + 1) * 48)
                    pool.tensor_tensor(x_in[r][:, 0:k, :], x_in[r][:, 0:k, :],
                                       c["ob_rows"][:, :].unsqueeze(1).broadcast_to([P, k, D]),
                                       ALU.add).then_inc(biased, 1)
                if v.live(3):
                    norm.rstds(pool, v)
            pipeline(pool, total, L, 3, L, step)

        @block.tensor
        def _(pe):
            def step(v):
                if v.live(0):
                    n, r, s, k = v.chunk(0), v.slot(0, L), v.slot(0, 2), node_cols(v.chunk(0))
                    pe.wait_ge(loaded[r], (v.turn(0, L) + 1) * 48)
                    for a in range(2):
                        wait(pe, feat_ready, n * 2 - 3 + a)
                        for j in range(k):
                            ins = pe.transpose(ps_f[a][s][:, j * P:(j + 1) * P], parts[a][r][:, j, :], c["ident"][:, :])
                        ins.then_inc(turned, 1)
                if v.live(1):
                    n, s, k = v.chunk(1), v.slot(1, 2), node_cols(v.chunk(1))
                    pe.wait_ge(feat_ready, n * 2 + 2)
                    wait(pe, added, n - 1)
                    for j in range(k):
                        for a in range(2):
                            ins = pe.matmul(ps_o[s][:, j * P:(j + 1) * P], feat_t[a][s][:, j * P:(j + 1) * P],
                                            c["w2t"][:, a, :], start=(a == 0), stop=(a == 1))
                    ins.then_inc(projected, 1)
            pipeline(pe, total, L, 1, L, step)

        @block.scalar
        def _(act):
            def step(v):
                if v.live(0):
                    n, s, k = v.chunk(0), v.slot(0, 2), node_cols(v.chunk(0))
                    for a in range(2):
                        act.wait_ge(turned, n * 2 + 1 + a)
                        wait(act, projected, n - 1)
                        act.activation(feat_t[a][s][:, 0:k * P], ps_f[a][s][:, 0:k * P], ACT.Gelu).then_inc(feat_ready, 1)
                if v.live(2):
                    norm.squares(act, v, 2)
            pipeline(act, total, L, 2, L, step)

        @block.vector
        def _(dve):
            chain = Chain(dve, chain_sem)

            def step(v):
                if v.live(2):
                    norm.variances(dve, v)
                if v.live(0):
                    n, r, q, s, k = v.chunk(0), v.slot(0, R), v.slot(0, L), v.slot(0, 2), node_cols(v.chunk(0))
                    dve.wait_ge(biased, n + 2)
                    dve.wait_ge(projected, n + 1)
                    wait(dve, stored[r], v.turn(0, R) * 16)
                    dve.tensor_tensor(y[r][:, 0:k, :], ps_o[s][:, 0:k * P].rearrange("p (a b) -> p a b", a=k),
                                      x_in[q][:, 0:k, :], ALU.add).then_inc(added, 1)
                    dve.wait_ge(added, n + 1)
                    norm.sums(dve, chain, v)
                if v.live(3):
                    norm.normalise(dve, chain, v)
            pipeline(dve, total, L, 3, L, step, chain.restart)


_INS = ["x", "src", "dst"] + [f"L0_gnn_{w}{l}" for l in range(3) for w in ("Wl", "Wr", "att", "b")] \
    + [f"L1_gnn_{w}" for w in ("W1", "b1", "WA", "WB", "W2", "b2")]


def kernel(**inputs):
    import numpy as _np
    import concourse.bacc as _bacc
    from concourse import mybir as _mybir
    from concourse.bass_utils import run_bass_kernel_spmd as _run

    nc = _bacc.Bacc("TRN2", target_bir_lowering=False, num_devices=1)
    arrays, args = {}, {}
    for name in _INS:
        a = _np.ascontiguousarray(inputs[name])
        arrays[f"in_{name}"] = a
        args[name] = nc.dram_tensor(f"in_{name}", a.shape, _mybir.dt.from_np(a.dtype), kind="ExternalInput").ap()
    out = nc.dram_tensor("out_0", (N, D), F32, kind="ExternalOutput").ap()
    build(nc, args, out)
    r = _run(nc, [arrays], core_ids=[0])
    return r.results[0]["out_0"]
```
